# Optimizing a Trainium2 kernel written in Bass

```python
import numpy as np
import jax
import jax.numpy as jnp

def _softmax(x, axis=-1):
    return jax.nn.softmax(x, axis=axis)

def _gelu(x):
    return jax.nn.gelu(x, approximate=True)

def _silu(x):
    return jax.nn.silu(x)

def _sigmoid(x):
    return jax.nn.sigmoid(x)

def _layernorm(x, axis=-1, eps=1e-05):
    m = jnp.mean(x, axis=axis, keepdims=True)
    v = jnp.var(x, axis=axis, keepdims=True)
    return (x - m) / jnp.sqrt(v + eps)

def _scatter_add(tgt, idx, src, axis=0):
    return tgt.at[idx].add(src)

def _segment_sum(src, seg, n):
    return jax.ops.segment_sum(src, seg, n)
kernel_name = 'mk_adaln_ffn_d2_seqx_r4_2b4a86'

def setup_inputs(seed: int=0):
    np.random.seed(seed)
    _w = jnp.asarray

    def _rec_inputs():
        import jax
        import jax.numpy as jnp
        _rk = jax.random.key(seed)
        x = -0.0002928 + 1 * jax.random.normal(jax.random.fold_in(_rk, 1), (2, 1024, 256), jnp.float32)
        _lenS = 1024 - jax.random.randint(jax.random.fold_in(_rk, 7), (2,), 0, max(1, 1024 // 4) + 1, jnp.int32)
        _lenS2 = 1024 - jax.random.randint(jax.random.fold_in(_rk, 8), (2,), 0, max(1, 1024 // 4) + 1, jnp.int32)
        fside_16xSxS_0 = -5.72187e-05 + 0.999849 * jax.random.normal(jax.random.fold_in(_rk, 11), (16, 1024, 1024), jnp.float32)
        cond_64 = -0.0265395 + 0.99382 * jax.random.normal(jax.random.fold_in(_rk, 13), (2, 64), jnp.float32)
        _validS = jnp.arange(1024)[None, :] < _lenS[:, None]
        _validS2 = jnp.arange(1024)[None, :] < _lenS2[:, None]
        _causal = jnp.tril(jnp.ones((1024, 1024), dtype=bool))
        mask_BxS_bk0 = jnp.logical_not(jnp.broadcast_to(_validS[:, :], (2, 1024)))
        return (x, fside_16xSxS_0, cond_64, mask_BxS_bk0)
    x, fside_16xSxS_0, cond_64, mask_BxS_bk0 = _rec_inputs()

    def _L0_cond_setup():
        import jax, jax.numpy as jnp
        import numpy as np
        B, N, DIM, H, DH = (2, 512, 256, 16, 64)
        INNER = H * DH
        EPS = 1e-05

        def layernorm(x, g):
            mean = jnp.mean(x, axis=-1, keepdims=True)
            var = jnp.var(x, axis=-1, keepdims=True)
            return (x - mean) * jax.lax.rsqrt(var + EPS) * g
        key = jax.random.key(seed)
        ks = jax.random.split(key, 10)
        x = jax.random.normal(ks[0], (B, N, DIM), dtype=jnp.float32)
        attn_bias = jax.random.normal(ks[1], (H, N, N), dtype=jnp.float32)
        mask = jax.random.randint(ks[2], (B, N), 0, 2).astype(bool)
        g_in = jnp.ones((DIM,), dtype=jnp.float32)
        null_attn_bias = jax.random.normal(ks[3], (H,), dtype=jnp.float32)
        null_kv = jax.random.normal(ks[4], (2, DH), dtype=jnp.float32)
        Wq = jax.random.normal(ks[5], (DIM, INNER), dtype=jnp.float32) * 0.02
        Wkv = jax.random.normal(ks[6], (DIM, 2 * DH), dtype=jnp.float32) * 0.02
        Wo = jax.random.normal(ks[7], (INNER, DIM), dtype=jnp.float32) * 0.02
        g_out = jnp.ones((DIM,), dtype=jnp.float32)
        return {'x': x, 'attn_bias': attn_bias, 'mask': mask, 'g_in': g_in, 'null_attn_bias': null_attn_bias, 'null_kv': null_kv, 'Wq': Wq, 'Wkv': Wkv, 'Wo': Wo, 'g_out': g_out}
    _L0_cond_all = _L0_cond_setup()
    _L0_cond_in = {k: v for k, v in _L0_cond_all.items() if k in ('g_in', 'null_attn_bias', 'Wq', 'Wkv', 'Wo', 'g_out')}
    del _L0_cond_all

    def _L0_ffn_setup():
        import jax, jax.numpy as jnp
        import numpy as np
        import math
        B, L, D = (4, 1024, 256)
        F = 1024
        E = 16
        CAP_FACTOR = 1.0
        EPS = 1e-05
        key = jax.random.key(seed)
        ks = jax.random.split(key, 8)
        std = 0.02
        return {'x': jax.random.normal(ks[0], (B, L, D), dtype=jnp.float32), 'norm_weight': jnp.ones((D,), dtype=jnp.float32), 'router_weight': jax.random.normal(ks[1], (E, D), dtype=jnp.float32) * std, 'router_bias': jnp.zeros((E,), dtype=jnp.float32), 'fc1_weight': jax.random.normal(ks[2], (E, F, D), dtype=jnp.float32) * std, 'fc1_bias': jnp.zeros((E, F), dtype=jnp.float32), 'fc2_weight': jax.random.normal(ks[3], (E, D, F), dtype=jnp.float32) * std, 'fc2_bias': jnp.zeros((E, D), dtype=jnp.float32)}
    _L0_ffn_all = _L0_ffn_setup()
    _L0_ffn_in = {k: v for k, v in _L0_ffn_all.items() if k in ('norm_weight', 'router_weight', 'router_bias', 'fc1_weight', 'fc1_bias', 'fc2_weight', 'fc2_bias')}
    del _L0_ffn_all

    def _L1_cond_setup():
        import jax, jax.numpy as jnp
        import numpy as np
        B, S, H = (4, 512, 256)
        E = 8
        M = 128
        K = 2
        N_SHARED = 2
        SM = M * N_SHARED
        G = 64
        GE_TEMP = 1.0
        ALPHA = 0.001
        SEQ_AUX = True
        NORM_TOPK = True
        COS_TEMP = 0.78
        CONS_ALPHA = 0.01
        LEAKY_SLOPE = 0.01
        EPS_COS = 1e-08

        def _leaky(x):
            return jnp.where(x >= 0, x, LEAKY_SLOPE * x)

        def _moe_forward(hidden_states, g, wt, wg, w_gate, w_up, w_down, sw_gate, sw_up, sw_down):
            b, s, h = hidden_states.shape
            x = hidden_states.reshape(-1, h)
            T = x.shape[0]
            logits_h = x @ wt.T
            logits_g = g @ wg.T
            logits_g = jnp.repeat(logits_g, s, axis=0)
            logits = (logits_h + logits_g / GE_TEMP) / (1.0 + 1.0 / GE_TEMP)
            scores = jax.nn.softmax(logits, axis=-1)
            topk_w, topk_idx = jax.lax.top_k(scores, K)
            if K > 1 and NORM_TOPK:
                topk_w = topk_w / (topk_w.sum(-1, keepdims=True) + 1e-20)
            onehot = jax.nn.one_hot(topk_idx.reshape(b, s * K), E, dtype=jnp.float32)
            ce = onehot.sum(1) / (s * K / E)
            aux_loss = (ce * scores.reshape(b, s, E).mean(1)).sum(1).mean() * ALPHA
            gp = _leaky(jnp.einsum('th,ehm->etm', x, w_gate))
            up = jnp.einsum('th,ehm->etm', x, w_up)
            y_all = jnp.einsum('etm,emh->eth', gp * up, w_down)
            y_sel = y_all[topk_idx, jnp.arange(T)[:, None], :]
            y = (y_sel * topk_w[..., None]).sum(1).reshape(b, s, h)
            p = _leaky(hidden_states @ sw_gate) * (hidden_states @ sw_up) @ sw_down
            y = y + p
            num = jnp.sum(y * p, -1)
            den = jnp.maximum(jnp.linalg.norm(y, axis=-1), EPS_COS) * jnp.maximum(jnp.linalg.norm(p, axis=-1), EPS_COS)
            closs = CONS_ALPHA * jnp.mean(num / den / (1.0 + COS_TEMP))
            return (y, aux_loss + closs)
        key = jax.random.key(seed)
        ks = jax.random.split(key, 12)
        sh = 1.0 / np.sqrt(H)
        sm = 1.0 / np.sqrt(M)
        ssm = 1.0 / np.sqrt(SM)
        sg = 1.0 / np.sqrt(G)
        return {'hidden_states': jax.random.normal(ks[0], (B, S, H), jnp.float32), 'g': jax.random.normal(ks[1], (B, G), jnp.float32), 'wt': jax.random.uniform(ks[2], (E, H), jnp.float32, -sh, sh), 'wg': jax.random.uniform(ks[3], (E, G), jnp.float32, -sg, sg), 'w_gate': jax.random.uniform(ks[4], (E, H, M), jnp.float32, -sh, sh), 'w_up': jax.random.uniform(ks[5], (E, H, M), jnp.float32, -sh, sh), 'w_down': jax.random.uniform(ks[6], (E, M, H), jnp.float32, -sm, sm), 'sw_gate': jax.random.uniform(ks[7], (H, SM), jnp.float32, -sh, sh), 'sw_up': jax.random.uniform(ks[8], (H, SM), jnp.float32, -sh, sh), 'sw_down': jax.random.uniform(ks[9], (SM, H), jnp.float32, -ssm, ssm)}
    _L1_cond_all = _L1_cond_setup()
    _L1_cond_in = {k: v for k, v in _L1_cond_all.items() if k in ('wt', 'wg', 'w_gate', 'w_up', 'w_down', 'sw_gate', 'sw_up', 'sw_down')}
    del _L1_cond_all

    def _L1_ffn_setup():
        import jax, jax.numpy as jnp
        import numpy as np
        EMBED_DIM = 256
        HIDDEN_DIM = 1024
        NUM_EXPERTS = 8
        TOP_K = 2
        key = jax.random.key(seed)
        ks = jax.random.split(key, 4)
        std1 = float(np.sqrt(2.0 / EMBED_DIM))
        std2 = float(np.sqrt(2.0 / HIDDEN_DIM))
        x = jax.random.normal(ks[0], (1, 512, EMBED_DIM), dtype=jnp.float32)
        w_router = jax.random.normal(ks[1], (EMBED_DIM, NUM_EXPERTS), dtype=jnp.float32) * 0.02
        w1 = jax.random.normal(ks[2], (NUM_EXPERTS, EMBED_DIM, HIDDEN_DIM), dtype=jnp.float32) * std1
        b1 = jnp.zeros((NUM_EXPERTS, HIDDEN_DIM), dtype=jnp.float32)
        w2 = jax.random.normal(ks[3], (NUM_EXPERTS, HIDDEN_DIM, EMBED_DIM), dtype=jnp.float32) * std2
        b2 = jnp.zeros((NUM_EXPERTS, EMBED_DIM), dtype=jnp.float32)
        return {'x': x, 'w_router': w_router, 'w1': w1, 'b1': b1, 'w2': w2, 'b2': b2}
    _L1_ffn_all = _L1_ffn_setup()
    _L1_ffn_in = {k: v for k, v in _L1_ffn_all.items() if k in ('w_router', 'w1', 'b1', 'w2', 'b2')}
    del _L1_ffn_all
    return {'x': x, 'fside_16xSxS_0': fside_16xSxS_0, 'cond_64': cond_64, 'mask_BxS_bk0': mask_BxS_bk0, 'L0_cond_g_in': _L0_cond_in['g_in'], 'L0_cond_null_attn_bias': _L0_cond_in['null_attn_bias'], 'L0_cond_Wq': _L0_cond_in['Wq'], 'L0_cond_Wkv': _L0_cond_in['Wkv'], 'L0_cond_Wo': _L0_cond_in['Wo'], 'L0_cond_g_out': _L0_cond_in['g_out'], 'L0_ffn_norm_weight': _L0_ffn_in['norm_weight'], 'L0_ffn_router_weight': _L0_ffn_in['router_weight'], 'L0_ffn_router_bias': _L0_ffn_in['router_bias'], 'L0_ffn_fc1_weight': _L0_ffn_in['fc1_weight'], 'L0_ffn_fc1_bias': _L0_ffn_in['fc1_bias'], 'L0_ffn_fc2_weight': _L0_ffn_in['fc2_weight'], 'L0_ffn_fc2_bias': _L0_ffn_in['fc2_bias'], 'L1_cond_wt': _L1_cond_in['wt'], 'L1_cond_wg': _L1_cond_in['wg'], 'L1_cond_w_gate': _L1_cond_in['w_gate'], 'L1_cond_w_up': _L1_cond_in['w_up'], 'L1_cond_w_down': _L1_cond_in['w_down'], 'L1_cond_sw_gate': _L1_cond_in['sw_gate'], 'L1_cond_sw_up': _L1_cond_in['sw_up'], 'L1_cond_sw_down': _L1_cond_in['sw_down'], 'L1_ffn_w_router': _L1_ffn_in['w_router'], 'L1_ffn_w1': _L1_ffn_in['w1'], 'L1_ffn_b1': _L1_ffn_in['b1'], 'L1_ffn_w2': _L1_ffn_in['w2'], 'L1_ffn_b2': _L1_ffn_in['b2']}

def reference(x, fside_16xSxS_0, cond_64, mask_BxS_bk0, L0_cond_g_in, L0_cond_null_attn_bias, L0_cond_Wq, L0_cond_Wkv, L0_cond_Wo, L0_cond_g_out, L0_ffn_norm_weight, L0_ffn_router_weight, L0_ffn_router_bias, L0_ffn_fc1_weight, L0_ffn_fc1_bias, L0_ffn_fc2_weight, L0_ffn_fc2_bias, L1_cond_wt, L1_cond_wg, L1_cond_w_gate, L1_cond_w_up, L1_cond_w_down, L1_cond_sw_gate, L1_cond_sw_up, L1_cond_sw_down, L1_ffn_w_router, L1_ffn_w1, L1_ffn_b1, L1_ffn_w2, L1_ffn_b2):
    import jax
    import jax.numpy as jnp

    def _L0_cond_ref(x, attn_bias, mask, g_in, null_attn_bias, null_kv, Wq, Wkv, Wo, g_out):
        import jax, jax.numpy as jnp
        import numpy as np
        B, N, DIM, H, DH = (2, 512, 256, 16, 64)
        INNER = H * DH
        EPS = 1e-05

        def layernorm(x, g):
            mean = jnp.mean(x, axis=-1, keepdims=True)
            var = jnp.var(x, axis=-1, keepdims=True)
            return (x - mean) * jax.lax.rsqrt(var + EPS) * g
        b, n, _ = x.shape
        scale = DH ** (-0.5)
        xn = layernorm(x, g_in)
        q = (xn @ Wq).reshape(b, n, H, DH).transpose(0, 2, 1, 3) * scale
        kv = xn @ Wkv
        k, v = (kv[..., :DH], kv[..., DH:])
        nk = jnp.broadcast_to(null_kv[0], (b, 1, DH))
        nv = jnp.broadcast_to(null_kv[1], (b, 1, DH))
        k = jnp.concatenate([nk, k], axis=1)
        v = jnp.concatenate([nv, v], axis=1)
        sim = jnp.einsum('bhid,bjd->bhij', q, k)
        null_col = jnp.broadcast_to(null_attn_bias[:, None, None], (H, n, 1))
        bias = jnp.concatenate([null_col, attn_bias], axis=-1)
        sim = sim + bias
        neg = -jnp.finfo(sim.dtype).max
        j = n + 1
        causal_mask = jnp.triu(jnp.ones((n, j), dtype=bool), k=j - n + 1)
        sim = jnp.where(causal_mask, neg, sim)
        mask_p = jnp.pad(mask, ((0, 0), (1, 0)), constant_values=True)
        sim = jnp.where(mask_p[:, None, None, :], sim, neg)
        attn = jax.nn.softmax(sim, axis=-1)
        out = jnp.einsum('bhij,bjd->bhid', attn, v)
        out = out.transpose(0, 2, 1, 3).reshape(b, n, INNER)
        out = out @ Wo
        return layernorm(out, g_out)

    def _L0_ffn_ref(x, norm_weight, router_weight, router_bias, fc1_weight, fc1_bias, fc2_weight, fc2_bias):
        import jax, jax.numpy as jnp
        import numpy as np
        import math
        B, L, D = (4, 1024, 256)
        F = 1024
        E = 16
        CAP_FACTOR = 1.0
        EPS = 1e-05
        b, l, d = x.shape
        n_tokens = b * l
        n_experts = router_weight.shape[0]
        capacity = max(1, math.ceil(CAP_FACTOR * n_tokens / n_experts))
        top_k = min(capacity, n_tokens)
        xf = x.reshape(n_tokens, d)
        rms = jnp.sqrt(jnp.mean(xf * xf, axis=-1, keepdims=True) + EPS)
        xn = xf / rms * norm_weight
        logits = xn @ router_weight.T + router_bias
        probs = jax.nn.softmax(logits, axis=-1)
        _, idx = jax.lax.top_k(logits.T, top_k)
        xe = xn[idx]
        h = jnp.einsum('ecd,efd->ecf', xe, fc1_weight) + fc1_bias[:, None, :]
        h = jax.nn.gelu(h, approximate=False)
        y = jnp.einsum('ecf,edf->ecd', h, fc2_weight) + fc2_bias[:, None, :]
        gates = jnp.take_along_axis(probs.T, idx, axis=1)
        flat_idx = idx.reshape(-1)
        contrib = (y * gates[:, :, None]).reshape(-1, d)
        output = jnp.zeros((n_tokens, d), dtype=x.dtype).at[flat_idx].add(contrib)
        gate_sums = jnp.zeros((n_tokens, 1), dtype=x.dtype).at[flat_idx].add(gates.reshape(-1, 1))
        assigned = gate_sums > 0
        output = jnp.where(assigned, output / jnp.where(assigned, gate_sums, 1.0), output)
        return output.reshape(b, l, d)

    def _L1_cond_ref(hidden_states, g, wt, wg, w_gate, w_up, w_down, sw_gate, sw_up, sw_down):
        import jax, jax.numpy as jnp
        import numpy as np
        B, S, H = (4, 512, 256)
        E = 8
        M = 128
        K = 2
        N_SHARED = 2
        SM = M * N_SHARED
        G = 64
        GE_TEMP = 1.0
        ALPHA = 0.001
        SEQ_AUX = True
        NORM_TOPK = True
        COS_TEMP = 0.78
        CONS_ALPHA = 0.01
        LEAKY_SLOPE = 0.01
        EPS_COS = 1e-08

        def _leaky(x):
            return jnp.where(x >= 0, x, LEAKY_SLOPE * x)

        def _moe_forward(hidden_states, g, wt, wg, w_gate, w_up, w_down, sw_gate, sw_up, sw_down):
            b, s, h = hidden_states.shape
            x = hidden_states.reshape(-1, h)
            T = x.shape[0]
            logits_h = x @ wt.T
            logits_g = g @ wg.T
            logits_g = jnp.repeat(logits_g, s, axis=0)
            logits = (logits_h + logits_g / GE_TEMP) / (1.0 + 1.0 / GE_TEMP)
            scores = jax.nn.softmax(logits, axis=-1)
            topk_w, topk_idx = jax.lax.top_k(scores, K)
            if K > 1 and NORM_TOPK:
                topk_w = topk_w / (topk_w.sum(-1, keepdims=True) + 1e-20)
            onehot = jax.nn.one_hot(topk_idx.reshape(b, s * K), E, dtype=jnp.float32)
            ce = onehot.sum(1) / (s * K / E)
            aux_loss = (ce * scores.reshape(b, s, E).mean(1)).sum(1).mean() * ALPHA
            gp = _leaky(jnp.einsum('th,ehm->etm', x, w_gate))
            up = jnp.einsum('th,ehm->etm', x, w_up)
            y_all = jnp.einsum('etm,emh->eth', gp * up, w_down)
            y_sel = y_all[topk_idx, jnp.arange(T)[:, None], :]
            y = (y_sel * topk_w[..., None]).sum(1).reshape(b, s, h)
            p = _leaky(hidden_states @ sw_gate) * (hidden_states @ sw_up) @ sw_down
            y = y + p
            num = jnp.sum(y * p, -1)
            den = jnp.maximum(jnp.linalg.norm(y, axis=-1), EPS_COS) * jnp.maximum(jnp.linalg.norm(p, axis=-1), EPS_COS)
            closs = CONS_ALPHA * jnp.mean(num / den / (1.0 + COS_TEMP))
            return (y, aux_loss + closs)
        y, _ = _moe_forward(hidden_states, g, wt, wg, w_gate, w_up, w_down, sw_gate, sw_up, sw_down)
        return y

    def _L1_ffn_ref(x, w_router, w1, b1, w2, b2):
        import jax, jax.numpy as jnp
        import numpy as np
        EMBED_DIM = 256
        HIDDEN_DIM = 1024
        NUM_EXPERTS = 8
        TOP_K = 2
        orig_shape = x.shape
        xf = x.reshape(-1, EMBED_DIM)
        logits = xf @ w_router
        probs = jax.nn.softmax(logits, axis=-1)
        topk_w, topk_idx = jax.lax.top_k(probs, TOP_K)
        mask = jax.nn.one_hot(topk_idx, NUM_EXPERTS, dtype=xf.dtype)
        weights = jnp.sum(topk_w[..., None] * mask, axis=1)
        h = jnp.einsum('te,ieh->tih', xf, w1) + b1
        h = jax.nn.gelu(h)
        out = jnp.einsum('tih,ihe->tie', h, w2) + b2
        out = jnp.sum(out * weights[..., None], axis=1)
        return out.reshape(orig_shape)
    x = x + _L0_ffn_ref(_L0_cond_ref(x, fside_16xSxS_0, mask_BxS_bk0, L0_cond_g_in, L0_cond_null_attn_bias, cond_64, L0_cond_Wq, L0_cond_Wkv, L0_cond_Wo, L0_cond_g_out), L0_ffn_norm_weight, L0_ffn_router_weight, L0_ffn_router_bias, L0_ffn_fc1_weight, L0_ffn_fc1_bias, L0_ffn_fc2_weight, L0_ffn_fc2_bias)
    x = x + _L1_ffn_ref(_L1_cond_ref(x, cond_64, L1_cond_wt, L1_cond_wg, L1_cond_w_gate, L1_cond_w_up, L1_cond_w_down, L1_cond_sw_gate, L1_cond_sw_up, L1_cond_sw_down), L1_ffn_w_router, L1_ffn_w1, L1_ffn_b1, L1_ffn_w2, L1_ffn_b2)
    return x

_drawn_inputs = setup_inputs


def setup_inputs(seed=0):
    import zlib

    import numpy as np

    out = dict(_drawn_inputs(seed))
    spreads = {'L0_cond_g_in': (1.0, 0.6),
     'L0_cond_g_out': (1.0, 0.6),
     'L0_ffn_norm_weight': (1.0, 0.6),
     'L0_ffn_router_bias': (0.0, 0.8),
     'L0_ffn_fc1_bias': (0.0, 0.8),
     'L0_ffn_fc2_bias': (0.0, 0.375),
     'L1_ffn_b1': (0.0, 0.557),
     'L1_ffn_b2': (0.0, 0.424)}
    factors = {'L0_cond_null_attn_bias': 3.436, 'L0_cond_Wq': 4.704}
    for name, (base, spread) in spreads.items():
        noise = np.random.default_rng([zlib.crc32(name.encode()), seed]).standard_normal(out[name].shape)
        drawn = base * np.exp(spread * noise) if base else spread * noise
        out[name] = jnp.asarray(drawn.astype(out[name].dtype))
    for name, factor in factors.items():
        out[name] = (out[name] * factor).astype(out[name].dtype)
    return out
```

```python
from contextlib import ExitStack

import concourse.bass as bass
from concourse import mybir

P = 128
F32 = mybir.dt.float32
I32 = mybir.dt.int32
U32 = mybir.dt.uint32
U8 = mybir.dt.uint8
ALU = mybir.AluOpType
ACT = mybir.ActivationFunctionType
AX = mybir.AxisListType.X
ds = bass.ds

B, N, D = 2, 1024, 256
KD = D // P
T = B * N // P
QT = N // P
H, DH = 16, 64
E0, F0 = 16, 1024
FC = F0 // P
CAP = B * N // E0
E1, M1 = 8, 128
EG = E1 + 2
BLK = 2 * B * N // P + E1
ROW = D + E0
RING = 4
EPS = 1e-5
HIDE = -1e38
assert CAP == P and F0 == 1024


def bcast(ap, n):
    return ap.unsqueeze(2).to_broadcast([ap.shape[0], ap.shape[1], n])


def repeat(ap, n):
    return ap.unsqueeze(1).to_broadcast([ap.shape[0], n, ap.shape[1]])


def moe_kernel(nc, x, bias, cond, condT, mask, g_in, null_bias, wq, wkv, wo, g_out, norm_w, rw, rb,
               w1, b1, w2, b2, wt, wg, wgate, wup, wdown, wr, v1, c1, v2, c2, out, upto="end"):
    with ExitStack() as ctx:
        def sem(name):
            return ctx.enter_context(nc.semaphore(name))

        def sb(name, shape, dt=F32, into=ctx):
            return into.enter_context(nc.sbuf_tensor(name, shape, dt))

        def ps(name, shape, into):
            return into.enter_context(nc.psum_tensor(name, shape, F32))

        def dram(name, shape):
            return nc.dram_tensor(name, shape, F32, kind="Internal").ap()

        table = dram("table", (B * N, ROW))
        acc0 = dram("acc0", (B * N, D + 1))
        ytab = dram("ytab", (B * N, D))
        acc1 = dram("acc1", (B * N + P, D))

        x_sb = sb("x_sb", [P, T, D])
        ident = sb("ident", [P, P])
        ones = sb("ones", [P, P])
        w1_sb = sb("w1_sb", [P, RING, KD, F0])
        w2_sb = sb("w2_sb", [P, RING, FC, D])
        stats = sb("stats", [P, T, 6])
        mom = sb("mom", [P, 6, T])
        MEAN, VAR, RSTD, TMP, TMQ, MSQ = range(6)
        xc = sb("xc", [P, T, D])
        ring_row = sb("ring_row", [P, 2, D])
        ring_col = sb("ring_col", [P, 2, KD, P])
        gi = sb("gi", [P, 1], U32)
        si = sb("si", [P, 1], U32)
        held = sb("held", [P, 4])

        w_in = [sem(f"w_in{u}") for u in range(RING)]
        consts_done = sem("consts_done")
        x_in = sem("x_in")

        def load_expert(eng, w1t, w2t, e, u):
            eng.dma_start(w1_sb[:, u], w1t[e].rearrange("(k p) f -> p k f", p=P)).then_inc(w_in[u], 16)
            eng.dma_start(w2_sb[:, u], w2t[e].rearrange("(c p) d -> p c d", p=P)).then_inc(w_in[u], 16)

        def load_expert_at(eng, w1t, w2t, e, u):
            eng.dma_start(w1_sb[:, u], w1t[ds(e, 1)].rearrange("a (k p) f -> p (a k) f", p=P)).then_inc(w_in[u], 16)
            eng.dma_start(w2_sb[:, u], w2t[ds(e, 1)].rearrange("a (c p) d -> p (a c) d", p=P)).then_inc(w_in[u], 16)

        def held_here(pool, n):
            pool.tensor_tensor(held[:, n:n + 1], ones[:, 0:1], ones[:, 0:1], ALU.mult)

        def finish_moments(dve, link):
            ev, od = stats[:, :, 1], stats[:, :, 4]
            link(dve.tensor_tensor(mom[:, MEAN], ev, od, ALU.add))
            link(dve.tensor_tensor(mom[:, TMP], ev, od, ALU.subtract))
            link(dve.tensor_scalar(mom[:, MEAN], mom[:, MEAN], 0.5, None, ALU.mult))
            link(dve.tensor_scalar(mom[:, TMP], mom[:, TMP], 0.5, None, ALU.mult))
            link(dve.tensor_tensor(mom[:, TMP], mom[:, TMP], mom[:, TMP], ALU.mult))
            link(dve.tensor_tensor(mom[:, TMQ], stats[:, :, 2], stats[:, :, 5], ALU.add))
            link(dve.scalar_tensor_tensor(mom[:, VAR], mom[:, TMQ], 1.0 / D, mom[:, TMP], ALU.mult, ALU.add))

        att = ctx.enter_context(ExitStack())
        xnT = sb("xnT", [P, KD, B * N], into=att)
        kT = sb("kT", [P, B * N], into=att)
        v_sb = sb("v_sb", [P, T, DH], into=att)
        hide = sb("hide", [P, B * N], into=att)
        window = sb("window", [P, 2 * N - P], into=att)
        wq_sb = sb("wq_sb", [P, KD, H * DH], into=att)
        wo_sb = sb("wo_sb", [P, FC, D], into=att)
        wk2 = sb("wk2", [P, KD, 2, DH], into=att)
        wv = sb("wv", [P, KD, DH], into=att)
        gcol = sb("gcol", [P, KD], into=att)
        mask8 = sb("mask8", [P, B * N], U8, into=att)
        nkT = sb("nkT", [P, 2], into=att)
        nv = sb("nv", [P, DH], into=att)
        nullb = sb("nullb", [P, H], into=att)
        blockseq = sb("blockseq", [1, B, QT], into=att)
        anylive = sb("anylive", [1, B, QT], into=att)
        startf = sb("startf", [1, B], into=att)
        start = sb("start", [1, B], I32, into=att)
        zrow = sb("zrow", [P, D + 1], into=att)

        att_in, mask_in, moments, rooted = sem("att_in"), sem("mask_in"), sem("moments"), sem("rooted")
        xn_row, xn_t, xn_col, xn_kept, kv_done, kv_kept = (
            sem("xn_row"), sem("xn_t"), sem("xn_col"), sem("xn_kept"), sem("kv_done"), sem("kv_kept"))
        zeroed, acc0_zero, mask_step, pool_step = sem("zeroed"), sem("acc0_zero"), sem("mask_step"), sem("pool_step")

        with ExitStack() as ph:
            pt = [ps(f"a_pt{u}", [P, 512], ph) for u in range(2)]
            pk = [ps(f"a_pk{u}", [P, 512], ph) for u in range(2)]
            pv = [ps(f"a_pv{u}", [P, 512], ph) for u in range(2)]
            with nc.Block() as block:
                @block.sync
                def _(sp):
                    sp.dma_start(x_sb[:], x.rearrange("b (t p) d -> p (b t) d", p=P)).then_inc(x_in, 16)
                    sp.dma_start(gcol[:], g_in).then_inc(att_in, 16)
                    for half in range(2):
                        sp.dma_start(wk2[:, :, half], wkv[:, 0:DH].rearrange("(k p) n -> p k n", p=P)).then_inc(att_in, 16)
                    sp.dma_start(wv[:], wkv[:, DH:2 * DH].rearrange("(k p) n -> p k n", p=P)).then_inc(att_in, 16)
                    sp.dma_start(wq_sb[:], wq.rearrange("(k p) n -> p k n", p=P)).then_inc(att_in, 16)
                    sp.dma_start(wo_sb[:], wo.rearrange("(c p) d -> p c d", p=P)).then_inc(att_in, 16)
                    for half in range(2):
                        sp.dma_start(nkT[half * DH:(half + 1) * DH, :], condT).then_inc(att_in, 16)
                    sp.dma_start(nv[:], cond[1:2, :].partition_broadcast(P)).then_inc(att_in, 16)
                    sp.dma_start(nullb[:], null_bias.partition_broadcast(P)).then_inc(att_in, 16)
                    sp.dma_start(mask8[:], mask.partition_broadcast(P)).then_inc(mask_in, 16)
                    for u in range(RING):
                        load_expert(sp, w1, w2, u, u)
                    sp.wait_ge(zeroed, 1)
                    for t in range(T):
                        sp.dma_start(acc0[t * P:(t + 1) * P, :], zrow[:]).then_inc(acc0_zero, 16)
                    sp.wait_ge(att_in, 16 * 10)
                    sp.wait_ge(acc0_zero, 16 * T)

                @block.gpsimd
                def _(pool):
                    pool.memset(ident[:], 0.0).then_inc(pool_step, 1)
                    pool.wait_ge(pool_step, 1)
                    pool.affine_select(out=ident[:], in_=ident[:], compare_op=ALU.not_equal, fill=1.0, base=0,
                                       pattern=[[-1, P]], channel_multiplier=1).then_inc(consts_done, 1)
                    pool.memset(ones[:], 1.0).then_inc(consts_done, 1)
                    pool.memset(zrow[:], 0.0).then_inc(zeroed, 1)
                    pool.memset(window[:], 0.0).then_inc(pool_step, 1)
                    pool.wait_ge(pool_step, 2)
                    pool.affine_select(out=window[:], in_=window[:], compare_op=ALU.is_ge, fill=HIDE, base=N - P,
                                       pattern=[[-1, 2 * N - P]], channel_multiplier=1).then_inc(pool_step, 1)
                    pool.iota(blockseq[:], pattern=[[0, B], [1, QT]], base=-QT, channel_multiplier=0,
                              allow_small_or_imprecise_dtypes=True).then_inc(consts_done, 1)
                    with pool.Fori(0, T // 2) as i:
                        for u in range(2):
                            pool.wait_ge(xn_col, 2 * i + u + 1)
                            pool.tensor_copy(xnT[:, :, ds((2 * i + u) * P, P)], ring_col[:, u]).then_inc(xn_kept, 1)

                @block.vector
                def _(dve):
                    steps = [0]

                    def link(ins):
                        steps[0] += 1
                        ins.then_inc(moments, 1)
                        dve.wait_ge(moments, steps[0])

                    dve.wait_ge(x_in, 16)
                    with dve.Fori(0, T) as t:
                        dve.bn_stats(stats[:, ds(t, 1)].rearrange("p a s -> p (a s)"),
                                     x_sb[:, ds(t, 1)].rearrange("p a d -> p (a d)")).then_inc(moments, 1)
                    steps[0] = T
                    dve.wait_ge(moments, T)
                    finish_moments(dve, link)
                    link(dve.tensor_scalar(mom[:, TMP], mom[:, VAR], EPS, None, ALU.add))
                    dve.wait_ge(rooted, 1)
                    link(dve.reciprocal(mom[:, RSTD], mom[:, TMQ]))
                    with dve.Fori(0, T // 2) as i:
                        for u in range(2):
                            t = 2 * i + u
                            dve.tensor_scalar(ring_row[:, u], x_sb[:, ds(t, 1)].rearrange("p a d -> p (a d)"),
                                              mom[:, MEAN, ds(t, 1)], mom[:, RSTD, ds(t, 1)],
                                              ALU.subtract, ALU.mult).then_inc(xn_row, 1)
                            dve.wait_ge(kv_done, 2 * i + u + 1)
                            dve.tensor_copy(kT[:, ds(t * P, P)], pk[u][:, 0:P]).then_inc(kv_kept, 1)
                            dve.tensor_copy(v_sb[:, ds(t, 1)].rearrange("p a d -> p (a d)"),
                                            pv[u][:, 0:DH]).then_inc(kv_kept, 1)
                    dve.wait_ge(mask_in, 16)
                    dve.tensor_scalar(hide[:], mask8[:], 1.0, -HIDE, ALU.subtract, ALU.mult).then_inc(mask_step, 1)
                    dve.tensor_reduce(anylive[:], mask8[0:1, :].rearrange("p (b t k) -> p b t k", b=B, k=P),
                                      AX, ALU.max).then_inc(mask_step, 1)
                    dve.wait_ge(mask_step, 2)
                    dve.wait_ge(consts_done, 3)
                    dve.tensor_tensor(anylive[:], anylive[:], blockseq[:], ALU.mult).then_inc(mask_step, 1)
                    dve.wait_ge(mask_step, 3)
                    dve.tensor_reduce(startf[:], anylive[:], AX, ALU.min).then_inc(mask_step, 1)
                    dve.wait_ge(mask_step, 4)
                    dve.tensor_scalar(start[:], startf[:], float(QT), None, ALU.add).then_inc(mask_step, 1)
                    dve.wait_ge(mask_step, 5)

                @block.scalar
                def _(act):
                    act.wait_ge(moments, T + 8)
                    act.activation(mom[:, TMQ], mom[:, TMP], ACT.Sqrt).then_inc(rooted, 1)
                    act.wait_ge(att_in, 16 * 10)
                    with act.Fori(0, T // 2) as i:
                        for u in range(2):
                            t = 2 * i + u
                            act.wait_ge(xn_t, t + 1)
                            act.wait_ge(xn_kept, 2 * i)
                            act.wait_ge(kv_done, 2 * i)
                            act.activation(ring_col[:, u, 0], pt[u][:, 0:P], ACT.Copy, scale=gcol[:, 0:1])
                            act.activation(ring_col[:, u, 1], pt[u][:, P:2 * P], ACT.Copy,
                                           scale=gcol[:, 1:2]).then_inc(xn_col, 1)

                @block.tensor
                def _(pe):
                    pe.wait_ge(consts_done, 3)
                    pe.wait_ge(att_in, 16 * 10)
                    with pe.Fori(0, T // 2) as i:
                        for u in range(2):
                            t = 2 * i + u
                            pe.wait_ge(xn_row, t + 1)
                            for k in range(KD):
                                ins = pe.transpose(pt[u][:, k * P:(k + 1) * P], ring_row[:, u, k * P:(k + 1) * P], ident[:])
                            ins.then_inc(xn_t, 1)
                            pe.wait_ge(xn_col, t + 1)
                            pe.wait_ge(kv_kept, 4 * i)
                            for k in range(KD):
                                pe.matmul(pk[u][:, 0:P], wk2[:, k].rearrange("p a d -> p (a d)"), ring_col[:, u, k],
                                          start=(k == 0), stop=(k == KD - 1))
                            for k in range(KD):
                                ins = pe.matmul(pv[u][:, 0:DH], ring_col[:, u, k], wv[:, k],
                                                start=(k == 0), stop=(k == KD - 1))
                            ins.then_inc(kv_done, 1)

        with ExitStack() as ph:
            bias_sb = sb("bias_sb", [P, H, P], into=ph)
            sc = sb("sc", [P, H, P], into=ph)
            PT = sb("PT", [P, 4, P], into=ph)
            O = sb("O", [P, H, DH], into=ph)
            OT = sb("OT", [P, FC, P], into=ph)
            qT = sb("qT", [P, FC, P], into=ph)
            kblk = sb("kblk", [P, P], into=ph)
            vblk = sb("vblk", [P, DH], into=ph)
            comb = sb("comb", [P, P], into=ph)
            st = sb("st", [P, 8, H], into=ph)
            MAX, LEN, TMAX, NEG, DIF, ALPHA, RS, RL = range(8)
            pS = ps("pS", [P, 4, 512], ph)
            pT = ps("pT", [P, 2, 512], ph)
            pO = ps("pO", [P, 2, 512], ph)
            q_proj, q_ready, null_done, q_step = sem("q_proj"), sem("q_ready"), sem("null_done"), sem("q_step")
            bias_in, staged, bias_ready, s_done, sc_ready = (
                sem("bias_in"), sem("staged"), sem("bias_ready"), sem("s_done"), sem("sc_ready"))
            k_step, p_ready, alpha_ready, t_done, pt_ready, pv_done, k_done = (
                sem("k_step"), sem("p_ready"), sem("alpha_ready"), sem("t_done"), sem("pt_ready"), sem("pv_done"), sem("k_done"))
            o_ready, ot_done, ot_ready, o_proj, q_done, comb_ready, dead_done = (
                sem("o_ready"), sem("ot_done"), sem("ot_ready"), sem("o_proj"), sem("q_done"), sem("comb_ready"), sem("dead_done"))
            QSTEP = 6
            KSTEP = 8

            def live_tiles(eng, name, on_queries, on_keys, after):
                nq, nk = eng.alloc_register(name + "_nq"), eng.alloc_register(name + "_nk")
                eng.reg_mov(nq, 0)
                eng.reg_mov(nk, 0)
                with eng.Fori(0, B) as b:
                    first = eng.value_load(start[0:1, ds(b, 1)], min_val=0, max_val=QT)
                    with eng.If(first < QT):
                        with eng.Fori(first, QT) as qt:
                            on_queries(b, qt, eng.snap(nq))
                            with eng.Fori(first, qt + 1) as kt:
                                on_keys(b, qt, kt, eng.snap(nq), eng.snap(nk))
                                eng.reg_add(nk, nk, 1)
                            after(b, qt, eng.snap(nq), eng.snap(nk))
                            eng.reg_add(nq, nq, 1)

            def by_bank(tile, g):
                return tile[:].rearrange("p (a i r) k -> p a r i k", a=2, r=2)[:, g // 2, g % 2]

            def nothing(*_):
                pass

            with nc.Block() as block:
                @block.sync
                def _(sp):
                    def keys(b, qt, kt, nq, nk):
                        sp.wait_ge(sc_ready, nk * 4)
                        sp.dma_start(bias_sb[:], bias[:, ds(qt * P, P), ds(kt * P, P)].rearrange("h q k -> q h k")).then_inc(bias_in, 16)
                    live_tiles(sp, "sp", nothing, keys, nothing)

                @block.gpsimd
                def _(pool):
                    def keys(b, qt, kt, nq, nk):
                        pool.wait_ge(pv_done, nk * 2)
                        pool.tensor_copy(kblk[:], kT[:, ds(b * N + kt * P, P)]).then_inc(staged, 1)
                        pool.tensor_copy(vblk[:], v_sb[:, ds(b * QT + kt, 1)].rearrange("p a d -> p (a d)")).then_inc(staged, 1)
                        pool.wait_ge(bias_ready, nk)
                        pool.tensor_tensor(comb[:], window[:, ds((kt - qt + QT - 1) * P, P)],
                                           hide[:, ds(b * N + kt * P, P)], ALU.add).then_inc(comb_ready, 1)
                        pool.wait_ge(comb_ready, nk + 1)
                        pool.wait_ge(bias_in, nk * 16 + 16)
                        pool.tensor_tensor(bias_sb[:], bias_sb[:], repeat(comb[:], H), ALU.add).then_inc(bias_ready, 1)
                    live_tiles(pool, "pool", nothing, keys, nothing)

                @block.tensor
                def _(pe):
                    def project(n):
                        pe.wait_ge(o_ready, n + 1)
                        for c in range(FC):
                            ins = pe.transpose(pT[:, c // 4, (c % 4) * P:(c % 4 + 1) * P],
                                               O[:, 2 * c:2 * c + 2].rearrange("p h d -> p (h d)"), ident[:])
                        ins.then_inc(ot_done, 1)
                        pe.wait_ge(ot_ready, n + 1)
                        for c in range(FC):
                            ins = pe.matmul(pO[:, 0, 0:D], OT[:, c], wo_sb[:, c], start=(c == 0), stop=(c == FC - 1))
                        ins.then_inc(o_proj, 1)

                    project(0)

                    def queries(b, qt, nq):
                        pe.wait_ge(q_done, nq + 1)
                        for c in range(FC):
                            for k in range(KD):
                                ins = pe.matmul(pT[:, c // 4, (c % 4) * P:(c % 4 + 1) * P], wq_sb[:, k, c * P:(c + 1) * P],
                                                xnT[:, k, ds(b * N + qt * P, P)], start=(k == 0), stop=(k == KD - 1))
                        ins.then_inc(q_proj, 1)
                        pe.wait_ge(q_ready, nq * 2 + 2)
                        for h in range(H):
                            at = (h % 2) * DH
                            ins = pe.matmul(pO[:, h % 2, h // 2:h // 2 + 1], qT[at:at + DH, h // 2], nkT[at:at + DH, 0:1], start=True, stop=True)
                        ins.then_inc(null_done, 1)

                    def keys(b, qt, kt, nq, nk):
                        pe.wait_ge(staged, nk * 2 + 2)
                        for h in range(H):
                            at = (h % 2) * DH
                            ins = pe.matmul(pS[:, 2 * (h // 8) + h % 2, (h % 8 // 2) * P:(h % 8 // 2 + 1) * P],
                                            qT[at:at + DH, h // 2], kblk[at:at + DH, :], start=True, stop=True)
                            if h % 8 >= 6:
                                ins.then_inc(s_done, 1)
                        for g in range(4):
                            pe.wait_ge(p_ready, nk * 16 + 4 * g + 4)
                            if g >= 2:
                                pe.wait_ge(pt_ready, nk * 4 + g - 1)
                            for h in range(4 * g, 4 * g + 4):
                                ins = pe.transpose(pT[:, g % 2, (h % 4) * P:(h % 4 + 1) * P], sc[:, h], ident[:])
                            ins.then_inc(t_done, 1)
                            pe.wait_ge(pt_ready, nk * 4 + g + 1)
                            for h in range(4 * g, 4 * g + 4):
                                ins = pe.matmul(pO[:, h // 8, (h % 8) * DH:(h % 8 + 1) * DH], PT[:, h % 4], vblk[:],
                                                start=True, stop=True)
                            if g % 2:
                                ins.then_inc(pv_done, 1)

                    live_tiles(pe, "pe", queries, keys, lambda b, qt, nq, nk: project(nq + 1))

                @block.scalar
                def _(act):
                    def queries(b, qt, nq):
                        act.wait_ge(q_proj, nq + 1)
                        for g in range(2):
                            act.activation(qT[:, 4 * g:4 * g + 4].rearrange("p c q -> p (c q)"), pT[:, g], ACT.Copy,
                                           scale=DH ** -0.5).then_inc(q_ready, 1)

                    def keys(b, qt, kt, nq, nk):
                        act.wait_ge(k_step, nk * KSTEP + 4)
                        for h in range(H):
                            act.activation(sc[:, h], sc[:, h], ACT.Exp, bias=st[:, NEG, h:h + 1],
                                           accum_out=st[:, RS, h:h + 1]).then_inc(p_ready, 1)
                        act.activation(st[:, ALPHA], st[:, DIF], ACT.Exp).then_inc(alpha_ready, 1)

                    live_tiles(act, "act", queries, keys, nothing)

                @block.vector
                def _(dve):
                    def project(n, into, out_sem):
                        dve.wait_ge(ot_done, n + 1)
                        dve.tensor_copy(OT[:].rearrange("p c q -> p (c q)"), pT[:].rearrange("p b n -> p (b n)")).then_inc(ot_ready, 1)
                        dve.wait_ge(o_proj, n + 1)
                        dve.tensor_copy(into, pO[:, 0, 0:D]).then_inc(out_sem, 1)

                    dve.tensor_copy(O[:], repeat(nv[:], H)).then_inc(o_ready, 1)
                    project(0, ring_row[:, 0], dead_done)
                    dve.wait_ge(dead_done, 1)
                    dve.tensor_copy(xc[:], repeat(ring_row[:, 0], T)).then_inc(q_done, 1)

                    def queries(b, qt, nq):
                        dve.wait_ge(null_done, nq + 1)
                        dve.wait_ge(q_done, nq + 1)
                        dve.tensor_tensor(st[:, MAX].rearrange("p (c r) -> p r c", r=2), pO[:, :, 0:H // 2],
                                          nullb[:].rearrange("p (c r) -> p r c", r=2), ALU.add).then_inc(q_step, 1)
                        dve.memset(st[:, LEN], 1.0).then_inc(q_step, 1)
                        dve.tensor_copy(O[:], repeat(nv[:], H)).then_inc(q_step, 1)

                    def keys(b, qt, kt, nq, nk):
                        at = nk * KSTEP
                        dve.wait_ge(q_step, nq * QSTEP + 3)
                        dve.wait_ge(k_done, nk)
                        dve.wait_ge(k_step, at)
                        dve.wait_ge(bias_ready, nk + 1)
                        for g in range(4):
                            dve.wait_ge(s_done, nk * 4 + g + 1)
                            dve.tensor_tensor(by_bank(sc, g), pS[:, g].rearrange("p (i k) -> p i k", k=P),
                                              by_bank(bias_sb, g), ALU.add).then_inc(sc_ready, 1)
                        dve.wait_ge(sc_ready, nk * 4 + 4)
                        dve.tensor_reduce(st[:, TMAX], sc[:], AX, ALU.max).then_inc(k_step, 1)
                        dve.wait_ge(k_step, at + 1)
                        dve.tensor_tensor(st[:, TMAX], st[:, TMAX], st[:, MAX], ALU.max).then_inc(k_step, 1)
                        dve.wait_ge(k_step, at + 2)
                        dve.tensor_tensor(st[:, DIF], st[:, MAX], st[:, TMAX], ALU.subtract).then_inc(k_step, 1)
                        dve.tensor_scalar(st[:, NEG], st[:, TMAX], -1.0, None, ALU.mult).then_inc(k_step, 1)
                        dve.wait_ge(k_step, at + 4)
                        dve.tensor_copy(st[:, MAX], st[:, TMAX]).then_inc(k_step, 1)
                        for g in range(4):
                            dve.wait_ge(t_done, nk * 4 + g + 1)
                            if g:
                                dve.wait_ge(pt_ready, nk * 4 + g)
                            if g % 2 == 0 and g:
                                dve.wait_ge(pv_done, nk * 2 + g // 2)
                            dve.tensor_copy(PT[:].rearrange("p h q -> p (h q)"), pT[:, g % 2]).then_inc(pt_ready, 1)
                        dve.wait_ge(alpha_ready, nk + 1)
                        dve.tensor_tensor(O[:], O[:], bcast(st[:, ALPHA], DH), ALU.mult).then_inc(k_step, 1)
                        dve.tensor_tensor(st[:, LEN], st[:, LEN], st[:, ALPHA], ALU.mult).then_inc(k_step, 1)
                        dve.wait_ge(k_step, at + 7)
                        dve.tensor_tensor(st[:, LEN], st[:, LEN], st[:, RS], ALU.add).then_inc(k_step, 1)
                        dve.wait_ge(pv_done, nk * 2 + 2)
                        dve.tensor_tensor(O[:].rearrange("p h d -> p (h d)"), O[:].rearrange("p h d -> p (h d)"),
                                          pO[:].rearrange("p b n -> p (b n)"), ALU.add).then_inc(k_done, 1)

                    def after(b, qt, nq, nk):
                        dve.wait_ge(k_done, nk)
                        dve.wait_ge(k_step, nk * KSTEP)
                        dve.reciprocal(st[:, RL], st[:, LEN]).then_inc(q_step, 1)
                        dve.wait_ge(q_step, nq * QSTEP + 4)
                        dve.tensor_tensor(O[:], O[:], bcast(st[:, RL], DH), ALU.mult).then_inc(o_ready, 1)
                        project(nq + 1, xc[:, ds(b * QT + qt, 1)].rearrange("p a d -> p (a d)"), q_done)
                        dve.memset(st[:, RS], 0.0).then_inc(q_step, 1)
                        dve.memset(st[:, DIF], 0.0).then_inc(q_step, 1)

                    live_tiles(dve, "dve", queries, keys, after)
        att.close()
        if upto == "att":
            return

        with ExitStack() as mid:
            idx = sb("idx", [P, E0 + 2], U32, into=mid)
            gtab = sb("gtab", [P, E0 + 1], into=mid)
            b1_sb = sb("b1_sb", [P, E0, FC], into=mid)
            b2_sb = sb("b2_sb", [P, E0, D], into=mid)
            with ExitStack() as ph:
                go_b = sb("go_b", [P, D], into=ph)
                nw_b = sb("nw_b", [P, D], into=ph)
                rw_sb = sb("rw_sb", [P, KD, E0], into=ph)
                rb_b = sb("rb_b", [P, E0], into=ph)
                lg = sb("lg", [P, T, E0], into=ph)
                lgr = sb("lgr", [P, 2, E0], into=ph)
                top = sb("top", [P, 2, T], into=ph)
                LT = sb("LT", [E0, B * N], into=ph)
                best = sb("best", [E0, CAP], into=ph)
                picks = sb("picks", [E0, CAP], U32, into=ph)
                picksf = sb("picksf", [E0, CAP], into=ph)
                pt = [ps(f"c_pt{u}", [P, 512], ph) for u in range(2)]
                pl = [ps(f"c_pl{u}", [P, 512], ph) for u in range(2)]
                pq = [ps(f"c_pq{u}", [P, 512], ph) for u in range(2)]
                c_in, c_mom, c_root = sem("c_in"), sem("c_mom"), sem("c_root")
                y_norm, y_scaled, row_done, row_out, col_t, col_ready, lg_done, lg_row, lt_done, lt_kept = (
                    sem("y_norm"), sem("y_scaled"), sem("row_done"), sem("row_out"), sem("col_t"), sem("col_ready"),
                    sem("lg_done"), sem("lg_row"), sem("lt_done"), sem("lt_kept"))
                soft, soft_exp, gates_out, pick_step, pick_t = (
                    sem("soft"), sem("soft_exp"), sem("gates_out"), sem("pick_step"), sem("pick_t"))
                with nc.Block() as block:
                    @block.sync
                    def _(sp):
                        sp.dma_start(go_b[:], g_out.partition_broadcast(P)).then_inc(c_in, 16)
                        sp.dma_start(nw_b[:], norm_w.partition_broadcast(P)).then_inc(c_in, 16)
                        sp.dma_start(rw_sb[:], rw).then_inc(c_in, 16)
                        sp.dma_start(rb_b[:], rb.partition_broadcast(P)).then_inc(c_in, 16)
                        sp.dma_start(b1_sb[:], b1).then_inc(c_in, 16)
                        sp.dma_start(b2_sb[:].rearrange("p e d -> p (e d)"), b2.partition_broadcast(P)).then_inc(c_in, 16)
                        with sp.Fori(0, T // 2) as i:
                            for u in range(2):
                                sp.wait_ge(row_done, 2 * i + u + 1)
                                sp.dma_start(table[ds((2 * i + u) * P, P), 0:D], ring_row[:, u]).then_inc(row_out, 16)
                        sp.wait_ge(soft, 5)
                        sp.dma_start(table[:, D:ROW].rearrange("(t p) e -> p t e", p=P), lg[:]).then_inc(gates_out, 16)
                        sp.wait_ge(gates_out, 16)
                        sp.wait_ge(row_out, 16 * T)
                        sp.wait_ge(c_in, 16 * 6)

                    @block.vector
                    def _(dve):
                        steps = [0]

                        def link(ins):
                            steps[0] += 1
                            ins.then_inc(c_mom, 1)
                            dve.wait_ge(c_mom, steps[0])

                        def tile_stats(done):
                            with dve.Fori(0, T) as t:
                                dve.bn_stats(stats[:, ds(t, 1)].rearrange("p a s -> p (a s)"),
                                             xc[:, ds(t, 1)].rearrange("p a d -> p (a d)")).then_inc(c_mom, 1)
                            steps[0] += T
                            dve.wait_ge(c_mom, steps[0])
                            finish_moments(dve, link)

                        tile_stats(0)
                        link(dve.tensor_scalar(mom[:, TMP], mom[:, VAR], EPS, None, ALU.add))
                        dve.wait_ge(c_root, 1)
                        link(dve.reciprocal(mom[:, RSTD], mom[:, TMQ]))
                        dve.wait_ge(c_in, 16 * 6)
                        with dve.Fori(0, T) as t:
                            row = xc[:, ds(t, 1)].rearrange("p a d -> p (a d)")
                            dve.tensor_scalar(row, row, mom[:, MEAN, ds(t, 1)], mom[:, RSTD, ds(t, 1)],
                                              ALU.subtract, ALU.mult).then_inc(y_norm, 1)
                            dve.wait_ge(y_norm, t + 1)
                            dve.tensor_tensor(row, row, go_b[:], ALU.mult).then_inc(y_scaled, 1)
                        dve.wait_ge(y_scaled, T)
                        tile_stats(1)
                        link(dve.tensor_tensor(mom[:, MSQ], mom[:, MEAN], mom[:, MEAN], ALU.mult))
                        link(dve.scalar_tensor_tensor(mom[:, TMP], mom[:, VAR], EPS, mom[:, MSQ], ALU.add, ALU.add))
                        dve.wait_ge(c_root, 2)
                        link(dve.reciprocal(mom[:, RSTD], mom[:, TMQ]))

                        def keep_logits(i, u):
                            dve.wait_ge(lg_done, 2 * i + u + 1)
                            dve.tensor_tensor(lgr[:, u], pl[u][:, 0:E0], rb_b[:], ALU.add).then_inc(lg_row, 1)
                            dve.wait_ge(lg_row, 2 * i + u + 1)
                            dve.tensor_copy(lg[:, ds(2 * i + u, 1)].rearrange("p a e -> p (a e)"), lgr[:, u]).then_inc(lt_kept, 1)
                            dve.wait_ge(lt_done, 2 * i + u + 1)
                            dve.tensor_copy(LT[:, ds((2 * i + u) * P, P)], pq[u][0:E0, 0:P]).then_inc(lt_kept, 1)

                        with dve.Fori(0, T // 2) as i:
                            for u in range(2):
                                dve.wait_ge(row_out, 32 * i)
                                dve.wait_ge(col_t, 2 * i)
                                dve.scalar_tensor_tensor(ring_row[:, u], xc[:, ds(2 * i + u, 1)].rearrange("p a d -> p (a d)"),
                                                         mom[:, RSTD, ds(2 * i + u, 1)], nw_b[:], ALU.mult, ALU.mult).then_inc(row_done, 1)
                            for u in range(2):
                                keep_logits(i, u)
                        dve.wait_ge(lt_kept, 2 * T)
                        dve.tensor_reduce(top[:, 0], lg[:], AX, ALU.max).then_inc(soft, 1)
                        dve.wait_ge(soft, 1)
                        dve.tensor_tensor(lg[:], lg[:], bcast(top[:, 0], E0), ALU.subtract).then_inc(soft, 1)
                        dve.wait_ge(soft_exp, 1)
                        dve.tensor_reduce(top[:, 0], lg[:], AX, ALU.add).then_inc(soft, 1)
                        dve.wait_ge(soft, 3)
                        dve.reciprocal(top[:, 1], top[:, 0]).then_inc(soft, 1)
                        dve.wait_ge(soft, 4)
                        dve.tensor_tensor(lg[:], lg[:], bcast(top[:, 1], E0), ALU.mult).then_inc(soft, 1)
                        step = 0
                        for r in range(CAP // 8):
                            now = slice(8 * r, 8 * r + 8)
                            dve.max(best[:, now], LT[:]).then_inc(pick_step, 1)
                            dve.wait_ge(pick_step, step + 1)
                            dve.max_index(picks[:, now], best[:, now], LT[:]).then_inc(pick_step, 1)
                            dve.wait_ge(pick_step, step + 2)
                            dve.match_replace(LT[:], best[:, now], LT[:], -3e38).then_inc(pick_step, 1)
                            dve.wait_ge(pick_step, step + 3)
                            step += 3
                        dve.tensor_copy(picksf[:], picks[:]).then_inc(pick_step, 1)
                        dve.memset(idx[:], 0).then_inc(pick_step, 1)
                        dve.wait_ge(pick_t, 1)
                        dve.wait_ge(pick_step, step + 2)
                        dve.tensor_copy(idx[:, 0:E0], pq[0][:, 0:E0]).then_inc(pick_step, 1)
                        dve.wait_ge(pick_step, step + 3)

                    @block.scalar
                    def _(act):
                        act.wait_ge(c_mom, T + 8)
                        act.activation(mom[:, TMQ], mom[:, TMP], ACT.Sqrt).then_inc(c_root, 1)
                        act.wait_ge(c_mom, 2 * T + 18)
                        act.activation(mom[:, TMQ], mom[:, TMP], ACT.Sqrt).then_inc(c_root, 1)
                        with act.Fori(0, T // 2) as i:
                            for u in range(2):
                                act.wait_ge(col_t, 2 * i + u + 1)
                                act.wait_ge(lg_done, 2 * i)
                                act.activation(ring_col[:, u].rearrange("p k t -> p (k t)"), pt[u][:, 0:D], ACT.Copy).then_inc(col_ready, 1)
                        act.wait_ge(soft, 2)
                        act.activation(lg[:], lg[:], ACT.Exp).then_inc(soft_exp, 1)

                    @block.tensor
                    def _(pe):
                        pe.wait_ge(c_in, 16 * 6)
                        with pe.Fori(0, T // 2) as i:
                            for u in range(2):
                                pe.wait_ge(row_done, 2 * i + u + 1)
                                for k in range(KD):
                                    ins = pe.transpose(pt[u][:, k * P:(k + 1) * P], ring_row[:, u, k * P:(k + 1) * P], ident[:])
                                ins.then_inc(col_t, 1)
                            for u in range(2):
                                pe.wait_ge(col_ready, 2 * i + u + 1)
                                pe.wait_ge(lt_kept, 4 * i)
                                for k in range(KD):
                                    ins = pe.matmul(pl[u][:, 0:E0], ring_col[:, u, k], rw_sb[:, k], start=(k == 0), stop=(k == KD - 1))
                                ins.then_inc(lg_done, 1)
                                pe.wait_ge(lg_row, 2 * i + u + 1)
                                pe.transpose(pq[u][0:E0, 0:P], lgr[:, u], ident[:]).then_inc(lt_done, 1)
                        pe.wait_ge(pick_step, 3 * CAP // 8 + 1)
                        pe.transpose(pq[0][:, 0:E0], picksf[:], ident[0:E0, 0:E0]).then_inc(pick_t, 1)
            if upto == "route0":
                return

            def expert_phase(tag, src, width, dst, out_width, gidx, sidx, gates, from_row, b1t, b2t, w1t, w2t,
                             experts, act_fn, counts, preload):
                with ExitStack() as ph:
                    G = sb(tag + "G", [P, width + 1], into=ph)
                    XT = sb(tag + "XT", [P, KD, P], into=ph)
                    hT = sb(tag + "hT", [P, FC, P], into=ph)
                    yt = sb(tag + "yt", [P, D], into=ph)
                    yg = sb(tag + "yg", [P, out_width], into=ph)
                    pX = ps(tag + "pX", [P, 512], ph)
                    pH = ps(tag + "pH", [P, 2, 512], ph)
                    pY = ps(tag + "pY", [P, 512], ph)
                    names = ("gathered", "turned", "xt_ready", "fc1_done", "gelu_done", "fc2_done", "y_read", "yg_ready",
                             "scattered", "gi_set", "si_set", "spare_set")
                    (gathered, turned, xt_ready, fc1_done, gelu_done, fc2_done, y_read, yg_ready, scattered, gi_set,
                     si_set, spare_set) = [sem(f"{tag}_{n}") for n in names]

                    def per_block(eng, name, body, begin=None):
                        if counts is None:
                            with eng.Fori(0, experts // RING) as r:
                                for u in range(RING):
                                    if begin:
                                        begin(r, RING * r + u, u)
                                    body(RING * r + u, RING * r + u, u)
                            return
                        nblk, _ = counts
                        reg = eng.alloc_register(f"{tag}_{name}")
                        eng.reg_mov(reg, 0)
                        with eng.Fori(0, experts // RING) as r:
                            for u in range(RING):
                                e = RING * r + u
                                if begin:
                                    begin(r, e, u)
                                n = eng.value_load(nblk[0:1, ds(e, 1)], min_val=0, max_val=B * N // P)
                                with eng.If(n > 0):
                                    with eng.Fori(0, n):
                                        body(eng.snap(reg), e, u)
                                        eng.reg_add(reg, reg, 1)

                    with nc.Block() as block:
                        @block.sync
                        def _(sp):
                            if preload:
                                for u in range(RING):
                                    load_expert(sp, w1t, w2t, u, u)
                            with sp.Fori(0, experts // RING - 1) as r:
                                for u in range(RING):
                                    if counts is None:
                                        sp.wait_ge(fc2_done, RING * r + u + 1)
                                    else:
                                        end = sp.value_load(counts[1][0:1, ds(RING * r + u, 1)], min_val=0, max_val=BLK)
                                        sp.wait_ge(fc2_done, end)
                                    load_expert_at(sp, w1t, w2t, RING * r + u + RING, u)

                        @block.gpsimd
                        def _(pool):
                            def gather(j, done):
                                pool.tensor_copy(gi[:], gidx[:, ds(j, 1)] if not isinstance(j, int) else gidx[:, j:j + 1]).then_inc(gi_set, 1)
                                pool.wait_ge(gi_set, j + 1)
                                held_here(pool, 0)
                                pool.indirect_dma_start(G[:, 0:width], None, src, bass.IndirectOffsetOnAxis(ap=gi[:], axis=0)).then_inc(gathered, 16)

                            gather(0, 0)
                            pool.wait_ge(turned, 1)
                            pool.wait_ge(xt_ready, 1)
                            pool.wait_ge(gathered, 16)
                            gather(1, 1)

                            def body(j, e, u):
                                pool.wait_ge(turned, j + 2)
                                pool.wait_ge(xt_ready, j + 2)
                                pool.wait_ge(gathered, j * 16 + 32)
                                held_here(pool, 1)
                                gather(j + 2, 2)
                                pool.wait_ge(scattered, j * 16)
                                held_here(pool, 2)
                                pool.tensor_copy(si[:], sidx[:, ds(j, 1)]).then_inc(si_set, 1)
                                pool.wait_ge(yg_ready, j + 1)
                                pool.wait_ge(si_set, j + 1)
                                held_here(pool, 3)
                                pool.indirect_dma_start(dst, bass.IndirectOffsetOnAxis(ap=si[:], axis=0), yg[:], None,
                                                        compute_op=ALU.add).then_inc(scattered, 16)
                            per_block(pool, "pool", body)

                        @block.tensor
                        def _(pe):
                            def turn(j):
                                pe.wait_ge(gathered, j * 16 + 16)
                                for k in range(KD):
                                    ins = pe.transpose(pX[:, k * P:(k + 1) * P], G[:, k * P:(k + 1) * P], ident[:])
                                ins.then_inc(turned, 1)

                            turn(0)

                            def begin(r, e, u):
                                pe.wait_ge(w_in[u], r * 32 + (w_round[0] + 1) * 32)

                            def body(j, e, u):
                                pe.wait_ge(xt_ready, j + 1)
                                for c in range(FC):
                                    for k in range(KD):
                                        ins = pe.matmul(pH[:, c // 4, (c % 4) * P:(c % 4 + 1) * P], w1_sb[:, u, k, c * P:(c + 1) * P],
                                                        XT[:, k], start=(k == 0), stop=(k == KD - 1))
                                    if c % 4 == 3:
                                        ins.then_inc(fc1_done, 1)
                                turn(j + 1)
                                pe.wait_ge(y_read, j)
                                for c in range(FC):
                                    pe.wait_ge(gelu_done, j * FC + c + 1)
                                    ins = pe.matmul(pY[:, 0:D], hT[:, c], w2_sb[:, u, c], start=(c == 0), stop=(c == FC - 1))
                                ins.then_inc(fc2_done, 1)
                            per_block(pe, "pe", body, begin)

                        @block.scalar
                        def _(act):
                            def body(j, e, u):
                                act.wait_ge(fc2_done, j)
                                for c in range(FC):
                                    if c % 4 == 0:
                                        act.wait_ge(fc1_done, j * 2 + c // 4 + 1)
                                    act.activation(hT[:, c], pH[:, c // 4, (c % 4) * P:(c % 4 + 1) * P], act_fn,
                                                   bias=b1t[:, ds(e, 1), c]).then_inc(gelu_done, 1)
                            per_block(act, "act", body)

                        @block.vector
                        def _(dve):
                            def column(j):
                                dve.wait_ge(turned, j + 1)
                                if from_row:
                                    dve.tensor_scalar(gates[:, ds(j, 1)] if not isinstance(j, int) else gates[:, 0:1],
                                                      G[:, ds(D + j, 1)] if not isinstance(j, int) else G[:, D:D + 1],
                                                      1.0, None, ALU.mult)
                                dve.tensor_copy(XT[:].rearrange("p k t -> p (k t)"), pX[:, 0:D]).then_inc(xt_ready, 1)

                            dve.memset(G[:, width:width + 1], 0.0).then_inc(spare_set, 1)
                            dve.wait_ge(spare_set, 1)
                            column(0)

                            def body(j, e, u):
                                dve.wait_ge(fc1_done, j * 2 + 2)
                                column(j + 1)
                                dve.wait_ge(fc2_done, j + 1)
                                dve.wait_ge(yg_ready, j)
                                dve.tensor_tensor(yt[:], pY[:, 0:D], b2t[:, ds(e, 1)].rearrange("p a d -> p (a d)"), ALU.add).then_inc(y_read, 1)
                                dve.wait_ge(y_read, j + 1)
                                dve.wait_ge(scattered, j * 16)
                                gate = gates[:, ds(j, 1)]
                                if out_width > D:
                                    dve.tensor_scalar(yg[:, D:D + 1], gate, 1.0, None, ALU.mult)
                                dve.tensor_scalar(yg[:, 0:D], yt[:], gate, None, ALU.mult).then_inc(yg_ready, 1)
                            per_block(dve, "dve", body)

                    return gathered, scattered

            w_round = [0]
            expert_phase("m", table, ROW, acc0, D + 1, idx, idx, gtab, True, b1_sb, b2_sb, w1, w2,
                         E0, ACT.Gelu, None, False)
        if upto == "moe0":
            return

        late = ctx.enter_context(ExitStack())
        W = sb("W", [P, T, EG], into=late)
        lg = sb("lg2", [P, T, E1], into=late)
        oh = sb("oh", [P, 2, T, E1], into=late)
        best2 = sb("best2", [P, 2, T], into=late)
        red = sb("red", [P, 2, T], into=late)
        scr = sb("scr", [P, T, E1], into=late)
        rev = sb("rev", [P, E1], into=late)
        lgc = sb("lgc", [P, B, E1], into=late)
        c1_sb = sb("c1_sb", [P, E1, FC], into=late)
        c2_sb = sb("c2_sb", [P, E1, D], into=late)
        zpad = sb("zpad", [P, D], into=late)
        late_const = sem("late_const")
        c_late = sem("c_late")
        acc1_set = sem("acc1_set")

        def softmax(dve, link, link_exp):
            link(dve.tensor_reduce(red[:, 0], lg[:], AX, ALU.max))
            link(dve.tensor_tensor(lg[:], lg[:], bcast(red[:, 0], E1), ALU.subtract))
            link_exp()
            link(dve.tensor_reduce(red[:, 0], lg[:], AX, ALU.add))
            link(dve.reciprocal(red[:, 1], red[:, 0]))
            link(dve.tensor_tensor(lg[:], lg[:], bcast(red[:, 1], E1), ALU.mult))

        def top_two(dve, link):
            for n in range(2):
                link(dve.tensor_reduce(best2[:, n], lg[:], AX, ALU.max))
                link(dve.tensor_tensor(scr[:], lg[:], bcast(best2[:, n], E1), ALU.is_equal))
                link(dve.tensor_tensor(scr[:], scr[:], repeat(rev[:], T), ALU.mult))
                link(dve.tensor_reduce(red[:, 0], scr[:], AX, ALU.max))
                link(dve.tensor_tensor(oh[:, n], scr[:], bcast(red[:, 0], E1), ALU.is_equal))
                if n == 0:
                    link(dve.scalar_tensor_tensor(lg[:], oh[:, 0], -4.0, lg[:], ALU.mult, ALU.add))

        with ExitStack() as x1s:
            x1T = sb("x1T", [P, KD, B * N], into=x1s)
            with ExitStack() as ph:
                sums = sb("sums", [P, T, D + 1], into=ph)
                den = sb("den", [P, 2, T], into=ph)
                wt_sb = sb("wt_sb", [P, KD, E1], into=ph)
                wg_sb = sb("wg_sb", [DH, E1], into=ph)
                cT = sb("cT", [DH, B], into=ph)
                cB = sb("cB", [DH, B, P], into=ph)
                pt = [ps(f"f_pt{u}", [P, 512], ph) for u in range(2)]
                pl = [ps(f"f_pl{u}", [P, 512], ph) for u in range(2)]
                pc = ps("f_pc", [P, 512], ph)
                sums_in, f_in, f_step, row_ready, row_kept, turned, col_ready, col_kept, lg_done, lg_kept, cond_done, cond_b, f_exp = [
                    sem(f"f_{n}") for n in ("sums_in", "in", "step", "row_ready", "row_kept", "turned", "col_ready", "col_kept",
                                            "lg_done", "lg_kept", "cond_done", "cond_b", "exp")]
                with nc.Block() as block:
                    @block.sync
                    def _(sp):
                        sp.dma_start(sums[:], acc0.rearrange("(t p) d -> p t d", p=P)).then_inc(sums_in, 16)
                        sp.dma_start(wt_sb[:], wt).then_inc(f_in, 16)
                        sp.dma_start(wg_sb[:], wg).then_inc(f_in, 16)
                        sp.dma_start(cT[:], condT).then_inc(f_in, 16)
                        sp.dma_start(c1_sb[:], c1).then_inc(c_late, 16)
                        sp.dma_start(c2_sb[:].rearrange("p e d -> p (e d)"), c2.partition_broadcast(P)).then_inc(c_late, 16)
                        for u in range(RING):
                            load_expert(sp, v1, v2, u, u)
                        sp.wait_ge(row_kept, T)
                        sp.dma_start(acc1[0:B * N, :].rearrange("(t p) d -> p t d", p=P), x_sb[:]).then_inc(acc1_set, 16)
                        sp.wait_ge(late_const, 2)
                        sp.dma_start(acc1[B * N:B * N + P, :], zpad[:]).then_inc(acc1_set, 16)
                        sp.wait_ge(f_in, 48)
                        sp.wait_ge(c_late, 32)

                    @block.gpsimd
                    def _(pool):
                        pool.iota(rev[:], pattern=[[-1, E1]], base=E1, channel_multiplier=0,
                                  allow_small_or_imprecise_dtypes=True).then_inc(late_const, 1)
                        pool.memset(zpad[:], 0.0).then_inc(late_const, 1)
                        pool.memset(W[:, :, E1:EG], 1.0).then_inc(late_const, 1)
                        with pool.Fori(0, T // 2) as i:
                            for u in range(2):
                                t = 2 * i + u
                                pool.wait_ge(row_ready, t + 1)
                                pool.tensor_tensor(held[:, u:u + 1], ones[:, 0:1], ones[:, 0:1], ALU.mult)
                                pool.tensor_copy(x_sb[:, ds(t, 1)].rearrange("p a d -> p (a d)"), ring_row[:, u]).then_inc(row_kept, 1)
                                pool.wait_ge(col_ready, t + 1)
                                pool.wait_ge(row_kept, t + 1)
                                pool.tensor_tensor(held[:, 2 + u:3 + u], ones[:, 0:1], ones[:, 0:1], ALU.mult)
                                pool.tensor_copy(x1T[:, :, ds(t * P, P)], ring_col[:, u]).then_inc(col_kept, 1)

                    @block.vector
                    def _(dve):
                        steps = [0]

                        def link(ins):
                            steps[0] += 1
                            ins.then_inc(f_step, 1)
                            dve.wait_ge(f_step, steps[0])

                        dve.wait_ge(f_in, 48)
                        dve.tensor_copy(cB[:], bcast(cT[:], P)).then_inc(cond_b, 1)
                        dve.wait_ge(sums_in, 16)
                        link(dve.tensor_scalar(den[:, 0], sums[:, :, D], 0.0, None, ALU.is_le))
                        link(dve.tensor_tensor(den[:, 0], den[:, 0], sums[:, :, D], ALU.add))
                        link(dve.reciprocal(den[:, 1], den[:, 0]))
                        with dve.Fori(0, T // 2) as i:
                            for u in range(2):
                                dve.wait_ge(row_kept, 2 * i)
                                dve.wait_ge(turned, 2 * i)
                                t = 2 * i + u
                                dve.scalar_tensor_tensor(ring_row[:, u], sums[:, ds(t, 1), 0:D].rearrange("p a d -> p (a d)"),
                                                         den[:, 1, ds(t, 1)], x_sb[:, ds(t, 1)].rearrange("p a d -> p (a d)"),
                                                         ALU.mult, ALU.add).then_inc(row_ready, 1)
                            for u in range(2):
                                dve.wait_ge(lg_done, 2 * i + u + 1)
                                dve.tensor_scalar(lg[:, ds(2 * i + u, 1)].rearrange("p a e -> p (a e)"), pl[u][:, 0:E1],
                                                  1.0, None, ALU.mult).then_inc(lg_kept, 1)
                        dve.wait_ge(lg_kept, T)
                        dve.wait_ge(cond_done, 1)
                        link(dve.tensor_copy(lgc[:].rearrange("p b e -> p (b e)"), pc[:, 0:B * E1]))
                        for b in range(B):
                            link(dve.tensor_tensor(lg[:, b * QT:(b + 1) * QT], lg[:, b * QT:(b + 1) * QT], repeat(lgc[:, b], QT), ALU.add))
                        softmax(dve, link, lambda: dve.wait_ge(f_exp, 1))
                        dve.wait_ge(late_const, 3)
                        top_two(dve, link)
                        link(dve.tensor_tensor(red[:, 0], best2[:, 0], best2[:, 1], ALU.add))
                        link(dve.tensor_scalar(red[:, 0], red[:, 0], 1e-20, None, ALU.add))
                        link(dve.reciprocal(red[:, 1], red[:, 0]))
                        for n in range(2):
                            link(dve.tensor_tensor(best2[:, n], best2[:, n], red[:, 1], ALU.mult))
                        link(dve.tensor_tensor(scr[:], oh[:, 0], bcast(best2[:, 0], E1), ALU.mult))
                        link(dve.tensor_tensor(lg[:], oh[:, 1], bcast(best2[:, 1], E1), ALU.mult))
                        link(dve.tensor_tensor(W[:, :, 0:E1], scr[:], lg[:], ALU.add))

                    @block.scalar
                    def _(act):
                        with act.Fori(0, T // 2) as i:
                            for u in range(2):
                                act.wait_ge(turned, 2 * i + u + 1)
                                act.wait_ge(lg_done, 2 * i)
                                act.wait_ge(col_kept, 2 * i)
                                act.activation(ring_col[:, u].rearrange("p k t -> p (k t)"), pt[u][:, 0:D], ACT.Copy).then_inc(col_ready, 1)
                        act.wait_ge(f_step, 8)
                        act.activation(lg[:], lg[:], ACT.Exp, scale=0.5).then_inc(f_exp, 1)

                    @block.tensor
                    def _(pe):
                        pe.wait_ge(cond_b, 1)
                        for b in range(B):
                            ins = pe.matmul(pc[:, b * E1:(b + 1) * E1], cB[:, b], wg_sb[:], start=True, stop=True)
                        ins.then_inc(cond_done, 1)
                        with pe.Fori(0, T // 2) as i:
                            for u in range(2):
                                pe.wait_ge(row_ready, 2 * i + u + 1)
                                for k in range(KD):
                                    ins = pe.transpose(pt[u][:, k * P:(k + 1) * P], ring_row[:, u, k * P:(k + 1) * P], ident[:])
                                ins.then_inc(turned, 1)
                            for u in range(2):
                                pe.wait_ge(col_ready, 2 * i + u + 1)
                                pe.wait_ge(lg_kept, 2 * i)
                                for k in range(KD):
                                    ins = pe.matmul(pl[u][:, 0:E1], ring_col[:, u, k], wt_sb[:, k], start=(k == 0), stop=(k == KD - 1))
                                ins.then_inc(lg_done, 1)
            if upto == "x1":
                return

            with ExitStack() as ph:
                NCH, CH = 4, 512
                STEPS = EG * NCH
                gw = sb("gw", [P, 2, KD, M1], into=ph)
                uw = sb("uw", [P, 2, KD, M1], into=ph)
                dw = sb("dw", [P, 2, D], into=ph)
                ga = sb("ga", [P, CH], into=ph)
                lk = sb("lk", [P, CH], into=ph)
                hid = sb("hid", [P, 2, CH], into=ph)
                pG = ps("pG", [P, 2, 512], ph)
                pU = ps("pU", [P, 2, 512], ph)
                pY = ps("pYc", [P, 2, 2, 512], ph)
                cw_in = [sem(f"cw_in{u}") for u in range(2)]
                up_done, ga_ready, lk_ready, hid_ready, down_done, acc_done = [
                    sem(f"d_{n}") for n in ("up_done", "ga_ready", "lk_ready", "hid_ready", "down_done", "acc_done")]

                def all_steps(eng, body):
                    def pair(r, peeled):
                        for u in range(2):
                            for c in range(NCH):
                                body(2 * r + u, (2 * r + u) * NCH + c, u, c, peeled and u == 1 and c == NCH - 1)
                    with eng.Fori(0, EG // 2 - 1) as r:
                        pair(r, False)
                    pair(EG // 2 - 1, True)

                with nc.Block() as block:
                    @block.sync
                    def _(sp):
                        def load(e, u):
                            one = ds(e, 1)
                            sp.dma_start(gw[:, u], wgate[one].rearrange("a (k p) m -> p (a k) m", p=P)).then_inc(cw_in[u], 16)
                            sp.dma_start(uw[:, u], wup[one].rearrange("a (k p) m -> p (a k) m", p=P)).then_inc(cw_in[u], 16)
                            sp.dma_start(dw[:, u], wdown[one].rearrange("a p d -> p (a d)")).then_inc(cw_in[u], 16)
                        for u in range(2):
                            load(u, u)
                        with sp.Fori(0, EG // 2 - 1) as r:
                            for u in range(2):
                                sp.wait_ge(down_done, (2 * r + u + 1) * NCH)
                                load(2 * r + u + 2, u)
                        sp.wait_ge(acc1_set, 32)

                    @block.tensor
                    def _(pe):
                        def up(s, u, c, at):
                            for ww, pp in ((gw, pG), (uw, pU)):
                                for k in range(KD):
                                    ins = pe.matmul(pp[:, at], ww[:, u, k], x1T[:, k, c * CH:(c + 1) * CH],
                                                    start=(k == 0), stop=(k == KD - 1))
                            ins.then_inc(up_done, 1)

                        pe.wait_ge(cw_in[0], 48)
                        up(0, 0, 0, 0)

                        def body(e, s, u, c, last):
                            if not last:
                                if c == NCH - 1:
                                    r = (e - u) // 2 if isinstance(e, int) else None
                                    nxt = 1 - u
                                    rounds = (s - (u * NCH + c)) * 6
                                    pe.wait_ge(cw_in[nxt], rounds + (48 if u == 0 else 96))
                                pe.wait_ge(hid_ready, s)
                                up(s + 1, u if c < NCH - 1 else 1 - u, (c + 1) % NCH, (c + 1) % 2)
                            pe.wait_ge(hid_ready, s + 1)
                            pe.wait_ge(acc_done, s)
                            for j in range(4):
                                ins = pe.matmul(pY[:, c % 2, j // 2, (j % 2) * D:(j % 2 + 1) * D], hid[:, c % 2, j * P:(j + 1) * P],
                                                dw[:, u], start=True, stop=True)
                            ins.then_inc(down_done, 1)
                        all_steps(pe, body)

                    @block.scalar
                    def _(act):
                        def body(e, s, u, c, last):
                            act.wait_ge(up_done, s + 1)
                            act.wait_ge(hid_ready, s)
                            act.activation(ga[:], pG[:, c % 2], ACT.Copy).then_inc(ga_ready, 1)
                        all_steps(act, body)

                    @block.vector
                    def _(dve):
                        dve.memset(xc[:], 0.0).then_inc(acc_done, 1)

                        def hidden(s, at):
                            dve.wait_ge(ga_ready, s + 1)
                            dve.scalar_tensor_tensor(lk[:], ga[:], 0.01, ga[:], ALU.mult, ALU.max).then_inc(lk_ready, 1)
                            dve.wait_ge(lk_ready, s + 1)
                            dve.tensor_tensor(hid[:, at], lk[:], pU[:, at], ALU.mult).then_inc(hid_ready, 1)

                        hidden(0, 0)

                        def body(e, s, u, c, last):
                            if not last:
                                dve.wait_ge(hid_ready, s + 1)
                                hidden(s + 1, (c + 1) % 2)
                            dve.wait_ge(down_done, s + 1)
                            dve.wait_ge(acc_done, s + 1)
                            for j in range(4):
                                t = 4 * c + j
                                ins = dve.scalar_tensor_tensor(xc[:, t], pY[:, c % 2, j // 2, (j % 2) * D:(j % 2 + 1) * D],
                                                               W[:, t, ds(e, 1)], xc[:, t], ALU.mult, ALU.add)
                            ins.then_inc(acc_done, 1)
                        all_steps(dve, body)
        if upto == "y":
            return

        COLS = BLK + 2
        gtab = sb("gates2", [P, COLS], into=late)
        gidx = sb("gidx", [P, COLS], U32, into=late)
        sidx = sb("sidx", [P, COLS], U32, into=late)
        nblk = sb("nblk", [1, E1], I32, into=late)
        ends = sb("ends", [1, E1], I32, into=late)
        with ExitStack() as ph:
            wr_sb = sb("wr_sb", [P, KD, E1], into=ph)
            before = sb("before", [P, P], into=ph)
            zeros = sb("zeros", [P, P], into=ph)
            lane = sb("lane", [P, P], into=ph)
            token = sb("token", [P, T], into=ph)
            spare = sb("spare", [P, 1], into=ph)
            M = sb("M", [P, T, E1], into=ph)
            tot = sb("tot", [P, 2, T, E1], into=ph)
            slot = sb("slot", [P, T, E1], into=ph)
            blocks = sb("blocks", [P, 4, E1], into=ph)
            blocksi = sb("blocksi", [P, 2, E1], I32, into=ph)
            at = sb("at", [P, 2, T], into=ph)
            ati = sb("ati", [P, 2, 2, T], I32, into=ph)
            lanes = sb("lanes", [P, 2, T], into=ph)
            block_of = sb("block_of", [P, 2, T], into=ph)
            A = sb("A", [P, 2, P], into=ph)
            Bv = sb("Bv", [P, 2, 3, COLS], into=ph)
            empty = sb("empty", [P, COLS], into=ph)
            pt = [ps(f"h_pt{u}", [P, 512], ph) for u in range(2)]
            pl = [ps(f"h_pl{u}", [P, 512], ph) for u in range(2)]
            pP = ps("h_pP", [P, 512], ph)
            pQ = ps("h_pQ", [P, 512], ph)
            pM = ps("h_pM", [P, 512], ph)
            (h_in, h_const, h_step, row_ready, row_out, turned, col_ready, lg_done, lg_kept, h_exp, counted, a_ready,
             a_used) = [sem(f"h_{n}") for n in ("in", "const", "step", "row_ready", "row_out", "turned", "col_ready", "lg_done",
                                                "lg_kept", "exp", "counted", "a_ready", "a_used")]
            m_ready = sem("h_m_ready")
            with nc.Block() as block:
                @block.sync
                def _(sp):
                    sp.dma_start(wr_sb[:], wr).then_inc(h_in, 16)
                    with sp.Fori(0, T // 2) as i:
                        for u in range(2):
                            sp.wait_ge(row_ready, 2 * i + u + 1)
                            sp.dma_start(ytab[ds((2 * i + u) * P, P), :], ring_row[:, u]).then_inc(row_out, 16)
                    sp.wait_ge(row_out, 16 * T)
                    sp.wait_ge(h_in, 16)

                @block.gpsimd
                def _(pool):
                    pool.iota(lane[:], pattern=[[1, P]], base=0, channel_multiplier=0,
                              allow_small_or_imprecise_dtypes=True).then_inc(h_const, 1)
                    pool.iota(token[:], pattern=[[P, T]], base=0, channel_multiplier=1,
                              allow_small_or_imprecise_dtypes=True).then_inc(h_const, 1)
                    pool.iota(spare[:], pattern=[[0, 1]], base=B * N, channel_multiplier=1,
                              allow_small_or_imprecise_dtypes=True).then_inc(h_const, 1)
                    pool.memset(zeros[:], 0.0).then_inc(h_const, 1)
                    pool.affine_select(out=before[:], in_=ones[:], compare_op=ALU.is_ge, fill=0.0, base=-1,
                                       pattern=[[1, P]], channel_multiplier=-1).then_inc(h_const, 1)

                @block.vector
                def _(dve):
                    steps = [0]

                    def link(ins):
                        steps[0] += 1
                        ins.then_inc(h_step, 1)
                        dve.wait_ge(h_step, steps[0])

                    with dve.Fori(0, T // 2) as i:
                        for u in range(2):
                            dve.wait_ge(row_out, 32 * i)
                            dve.wait_ge(turned, 2 * i)
                            dve.tensor_scalar(ring_row[:, u], xc[:, ds(2 * i + u, 1)].rearrange("p a d -> p (a d)"),
                                              1.0, None, ALU.mult).then_inc(row_ready, 1)
                        for u in range(2):
                            dve.wait_ge(lg_done, 2 * i + u + 1)
                            dve.tensor_scalar(lg[:, ds(2 * i + u, 1)].rearrange("p a e -> p (a e)"), pl[u][:, 0:E1],
                                              1.0, None, ALU.mult).then_inc(lg_kept, 1)
                    dve.wait_ge(lg_kept, T)
                    softmax(dve, link, lambda: dve.wait_ge(h_exp, 1))
                    top_two(dve, link)
                    dve.wait_ge(h_const, 5)
                    dve.tensor_tensor(M[:], oh[:, 0], oh[:, 1], ALU.add).then_inc(m_ready, 1)
                    dve.wait_ge(counted, 1)
                    link(dve.tensor_copy(tot[:, 0].rearrange("p t e -> p (t e)"), pQ[:, 0:T * E1]))
                    for n in range(4):
                        a, b, w = n % 2, (n + 1) % 2, 1 << n
                        link(dve.tensor_copy(tot[:, b, 0:w], tot[:, a, 0:w]))
                        link(dve.tensor_tensor(tot[:, b, w:T], tot[:, a, w:T], tot[:, a, 0:T - w], ALU.add))
                    link(dve.tensor_scalar(blocksi[:, 0], tot[:, 0, T - 1], float(P - 1), None, ALU.add))
                    link(dve.tensor_scalar(blocksi[:, 1], blocksi[:, 0], 7, None, ALU.arith_shift_right))
                    link(dve.tensor_copy(blocks[:, 0], blocksi[:, 1]))
                    link(dve.tensor_copy(blocks[:, 3], blocks[:, 0]))
                    for n in range(3):
                        a, b, w = (0, 1, 2)[n], (1, 2, 0)[n], 1 << n
                        link(dve.tensor_copy(blocks[:, b, 0:w], blocks[:, a, 0:w]))
                        link(dve.tensor_tensor(blocks[:, b, w:E1], blocks[:, a, w:E1], blocks[:, a, 0:E1 - w], ALU.add))
                    link(dve.tensor_copy(nblk[:], blocks[0:1, 3]))
                    link(dve.tensor_copy(ends[:], blocks[0:1, 0]))
                    link(dve.tensor_tensor(blocks[:, 3], blocks[:, 0], blocks[:, 3], ALU.subtract))
                    link(dve.tensor_scalar(blocks[:, 3], blocks[:, 3], float(P), None, ALU.mult))
                    link(dve.tensor_copy(slot[:, 0], blocks[:, 3]))
                    link(dve.tensor_tensor(slot[:, 1:T], tot[:, 0, 0:T - 1], repeat(blocks[:, 3], T - 1), ALU.add))
                    link(dve.tensor_tensor(slot[:].rearrange("p t e -> p (t e)"), slot[:].rearrange("p t e -> p (t e)"),
                                           pP[:, 0:T * E1], ALU.add))
                    for n in range(2):
                        link(dve.tensor_tensor(scr[:], slot[:], oh[:, n], ALU.mult))
                        link(dve.tensor_reduce(at[:, n], scr[:], AX, ALU.add))
                    link(dve.tensor_copy(ati[:, 0], at[:]))
                    link(dve.tensor_scalar(ati[:, 1], ati[:, 0], P - 1, None, ALU.bitwise_and))
                    link(dve.tensor_copy(lanes[:], ati[:, 1]))
                    link(dve.tensor_scalar(ati[:, 1], ati[:, 0], 7, None, ALU.arith_shift_right))
                    link(dve.tensor_copy(block_of[:], ati[:, 1]))
                    with dve.Fori(0, T) as t:
                        for n in range(2):
                            dve.wait_ge(a_used, 2 * t)
                            dve.tensor_scalar(A[:, n], lane[:], lanes[:, n, ds(t, 1)], None, ALU.is_equal)
                            cols = lane[:, 0:COLS]
                            mine = block_of[:, n, ds(t, 1)]
                            dve.tensor_scalar(Bv[:, n, 0], cols, mine, token[:, ds(t, 1)], ALU.is_equal, ALU.mult)
                            dve.tensor_scalar(Bv[:, n, 1], cols, mine, best2[:, n, ds(t, 1)], ALU.is_equal, ALU.mult)
                            dve.tensor_scalar(Bv[:, n, 2], cols, mine, None, ALU.is_equal).then_inc(a_ready, 1)
                    dve.wait_ge(a_used, 2 * T + 1)
                    link(dve.tensor_copy(gidx[:], pM[:, 0:COLS]))
                    link(dve.tensor_copy(gtab[:], pM[:, COLS:2 * COLS]))
                    link(dve.tensor_scalar(empty[:], pM[:, 2 * COLS:3 * COLS], -1.0, 1.0, ALU.mult, ALU.add))
                    link(dve.tensor_scalar(empty[:], empty[:], spare[:, 0:1], None, ALU.mult))
                    link(dve.tensor_tensor(sidx[:], empty[:], pM[:, 0:COLS], ALU.add))

                @block.scalar
                def _(act):
                    with act.Fori(0, T // 2) as i:
                        for u in range(2):
                            act.wait_ge(turned, 2 * i + u + 1)
                            act.wait_ge(lg_done, 2 * i)
                            act.activation(ring_col[:, u].rearrange("p k t -> p (k t)"), pt[u][:, 0:D], ACT.Copy).then_inc(col_ready, 1)
                    act.wait_ge(h_step, 2)
                    act.activation(lg[:], lg[:], ACT.Exp).then_inc(h_exp, 1)

                @block.tensor
                def _(pe):
                    pe.wait_ge(h_in, 16)
                    with pe.Fori(0, T // 2) as i:
                        for u in range(2):
                            pe.wait_ge(row_ready, 2 * i + u + 1)
                            for k in range(KD):
                                ins = pe.transpose(pt[u][:, k * P:(k + 1) * P], ring_row[:, u, k * P:(k + 1) * P], ident[:])
                            ins.then_inc(turned, 1)
                        for u in range(2):
                            pe.wait_ge(col_ready, 2 * i + u + 1)
                            pe.wait_ge(lg_kept, 2 * i)
                            for k in range(KD):
                                ins = pe.matmul(pl[u][:, 0:E1], ring_col[:, u, k], wr_sb[:, k], start=(k == 0), stop=(k == KD - 1))
                            ins.then_inc(lg_done, 1)
                    pe.wait_ge(h_const, 5)
                    pe.wait_ge(m_ready, 1)
                    pe.matmul(pP[:, 0:T * E1], before[:], M[:].rearrange("p t e -> p (t e)"), start=True, stop=True)
                    pe.matmul(pQ[:, 0:T * E1], ones[:], M[:].rearrange("p t e -> p (t e)"), start=True, stop=True).then_inc(counted, 1)
                    pe.matmul(pM[:, 0:P], zeros[:], zeros[:], start=True, stop=False)
                    with pe.Fori(0, T) as t:
                        for n in range(2):
                            pe.wait_ge(a_ready, 2 * t + n + 1)
                            pe.matmul(pM[:, 0:3 * COLS], A[:, n], Bv[:, n].rearrange("p v c -> p (v c)"),
                                      start=False, stop=False).then_inc(a_used, 1)
                    pe.matmul(pM[:, 0:P], zeros[:], zeros[:], start=False, stop=True).then_inc(a_used, 1)
        if upto == "route1":
            return

        w_round[0] = E0 // RING
        expert_phase("n", ytab, D, acc1, D, gidx, sidx, gtab, False, c1_sb, c2_sb, v1, v2,
                     E1, ACT.Gelu_apprx_tanh, (nblk, ends), False)
        late.close()
        result_out = sem("result_out")
        with nc.Block() as block:
            @block.sync
            def _(sp):
                sp.dma_start(out.rearrange("b n d -> (b n) d"), acc1[0:B * N, :]).then_inc(result_out, 16)
                sp.wait_ge(result_out, 16)


_OUTS = [((B, N, D), "float32")]


def kernel(**i):
    import numpy as np
    import concourse.bacc as bacc
    from concourse.bass_utils import run_bass_kernel_spmd as run

    halves = lambda w: w.reshape(D, 2, M1).transpose(1, 0, 2)
    cols = lambda w: w.reshape(KD, P, -1).transpose(1, 0, 2)
    laid = {
        "x": i["x"], "bias": i["fside_16xSxS_0"], "cond": i["cond_64"], "condT": i["cond_64"].T,
        "mask": i["mask_BxS_bk0"].reshape(1, B * N),
        "g_in": i["L0_cond_g_in"].reshape(KD, P).T, "null_bias": i["L0_cond_null_attn_bias"].reshape(1, H),
        "wq": i["L0_cond_Wq"], "wkv": i["L0_cond_Wkv"], "wo": i["L0_cond_Wo"],
        "g_out": i["L0_cond_g_out"].reshape(1, D), "norm_w": i["L0_ffn_norm_weight"].reshape(1, D),
        "rw": cols(np.asarray(i["L0_ffn_router_weight"]).T), "rb": i["L0_ffn_router_bias"].reshape(1, E0),
        "w1": i["L0_ffn_fc1_weight"].transpose(0, 2, 1), "b1": i["L0_ffn_fc1_bias"].reshape(E0, FC, P).transpose(2, 0, 1),
        "w2": i["L0_ffn_fc2_weight"].transpose(0, 2, 1), "b2": i["L0_ffn_fc2_bias"].reshape(1, E0 * D),
        "wt": cols(np.asarray(i["L1_cond_wt"]).T), "wg": i["L1_cond_wg"].T,
        "wgate": np.concatenate([i["L1_cond_w_gate"], halves(i["L1_cond_sw_gate"])]),
        "wup": np.concatenate([i["L1_cond_w_up"], halves(i["L1_cond_sw_up"])]),
        "wdown": np.concatenate([i["L1_cond_w_down"], i["L1_cond_sw_down"].reshape(2, M1, D)]),
        "wr": cols(i["L1_ffn_w_router"]), "v1": i["L1_ffn_w1"],
        "c1": i["L1_ffn_b1"].reshape(E1, FC, P).transpose(2, 0, 1),
        "v2": i["L1_ffn_w2"], "c2": i["L1_ffn_b2"].reshape(1, E1 * D),
    }
    nc = bacc.Bacc("TRN2", target_bir_lowering=False, num_devices=1)
    arrays, args = {}, []
    for name, a in laid.items():
        a = np.ascontiguousarray(a)
        arrays[f"in_{name}"] = a
        args.append(nc.dram_tensor(f"in_{name}", a.shape, mybir.dt.from_np(a.dtype), kind="ExternalInput").ap())
    shape, dtype = _OUTS[0]
    result = nc.dram_tensor("out_0", shape, mybir.dt.from_np(np.dtype(dtype)), kind="ExternalOutput").ap()
    moe_kernel(nc, *args, result)
    r = run(nc, [arrays], core_ids=[0])
    return r.results[0]["out_0"]
```

```python
from contextlib import ExitStack

import concourse.bass as bass
from concourse import mybir

P = 128
F32 = mybir.dt.float32
I32 = mybir.dt.int32
U32 = mybir.dt.uint32
U8 = mybir.dt.uint8
ALU = mybir.AluOpType
ACT = mybir.ActivationFunctionType
AX = mybir.AxisListType.X
ds = bass.ds

B, N, D = 2, 1024, 256
KD = D // P
T = B * N // P
QT = N // P
H, DH = 16, 64
E0, F0 = 16, 1024
FC = F0 // P
CAP = B * N // E0
E1, M1 = 8, 128
EG = E1 + 2
BLK = 2 * B * N // P + E1
ROW = D + E0
RING = 4
EPS = 1e-5
HIDE = -1e38
CPE = P // E0
CW = B * N // CPE
assert CAP == P and F0 == 1024


def bcast(ap, n):
    return ap.unsqueeze(2).to_broadcast([ap.shape[0], ap.shape[1], n])


def repeat(ap, n):
    return ap.unsqueeze(1).to_broadcast([ap.shape[0], n, ap.shape[1]])


def done(n):
    return n + 1


def moe_kernel(nc, x, bias, cond, condT, mask, g_in, null_bias, wq, wkv, wo, g_out, norm_w, rw, rb,
               w1, b1, w2, b2, wt, wg, wgate, wup, wdown, wr, v1, c1, v2, c2, out, upto="end"):
    with ExitStack() as ctx:
        def sem(name):
            return ctx.enter_context(nc.semaphore(name))

        def sb(name, shape, dt=F32, into=ctx):
            return into.enter_context(nc.sbuf_tensor(name, shape, dt))

        def ps(name, shape, into):
            return into.enter_context(nc.psum_tensor(name, shape, F32))

        def dram(name, shape):
            return nc.dram_tensor(name, shape, F32, kind="Internal").ap()

        table = dram("table", (B * N, ROW))
        acc0 = dram("acc0", (B * N, D + 1))
        ytab = dram("ytab", (B * N, D))
        acc1 = dram("acc1", (B * N + P, D))

        x_sb = sb("x_sb", [P, T, D])
        ident = sb("ident", [P, P])
        ones = sb("ones", [P, P])
        w1_sb = sb("w1_sb", [P, RING, KD, F0])
        w2_sb = sb("w2_sb", [P, RING, FC, D])
        stats = sb("stats", [P, T, 6])
        mom = sb("mom", [P, 5, T])
        MEAN, VAR, RSTD, TMP, TMQ = range(5)
        gi = sb("gi", [P, 1], U32)
        si = sb("si", [P, 1], U32)
        held = sb("held", [P, 4])

        w_in = [sem(f"w_in{u}") for u in range(RING)]
        consts_done = sem("consts_done")
        x_in = sem("x_in")

        def load_expert(eng, w1t, w2t, e, u):
            eng.dma_start(w1_sb[:, u], w1t[e].rearrange("(k p) f -> p k f", p=P)).then_inc(w_in[u], 16)
            eng.dma_start(w2_sb[:, u], w2t[e].rearrange("(c p) d -> p c d", p=P)).then_inc(w_in[u], 16)

        def load_expert_at(eng, w1t, w2t, e, u):
            eng.dma_start(w1_sb[:, u], w1t[ds(e, 1)].rearrange("a (k p) f -> p (a k) f", p=P)).then_inc(w_in[u], 16)
            eng.dma_start(w2_sb[:, u], w2t[ds(e, 1)].rearrange("a (c p) d -> p (a c) d", p=P)).then_inc(w_in[u], 16)

        def held_here(pool, n):
            pool.tensor_tensor(held[:, n:n + 1], ones[:, 0:1], ones[:, 0:1], ALU.mult)

        def finish_moments(dve, link):
            ev, od = stats[:, :, 1], stats[:, :, 4]
            link(dve.tensor_tensor(mom[:, MEAN], ev, od, ALU.add))
            link(dve.tensor_tensor(mom[:, TMP], ev, od, ALU.subtract))
            link(dve.tensor_scalar(mom[:, MEAN], mom[:, MEAN], 0.5, None, ALU.mult))
            link(dve.tensor_scalar(mom[:, TMP], mom[:, TMP], 0.5, None, ALU.mult))
            link(dve.tensor_tensor(mom[:, TMP], mom[:, TMP], mom[:, TMP], ALU.mult))
            link(dve.tensor_tensor(mom[:, TMQ], stats[:, :, 2], stats[:, :, 5], ALU.add))
            link(dve.scalar_tensor_tensor(mom[:, VAR], mom[:, TMQ], 1.0 / D, mom[:, TMP], ALU.mult, ALU.add))

        mid = ctx.enter_context(ExitStack())
        idx = sb("idx", [P, E0 + 2], U32, into=mid)
        gtab = sb("gtab", [P, E0 + 1], into=mid)
        lg = sb("lg", [P, T, E0], into=mid)
        LT = sb("LT", [E0, B * N], into=mid)
        wq_in = sem("wq_in")

        att = ctx.enter_context(ExitStack())
        xnT = sb("xnT", [P, KD, B * N], into=att)
        kT = sb("kT", [P, B * N], into=att)
        v_sb = sb("v_sb", [P, T, DH], into=att)
        hide = sb("hide", [P, B * N], into=att)
        window = sb("window", [P, 2 * N - P], into=att)
        wq_sb = sb("wq_sb", [P, KD, H * DH], into=att)
        wo_sb = sb("wo_sb", [P, FC, D], into=att)
        wk2 = sb("wk2", [P, KD, 2, DH], into=att)
        wv = sb("wv", [P, KD, DH], into=att)
        gcol = sb("gcol", [P, KD], into=att)
        mask8 = sb("mask8", [P, B * N], U8, into=att)
        nkT = sb("nkT", [P, B], into=att)
        nv = sb("nv", [P, DH], into=att)
        nullb = sb("nullb", [P, H], into=att)
        blockseq = sb("blockseq", [1, B, QT], into=att)
        anylive = sb("anylive", [1, B, QT], into=att)
        startf = sb("startf", [1, B], into=att)
        start = sb("start", [1, B], I32, into=att)
        zrow = sb("zrow", [P, D + 1], into=att)
        go_b = sb("go_b", [P, D], into=att)
        nw_b = sb("nw_b", [P, D], into=att)
        rw_sb = sb("rw_sb", [P, KD, E0], into=att)
        rb_b = sb("rb_b", [P, E0], into=att)

        att_in, mask_in, moments, rooted, zeroed, acc0_zero, mask_step, pool_step = [
            sem(n) for n in ("att_in", "mask_in", "moments", "rooted", "zeroed", "acc0_zero", "mask_step", "pool_step")]
        ATT_LOADS = 13

        with nc.Block() as block:
            @block.sync
            def _(sp):
                sp.dma_start(mask8[:], mask.partition_broadcast(P)).then_inc(mask_in, 16)
                sp.dma_start(x_sb[:], x.rearrange("b (t p) d -> p (b t) d", p=P)).then_inc(x_in, 16)
                sp.dma_start(gcol[:], g_in).then_inc(att_in, 16)
                for half in range(2):
                    sp.dma_start(wk2[:, :, half], wkv[:, 0:DH].rearrange("(k p) n -> p k n", p=P)).then_inc(att_in, 16)
                    sp.dma_start(nkT[half * DH:(half + 1) * DH, :], condT).then_inc(att_in, 16)
                sp.dma_start(wv[:], wkv[:, DH:2 * DH].rearrange("(k p) n -> p k n", p=P)).then_inc(att_in, 16)
                sp.dma_start(nv[:], cond[1:2, :].partition_broadcast(P)).then_inc(att_in, 16)
                sp.dma_start(nullb[:], null_bias.partition_broadcast(P)).then_inc(att_in, 16)
                sp.dma_start(rw_sb[:], rw).then_inc(att_in, 16)
                sp.dma_start(rb_b[:], rb.partition_broadcast(P)).then_inc(att_in, 16)
                sp.dma_start(go_b[:], g_out.partition_broadcast(P)).then_inc(att_in, 16)
                sp.dma_start(nw_b[:], norm_w.partition_broadcast(P)).then_inc(att_in, 16)
                sp.dma_start(wo_sb[:], wo.rearrange("(c p) d -> p c d", p=P)).then_inc(att_in, 16)
                sp.dma_start(wq_sb[:], wq.rearrange("(k p) n -> p k n", p=P)).then_inc(wq_in, 16)
                sp.wait_ge(zeroed, 1)
                sp.dma_start(acc0.rearrange("(t p) d -> p t d", p=P), repeat(zrow[:], T)).then_inc(acc0_zero, 16)

            @block.gpsimd
            def _(pool):
                pool.iota(blockseq[:], pattern=[[0, B], [1, QT]], base=-QT, channel_multiplier=0,
                          allow_small_or_imprecise_dtypes=True).then_inc(consts_done, 1)
                pool.memset(zrow[:], 0.0).then_inc(zeroed, 1)
                pool.memset(ident[:], 0.0).then_inc(pool_step, 1)
                pool.wait_ge(pool_step, 1)
                pool.affine_select(out=ident[:], in_=ident[:], compare_op=ALU.not_equal, fill=1.0, base=0,
                                   pattern=[[-1, P]], channel_multiplier=1).then_inc(consts_done, 1)
                pool.memset(ones[:], 1.0).then_inc(consts_done, 1)
                pool.memset(window[:], 0.0).then_inc(pool_step, 1)
                pool.wait_ge(pool_step, 2)
                pool.affine_select(out=window[:], in_=window[:], compare_op=ALU.is_ge, fill=HIDE, base=N - P,
                                   pattern=[[-1, 2 * N - P]], channel_multiplier=1).then_inc(pool_step, 1)

            @block.vector
            def _(dve):
                dve.wait_ge(mask_in, 16)
                dve.tensor_reduce(anylive[:], mask8[0:1, :].rearrange("p (b t k) -> p b t k", b=B, k=P),
                                  AX, ALU.max).then_inc(mask_step, 1)
                dve.wait_ge(mask_step, 1)
                dve.wait_ge(consts_done, 1)
                dve.tensor_tensor(anylive[:], anylive[:], blockseq[:], ALU.mult).then_inc(mask_step, 1)
                dve.wait_ge(mask_step, 2)
                dve.tensor_reduce(startf[:], anylive[:], AX, ALU.min).then_inc(mask_step, 1)
                dve.wait_ge(mask_step, 3)
                dve.tensor_scalar(start[:], startf[:], float(QT), None, ALU.add).then_inc(mask_step, 1)
                dve.tensor_scalar(hide[:], mask8[:], 1.0, -HIDE, ALU.subtract, ALU.mult).then_inc(mask_step, 1)
                dve.wait_ge(mask_step, 5)

        def live_tiles(eng, name, on_tile, on_keys=None, after=None):
            nq, nk = eng.alloc_register(name + "_nq"), eng.alloc_register(name + "_nk")
            eng.reg_mov(nq, 0)
            eng.reg_mov(nk, 0)
            with eng.Fori(0, B) as b:
                first = eng.value_load(start[0:1, ds(b, 1)], min_val=0, max_val=QT)
                with eng.If(first < QT):
                    with eng.Fori(first, QT) as qt:
                        if on_tile:
                            on_tile(b, qt, eng.snap(nq))
                        if on_keys:
                            with eng.Fori(first, qt + 1) as kt:
                                on_keys(b, qt, kt, eng.snap(nq), eng.snap(nk))
                                eng.reg_add(nk, nk, 1)
                        if after:
                            after(b, qt, eng.snap(nq), eng.snap(nk))
                        eng.reg_add(nq, nq, 1)
            return nq

        with ExitStack() as ph:
            xrow = sb("xrow", [P, D], into=ph)
            xcol = sb("xcol", [P, KD, P], into=ph)
            pt = ps("a_pt", [P, 512], ph)
            pk = ps("a_pk", [P, 512], ph)
            pv = ps("a_pv", [P, 512], ph)
            xn_row, xn_t, xn_col, xn_kept, kv_done, kv_kept = [
                sem(n) for n in ("xn_row", "xn_t", "xn_col", "xn_kept", "kv_done", "kv_kept")]
            with nc.Block() as block:
                @block.sync
                def _(sp):
                    for s in (xn_t, xn_kept, kv_done, kv_kept):
                        sp.sem_inc(s, 1)
                    sp.wait_ge(acc0_zero, 16)
                    for u in range(RING):
                        load_expert(sp, w1, w2, u, u)

                @block.gpsimd
                def _(pool):
                    def tile(b, qt, n):
                        pool.wait_ge(xn_col, 2 * n + 2)
                        pool.tensor_tensor(held[:, 0:1], ones[:, 0:1], ones[:, 0:1], ALU.mult)
                        pool.tensor_copy(xnT[:, :, ds(b * N + qt * P, P)], xcol[:]).then_inc(xn_kept, 1)
                    live_tiles(pool, "pool_kv", tile)

                @block.vector
                def _(dve):
                    steps = [0]

                    def link(ins):
                        steps[0] += 1
                        ins.then_inc(moments, 1)
                        dve.wait_ge(moments, steps[0])

                    dve.wait_ge(x_in, 16)
                    with dve.Fori(0, T) as t:
                        dve.bn_stats(stats[:, ds(t, 1)].rearrange("p a s -> p (a s)"),
                                     x_sb[:, ds(t, 1)].rearrange("p a d -> p (a d)")).then_inc(moments, 1)
                    steps[0] = T
                    dve.wait_ge(moments, T)
                    finish_moments(dve, link)
                    link(dve.tensor_scalar(mom[:, TMP], mom[:, VAR], EPS, None, ALU.add))
                    dve.wait_ge(rooted, 1)
                    link(dve.reciprocal(mom[:, RSTD], mom[:, TMQ]))

                    def tile(b, qt, n):
                        t = b * QT + qt
                        dve.wait_ge(xn_t, done(n))
                        dve.tensor_scalar(xrow[:], x_sb[:, ds(t, 1)].rearrange("p a d -> p (a d)"),
                                          mom[:, MEAN, ds(t, 1)], mom[:, RSTD, ds(t, 1)],
                                          ALU.subtract, ALU.mult).then_inc(xn_row, 1)
                        dve.wait_ge(kv_done, done(n + 1))
                        dve.tensor_scalar(kT[:, ds(b * N + qt * P, P)], pk[:, 0:P], 1.0, None, ALU.mult).then_inc(kv_kept, 1)
                        dve.tensor_scalar(v_sb[:, ds(t, 1)].rearrange("p a d -> p (a d)"), pv[:, 0:DH],
                                          1.0, None, ALU.mult).then_inc(kv_kept, 1)
                    live_tiles(dve, "dve_kv", tile)

                @block.scalar
                def _(act):
                    act.wait_ge(moments, T + 8)
                    act.activation(mom[:, TMQ], mom[:, TMP], ACT.Sqrt).then_inc(rooted, 1)
                    act.wait_ge(att_in, 16 * ATT_LOADS)

                    def tile(b, qt, n):
                        act.wait_ge(xn_t, done(n + 1))
                        act.wait_ge(xn_kept, done(n))
                        act.wait_ge(kv_done, done(n))
                        for k in range(KD):
                            act.activation(xcol[:, k], pt[:, k * P:(k + 1) * P], ACT.Copy, scale=gcol[:, k:k + 1]).then_inc(xn_col, 1)
                    live_tiles(act, "act_kv", tile)

                @block.tensor
                def _(pe):
                    pe.wait_ge(consts_done, 3)
                    pe.wait_ge(att_in, 16 * ATT_LOADS)

                    def tile(b, qt, n):
                        pe.wait_ge(xn_row, n + 1)
                        for k in range(KD):
                            ins = pe.transpose(pt[:, k * P:(k + 1) * P], xrow[:, k * P:(k + 1) * P], ident[:])
                        ins.then_inc(xn_t, 1)
                        pe.wait_ge(xn_col, 2 * n + 2)
                        pe.wait_ge(kv_kept, done(2 * n))
                        for k in range(KD):
                            pe.matmul(pk[:, 0:P], wk2[:, k].rearrange("p a d -> p (a d)"), xcol[:, k],
                                      start=(k == 0), stop=(k == KD - 1))
                        for k in range(KD):
                            ins = pe.matmul(pv[:, 0:DH], xcol[:, k], wv[:, k], start=(k == 0), stop=(k == KD - 1))
                        ins.then_inc(kv_done, 1)
                    live_tiles(pe, "pe_kv", tile)

        with ExitStack() as ph:
            bias_sb = sb("bias_sb", [P, 2, H, P], into=ph)
            sc = sb("sc", [P, H, P], into=ph)
            PT = sb("PT", [P, 2, 4, P], into=ph)
            O = sb("O", [P, H, DH], into=ph)
            OT = sb("OT", [P, FC, P], into=ph)
            qT = sb("qT", [P, FC, P], into=ph)
            kblk = sb("kblk", [P, P], into=ph)
            vblk = sb("vblk", [P, DH], into=ph)
            comb = sb("comb", [P, P], into=ph)
            st = sb("st", [P, 8, H], into=ph)
            MAX, LEN, TMAX, NEG, DIF, ALPHA, RS, RL = range(8)
            yr = sb("yr", [P, D], into=ph)
            row = sb("row", [P, D], into=ph)
            col = sb("col", [P, KD, P], into=ph)
            st6 = sb("st6", [P, 6], into=ph)
            mv = sb("mv", [P, 8], into=ph)
            lgr = sb("lgr", [P, E0], into=ph)
            pS = ps("pS", [P, 4, 512], ph)
            pT = ps("pT", [P, 2, 512], ph)
            pO = ps("pO", [P, 2, 512], ph)
            (q_proj, q_ready, null_done, q_step, bias_in, staged, comb_ready, bias_ready, s_done, sc_ready, k_step, p_ready,
             alpha_ready, t_done, pt_ready, pv_done, k_done, o_ready, ot_done, ot_ready, o_proj, q_done, f_step, f_root,
             row_turned, col_ready, lg_done, lg_row, lt_done, lt_kept, row_out) = [sem("t_" + n) for n in (
                 "q_proj", "q_ready", "null_done", "q_step", "bias_in", "staged", "comb_ready", "bias_ready", "s_done",
                 "sc_ready", "k_step", "p_ready", "alpha_ready", "t_done", "pt_ready", "pv_done", "k_done", "o_ready",
                 "ot_done", "ot_ready", "o_proj", "q_done", "f_step", "f_root", "row_turned", "col_ready", "lg_done",
                 "lg_row", "lt_done", "lt_kept", "row_out")]
            QSTEP = 4
            KSTEP = 23
            FSTEP = 24

            def by_bank(tile, g):
                if len(tile.shape) == 2:
                    return tile.rearrange("p (a i r) -> p a r i", a=2, r=2)[:, g // 2, g % 2]
                return tile.rearrange("p (a i r) k -> p a r i k", a=2, r=2)[:, g // 2, g % 2]

            def heads(g):
                return [8 * (g // 2) + g % 2 + 2 * i for i in range(4)]

            with nc.Block() as block:
                @block.sync
                def _(sp):
                    for s in (bias_in, pv_done, bias_ready, row_out, k_step, k_done):
                        sp.sem_inc(s, 1)
                    sp.sem_inc(sc_ready, 5)

                    def keys(b, qt, kt, nq, nk):
                        sp.wait_ge(bias_in, done(nk * 16))
                        sp.wait_ge(sc_ready, done(nk * 4))
                        sp.dma_start(bias_sb[:, ds(nk % 2, 1)].rearrange("p a h k -> p (a h) k"),
                                     bias[:, ds(qt * P, P), ds(kt * P, P)].rearrange("h q k -> q h k")).then_inc(bias_in, 16)
                    live_tiles(sp, "sp_att", None, keys)

                @block.gpsimd
                def _(pool):
                    def keys(b, qt, kt, nq, nk):
                        pool.wait_ge(pv_done, done(nk * 4))
                        pool.wait_ge(bias_ready, done(nk * 4))
                        pool.tensor_tensor(comb[:], window[:, ds((kt - qt + QT - 1) * P, P)],
                                           hide[:, ds(b * N + kt * P, P)], ALU.add).then_inc(comb_ready, 1)
                        pool.tensor_copy(kblk[:], kT[:, ds(b * N + kt * P, P)]).then_inc(staged, 1)
                        pool.tensor_copy(vblk[:], v_sb[:, ds(b * QT + kt, 1)].rearrange("p a d -> p (a d)")).then_inc(staged, 1)
                        pool.wait_ge(comb_ready, nk + 1)
                        pool.wait_ge(bias_in, done(nk * 16 + 16))
                        for g in range(4):
                            part = by_bank(bias_sb[:, ds(nk % 2, 1)].rearrange("p a h k -> p (a h) k"), g)
                            pool.tensor_tensor(part, part, repeat(comb[:], 4), ALU.add).then_inc(bias_ready, 1)
                    live_tiles(pool, "pool_att", None, keys)

                @block.tensor
                def _(pe):
                    def finish(n):
                        pe.wait_ge(o_ready, n + 1)
                        for c in range(FC):
                            ins = pe.transpose(pT[:, c // 4, (c % 4) * P:(c % 4 + 1) * P],
                                               O[:, 2 * c:2 * c + 2].rearrange("p h d -> p (h d)"), ident[:])
                        ins.then_inc(ot_done, 1)
                        pe.wait_ge(ot_ready, n + 1)
                        for c in range(FC):
                            ins = pe.matmul(pO[:, 0, 0:D], OT[:, c], wo_sb[:, c], start=(c == 0), stop=(c == FC - 1))
                        ins.then_inc(o_proj, 1)
                        pe.wait_ge(f_step, n * FSTEP + FSTEP)
                        for k in range(KD):
                            ins = pe.transpose(pT[:, 0, k * P:(k + 1) * P], row[:, k * P:(k + 1) * P], ident[:])
                        ins.then_inc(row_turned, 1)
                        pe.wait_ge(col_ready, n + 1)
                        for k in range(KD):
                            ins = pe.matmul(pT[:, 1, 0:E0], col[:, k], rw_sb[:, k], start=(k == 0), stop=(k == KD - 1))
                        ins.then_inc(lg_done, 1)
                        pe.wait_ge(lg_row, n + 1)
                        pe.transpose(pT[0:E0, 0, 0:P], lgr[:], ident[:]).then_inc(lt_done, 1)

                    finish(0)
                    pe.wait_ge(wq_in, 16)

                    def queries(b, qt, nq):
                        pe.wait_ge(q_done, nq + 1)
                        for c in range(FC):
                            for k in range(KD):
                                ins = pe.matmul(pT[:, c // 4, (c % 4) * P:(c % 4 + 1) * P], wq_sb[:, k, c * P:(c + 1) * P],
                                                xnT[:, k, ds(b * N + qt * P, P)], start=(k == 0), stop=(k == KD - 1))
                        ins.then_inc(q_proj, 1)
                        pe.wait_ge(q_ready, nq * 2 + 2)
                        for h in range(H):
                            at = (h % 2) * DH
                            ins = pe.matmul(pO[:, h % 2, h // 2:h // 2 + 1], qT[at:at + DH, h // 2], nkT[at:at + DH, 0:1],
                                            start=True, stop=True)
                        ins.then_inc(null_done, 1)

                    def keys(b, qt, kt, nq, nk):
                        pe.wait_ge(staged, nk * 2 + 2)
                        for h in range(H):
                            at = (h % 2) * DH
                            ins = pe.matmul(pS[:, 2 * (h // 8) + h % 2, (h % 8 // 2) * P:(h % 8 // 2 + 1) * P],
                                            qT[at:at + DH, h // 2], kblk[at:at + DH, :], start=True, stop=True)
                            if h % 8 >= 6:
                                ins.then_inc(s_done, 1)

                        def turn(g):
                            pe.wait_ge(p_ready, nk * 16 + 4 * g + 4)
                            if g >= 2:
                                pe.wait_ge(pt_ready, nk * 4 + g - 1)
                            for i, h in enumerate(heads(g)):
                                ins = pe.transpose(pT[:, g % 2, i * P:(i + 1) * P], sc[:, h], ident[:])
                            ins.then_inc(t_done, 1)

                        def weigh(g):
                            pe.wait_ge(pt_ready, nk * 4 + g + 1)
                            for i, h in enumerate(heads(g)):
                                ins = pe.matmul(pO[:, h // 8, (h % 8) * DH:(h % 8 + 1) * DH], PT[:, g % 2, i], vblk[:],
                                                start=True, stop=True)
                            ins.then_inc(pv_done, 1)

                        turn(0)
                        for g in range(1, 4):
                            turn(g)
                            weigh(g - 1)
                        weigh(3)

                    live_tiles(pe, "pe_att", queries, keys, lambda b, qt, nq, nk: finish(nq + 1))

                @block.scalar
                def _(act):
                    def finish(n, rows):
                        for m, at in enumerate((9, 22)):
                            act.wait_ge(f_step, n * FSTEP + at)
                            act.activation(mv[:, 6:7], mv[:, 5:6], ACT.Sqrt).then_inc(f_root, 1)
                        act.wait_ge(row_turned, n + 1)
                        act.activation(col[:].rearrange("p k t -> p (k t)"), pT[:, 0, 0:D], ACT.Copy).then_inc(col_ready, 1)
                        act.wait_ge(f_step, n * FSTEP + FSTEP)
                        act.dma_start(*rows()).then_inc(row_out, 16)

                    finish(0, lambda: (table[:, 0:D].rearrange("(t p) d -> p t d", p=P), repeat(row[:], T)))
                    act.wait_ge(row_out, done(16))

                    def queries(b, qt, nq):
                        act.wait_ge(q_proj, nq + 1)
                        for g in range(2):
                            act.activation(qT[:, 4 * g:4 * g + 4].rearrange("p c q -> p (c q)"), pT[:, g], ACT.Copy,
                                           scale=DH ** -0.5).then_inc(q_ready, 1)

                    def keys(b, qt, kt, nq, nk):
                        def exps(g):
                            act.wait_ge(k_step, done(nk * KSTEP + 5 * g + 4))
                            for h in heads(g):
                                act.activation(sc[:, h], sc[:, h], ACT.Exp, bias=st[:, NEG, h:h + 1],
                                               accum_out=st[:, RS, h:h + 1]).then_inc(p_ready, 1)

                        def keep(g):
                            act.wait_ge(t_done, nk * 4 + g + 1)
                            if g >= 2:
                                act.wait_ge(pv_done, done(nk * 4 + g - 1))
                            act.activation(PT[:, g % 2].rearrange("p h q -> p (h q)"), pT[:, g % 2], ACT.Copy).then_inc(pt_ready, 1)

                        exps(0)
                        for g in range(1, 4):
                            exps(g)
                            keep(g - 1)
                        act.activation(st[:, ALPHA], st[:, DIF], ACT.Exp).then_inc(alpha_ready, 1)
                        keep(3)

                    tiles = live_tiles(act, "act_att", queries, keys, lambda b, qt, nq, nk: finish(
                        nq + 1, lambda: (table[ds((b * QT + qt) * P, P), 0:D], row[:])))
                    act.wait_ge(row_out, done(16 * (act.snap(tiles) + 1)))
                    act.activation(held[:, 0:1], ones[:, 0:1], ACT.Copy)

                @block.vector
                def _(dve):
                    def moments_of(at, rows):
                        dve.bn_stats(st6[:], rows).then_inc(f_step, 1)
                        dve.wait_ge(f_step, at + 1)
                        dve.tensor_tensor(mv[:, 1:2], st6[:, 1:2], st6[:, 4:5], ALU.add).then_inc(f_step, 1)
                        dve.tensor_tensor(mv[:, 2:3], st6[:, 1:2], st6[:, 4:5], ALU.subtract).then_inc(f_step, 1)
                        dve.tensor_tensor(mv[:, 4:5], st6[:, 2:3], st6[:, 5:6], ALU.add).then_inc(f_step, 1)
                        dve.wait_ge(f_step, at + 4)
                        dve.tensor_scalar(mv[:, 0:1], mv[:, 1:2], 0.5, None, ALU.mult).then_inc(f_step, 1)
                        dve.tensor_tensor(mv[:, 3:4], mv[:, 2:3], mv[:, 2:3], ALU.mult).then_inc(f_step, 1)
                        dve.tensor_scalar(mv[:, 5:6], mv[:, 4:5], 1.0 / D, EPS, ALU.mult, ALU.add).then_inc(f_step, 1)
                        dve.wait_ge(f_step, at + 7)

                    def finish(n, keep):
                        at = n * FSTEP
                        dve.wait_ge(ot_done, n + 1)
                        dve.tensor_copy(OT[:].rearrange("p c q -> p (c q)"), pT[:].rearrange("p b n -> p (b n)")).then_inc(ot_ready, 1)
                        dve.wait_ge(o_proj, n + 1)
                        dve.tensor_copy(yr[:], pO[:, 0, 0:D]).then_inc(f_step, 1)
                        dve.wait_ge(f_step, at + 1)
                        moments_of(at + 1, yr[:])
                        dve.scalar_tensor_tensor(mv[:, 5:6], mv[:, 3:4], 0.25, mv[:, 5:6], ALU.mult, ALU.add).then_inc(f_step, 1)
                        dve.wait_ge(f_root, n * 2 + 1)
                        dve.reciprocal(mv[:, 7:8], mv[:, 6:7]).then_inc(f_step, 1)
                        dve.wait_ge(f_step, at + 10)
                        dve.tensor_scalar(yr[:], yr[:], mv[:, 0:1], mv[:, 7:8], ALU.subtract, ALU.mult).then_inc(f_step, 1)
                        dve.wait_ge(f_step, at + 11)
                        dve.tensor_tensor(yr[:], yr[:], go_b[:], ALU.mult).then_inc(f_step, 1)
                        dve.wait_ge(f_step, at + 12)
                        moments_of(at + 12, yr[:])
                        dve.tensor_tensor(mv[:, 4:5], mv[:, 0:1], mv[:, 0:1], ALU.mult).then_inc(f_step, 1)
                        dve.scalar_tensor_tensor(mv[:, 5:6], mv[:, 3:4], 0.25, mv[:, 5:6], ALU.mult, ALU.add).then_inc(f_step, 1)
                        dve.wait_ge(f_step, at + 21)
                        dve.tensor_tensor(mv[:, 5:6], mv[:, 5:6], mv[:, 4:5], ALU.add).then_inc(f_step, 1)
                        dve.wait_ge(f_root, n * 2 + 2)
                        dve.reciprocal(mv[:, 7:8], mv[:, 6:7]).then_inc(f_step, 1)
                        dve.wait_ge(f_step, at + 23)
                        dve.wait_ge(row_out, done(n * 16))
                        dve.scalar_tensor_tensor(row[:], yr[:], mv[:, 7:8], nw_b[:], ALU.mult, ALU.mult).then_inc(f_step, 1)
                        dve.wait_ge(lg_done, n + 1)
                        dve.tensor_tensor(lgr[:], pT[:, 1, 0:E0], rb_b[:], ALU.add).then_inc(lg_row, 1)
                        dve.wait_ge(lg_row, n + 1)
                        dve.wait_ge(lt_done, n + 1)
                        keep()

                    dve.wait_ge(att_in, 16 * ATT_LOADS)
                    dve.tensor_copy(O[:], repeat(nv[:], H)).then_inc(o_ready, 1)

                    def keep_dead():
                        dve.tensor_copy(lg[:], repeat(lgr[:], T)).then_inc(lt_kept, 1)
                        dve.tensor_copy(LT[:].rearrange("e (t p) -> e t p", p=P), repeat(pT[0:E0, 0, 0:P], T)).then_inc(q_done, 1)
                        dve.wait_ge(lt_kept, 1)
                        dve.wait_ge(q_done, 1)
                    finish(0, keep_dead)

                    def queries(b, qt, nq):
                        dve.wait_ge(null_done, nq + 1)
                        dve.tensor_tensor(st[:, MAX].rearrange("p (c r) -> p r c", r=2), pO[:, :, 0:H // 2],
                                          nullb[:].rearrange("p (c r) -> p r c", r=2), ALU.add).then_inc(q_step, 1)
                        dve.memset(st[:, LEN], 1.0).then_inc(q_step, 1)
                        dve.tensor_copy(O[:], repeat(nv[:], H)).then_inc(q_step, 1)

                    def keys(b, qt, kt, nq, nk):
                        at = nk * KSTEP
                        dve.wait_ge(q_step, nq * QSTEP + 3)
                        dve.wait_ge(k_done, done(nk * 2))
                        dve.wait_ge(k_step, done(at))
                        for g in range(4):
                            mine = [by_bank(st[:, n], g) for n in range(8)]
                            dve.wait_ge(bias_ready, done(nk * 4 + g + 1))
                            dve.wait_ge(s_done, nk * 4 + g + 1)
                            dve.tensor_tensor(by_bank(sc[:], g), pS[:, g].rearrange("p (i k) -> p i k", k=P),
                                              by_bank(bias_sb[:, ds(nk % 2, 1)].rearrange("p a h k -> p (a h) k"), g),
                                              ALU.add).then_inc(sc_ready, 1)
                            dve.wait_ge(sc_ready, done(nk * 4 + g + 5))
                            dve.tensor_reduce(mine[TMAX], by_bank(sc[:], g), AX, ALU.max).then_inc(k_step, 1)
                            dve.wait_ge(k_step, done(at + 5 * g + 1))
                            dve.tensor_tensor(mine[TMAX], mine[TMAX], mine[MAX], ALU.max).then_inc(k_step, 1)
                            dve.wait_ge(k_step, done(at + 5 * g + 2))
                            dve.tensor_tensor(mine[DIF], mine[MAX], mine[TMAX], ALU.subtract).then_inc(k_step, 1)
                            dve.tensor_scalar(mine[NEG], mine[TMAX], -1.0, None, ALU.mult).then_inc(k_step, 1)
                            dve.wait_ge(k_step, done(at + 5 * g + 4))
                            dve.tensor_copy(mine[MAX], mine[TMAX]).then_inc(k_step, 1)
                        dve.wait_ge(alpha_ready, nk + 1)
                        dve.tensor_tensor(O[:], O[:], bcast(st[:, ALPHA], DH), ALU.mult).then_inc(k_step, 1)
                        dve.tensor_tensor(st[:, LEN], st[:, LEN], st[:, ALPHA], ALU.mult).then_inc(k_step, 1)
                        dve.wait_ge(k_step, done(at + 22))
                        dve.tensor_tensor(st[:, LEN], st[:, LEN], st[:, RS], ALU.add).then_inc(k_step, 1)
                        for half in range(2):
                            dve.wait_ge(pv_done, done(nk * 4 + 2 * half + 2))
                            mine = O[:, 8 * half:8 * half + 8].rearrange("p h d -> p (h d)")
                            dve.tensor_tensor(mine, mine, pO[:, half], ALU.add).then_inc(k_done, 1)

                    def after(b, qt, nq, nk):
                        dve.wait_ge(k_done, done(nk * 2))
                        dve.wait_ge(k_step, done(nk * KSTEP))
                        dve.reciprocal(st[:, RL], st[:, LEN]).then_inc(q_step, 1)
                        dve.wait_ge(q_step, nq * QSTEP + 4)
                        dve.tensor_tensor(O[:], O[:], bcast(st[:, RL], DH), ALU.mult).then_inc(o_ready, 1)

                        def keep():
                            dve.tensor_scalar(lg[:, ds(b * QT + qt, 1)].rearrange("p a e -> p (a e)"), lgr[:], 1.0, None,
                                              ALU.mult).then_inc(lt_kept, 1)
                            dve.tensor_scalar(LT[:, ds((b * QT + qt) * P, P)], pT[0:E0, 0, 0:P], 1.0, None,
                                              ALU.mult).then_inc(q_done, 1)
                        finish(nq + 1, keep)

                    live_tiles(dve, "dve_att", queries, keys, after)
        if upto == "att":
            return

        att.close()

        with ExitStack() as picked:
            b1_sb = sb("b1_sb", [P, E0, FC], into=picked)
            b2_sb = sb("b2_sb", [P, E0, D], into=picked)
            with ExitStack() as ph:
                top = sb("top", [P, 2, T], into=ph)
                chunk = sb("chunk", [P, CW], into=ph)
                best = sb("best", [P, CAP], into=ph)
                pick = sb("pick", [P, CAP], U32, into=ph)
                pickf = sb("pickf", [P, CAP], into=ph)
                lists = sb("lists", [E0, CPE, CAP], into=ph)
                merge = sb("merge", [E0, 2, CPE // 2, CAP], into=ph)
                least = sb("least", [E0, 1], into=ph)
                lowest = sb("lowest", [P, 1], into=ph)
                test = sb("test", [P, 2, CAP], into=ph)
                num = sb("num", [P, 8], into=ph)
                GREATER, EQUAL, LEFT, TAKEN, FIRST, BASE = range(6)
                place = sb("place", [P, 3, CAP], into=ph)
                hot = sb("hot", [P, E0, CAP], into=ph)
                pickT = sb("pickT", [P, P], into=ph)
                mineT = sb("mineT", [P, P], into=ph)
                same = sb("same", [P, P], into=ph)
                earlier = sb("earlier", [P, P], into=ph)
                spread = sb("spread", [E0, P], into=ph)
                slots = sb("slots", [P, CAP], into=ph)
                rank = sb("rank", [P, 1], into=ph)
                pr = ps("c_pr", [P, 4, 512], ph)
                pv = ps("c_pv", [P, 512], ph)
                pn = ps("c_pn", [P, 512], ph)
                soft, soft_exp, gates_out, step, e_in, chunk_in, lists_in, pe_step, c_step = [
                    sem(n) for n in ("soft", "soft_exp", "gates_out", "pick_step", "e_in", "chunk_in", "lists_in",
                                     "pe_step", "c_step")]
                SORTED = 3 * CAP // 8
                table_steps = []
                with nc.Block() as block:
                    @block.sync
                    def _(sp):
                        sp.dma_start(chunk[:], LT[:].rearrange("e (c k) -> e c k", c=CPE)).then_inc(chunk_in, 16)
                        sp.dma_start(b1_sb[:], b1).then_inc(e_in, 16)
                        sp.dma_start(b2_sb[:].rearrange("p e d -> p (e d)"), b2.partition_broadcast(P)).then_inc(e_in, 16)
                        sp.wait_ge(soft, 5)
                        sp.dma_start(table[:, D:ROW].rearrange("(t p) e -> p t e", p=P), lg[:]).then_inc(gates_out, 16)
                        sp.wait_ge(step, SORTED)
                        sp.dma_start(lists[:], best[:]).then_inc(lists_in, 16)
                        sp.wait_ge(lists_in, 16)
                        sp.wait_ge(gates_out, 16)
                        sp.wait_ge(e_in, 32)

                    @block.gpsimd
                    def _(pool):
                        pool.memset(spread[:], 0.0).then_inc(c_step, 1)
                        pool.affine_select(out=same[:].rearrange("p (e c) -> p e c", c=CPE), in_=ones[:].rearrange("p (e c) -> p e c", c=CPE),
                                           compare_op=ALU.is_ge, fill=0.0, base=0, pattern=[[-CPE, E0], [0, CPE]],
                                           channel_multiplier=1).then_inc(c_step, 1)
                        pool.wait_ge(c_step, 2)
                        pool.affine_select(out=same[:].rearrange("p (e c) -> p e c", c=CPE), in_=same[:].rearrange("p (e c) -> p e c", c=CPE),
                                           compare_op=ALU.is_ge, fill=0.0, base=CPE - 1, pattern=[[CPE, E0], [0, CPE]],
                                           channel_multiplier=-1).then_inc(c_step, 1)
                        pool.affine_select(out=spread[:].rearrange("p (e c) -> p e c", c=CPE), in_=spread[:].rearrange("p (e c) -> p e c", c=CPE),
                                           compare_op=ALU.not_equal, fill=1.0, base=0, pattern=[[-1, E0], [0, CPE]],
                                           channel_multiplier=1).then_inc(c_step, 1)
                        pool.wait_ge(c_step, 3)
                        pool.affine_select(out=earlier[:], in_=same[:], compare_op=ALU.is_ge, fill=0.0, base=-1,
                                           pattern=[[1, P]], channel_multiplier=-1).then_inc(c_step, 1)
                        pool.iota(slots[:], pattern=[[1, CAP]], base=0, channel_multiplier=0,
                                  allow_small_or_imprecise_dtypes=True).then_inc(c_step, 1)
                        pool.iota(rank[:], pattern=[[0, 1]], base=0, channel_multiplier=1,
                                  allow_small_or_imprecise_dtypes=True).then_inc(c_step, 1)

                    @block.vector
                    def _(dve):
                        dve.tensor_reduce(top[:, 0], lg[:], AX, ALU.max).then_inc(soft, 1)
                        dve.wait_ge(soft, 1)
                        dve.tensor_tensor(lg[:], lg[:], bcast(top[:, 0], E0), ALU.subtract).then_inc(soft, 1)
                        dve.wait_ge(soft_exp, 1)
                        dve.tensor_reduce(top[:, 0], lg[:], AX, ALU.add).then_inc(soft, 1)
                        dve.wait_ge(soft, 3)
                        dve.reciprocal(top[:, 1], top[:, 0]).then_inc(soft, 1)
                        dve.wait_ge(soft, 4)
                        dve.tensor_tensor(lg[:], lg[:], bcast(top[:, 1], E0), ALU.mult).then_inc(soft, 1)
                        steps = [0]

                        def put(ins):
                            steps[0] += 1
                            ins.then_inc(step, 1)

                        def link(ins):
                            put(ins)
                            dve.wait_ge(step, steps[0])

                        dve.wait_ge(chunk_in, 16)
                        for r in range(CAP // 8):
                            now = slice(8 * r, 8 * r + 8)
                            link(dve.max(best[:, now], chunk[:]))
                            link(dve.max_index(pick[:, now], best[:, now], chunk[:]))
                            link(dve.match_replace(chunk[:], best[:, now], chunk[:], -3e38))
                        dve.wait_ge(lists_in, 16)
                        left, many = lists[:], CPE
                        while many > 1:
                            many //= 2
                            pairs = left.rearrange("e (j r) k -> e j r k", r=2)
                            out_at = merge[:, 0, 0:many]
                            link(dve.tensor_tensor(out_at, pairs[:, :, 0], pairs[:, :, 1, ::-1], ALU.max))
                            side, w = 0, CAP // 2
                            while w and many > 1:
                                view = [merge[:, n, 0:many].rearrange("e j (b r w) -> e (j b) r w", r=2, w=w) for n in (side, 1 - side)]
                                put(dve.tensor_tensor(view[1][:, :, 0], view[0][:, :, 0], view[0][:, :, 1], ALU.max))
                                link(dve.tensor_tensor(view[1][:, :, 1], view[0][:, :, 0], view[0][:, :, 1], ALU.min))
                                side, w = 1 - side, w // 2
                            left = merge[:, side, 0:many]
                        link(dve.tensor_reduce(least[:], merge[:, 0, 0], AX, ALU.min))
                        table_steps.append(steps[0])
                        put(dve.tensor_copy(pickf[:], pick[:]))
                        dve.wait_ge(pe_step, 1)
                        link(dve.tensor_copy(lowest[:], pn[:, 0:1]))
                        link(dve.tensor_scalar(num[:, BASE:BASE + 1], pn[:, 1:2], float(CW), None, ALU.mult))
                        put(dve.tensor_scalar(test[:, 0], best[:], lowest[:, 0:1], None, ALU.is_gt))
                        link(dve.tensor_scalar(test[:, 1], best[:], lowest[:, 0:1], None, ALU.is_equal))
                        link(dve.tensor_reduce(num[:, GREATER:EQUAL + 1], test[:], AX, ALU.add))
                        table_steps.append(steps[0])
                        link(dve.tensor_scalar(pickf[:], pickf[:], num[:, BASE:BASE + 1], None, ALU.add))
                        table_steps.append(steps[0])
                        dve.wait_ge(pe_step, 2)
                        link(dve.tensor_scalar(num[:, LEFT:LEFT + 1], pn[:, 2:3], -1.0, float(CAP), ALU.mult, ALU.add))
                        link(dve.tensor_tensor(num[:, LEFT:LEFT + 1], num[:, LEFT:LEFT + 1], pn[:, 3:4], ALU.subtract))
                        link(dve.tensor_scalar(num[:, LEFT:LEFT + 1], num[:, LEFT:LEFT + 1], 0.0, None, ALU.max))
                        link(dve.tensor_tensor(num[:, LEFT:LEFT + 1], num[:, LEFT:LEFT + 1], num[:, EQUAL:EQUAL + 1], ALU.min))
                        link(dve.tensor_tensor(num[:, TAKEN:TAKEN + 1], num[:, LEFT:LEFT + 1], num[:, GREATER:GREATER + 1], ALU.add))
                        table_steps.append(steps[0])
                        dve.wait_ge(c_step, 7)
                        dve.wait_ge(pe_step, 3)
                        link(dve.tensor_copy(num[:, FIRST:FIRST + 1], pn[:, 4:5]))
                        link(dve.tensor_scalar(place[:, 0], slots[:], num[:, FIRST:FIRST + 1], None, ALU.subtract))
                        link(dve.tensor_scalar(place[:, 1], place[:, 0], num[:, TAKEN:TAKEN + 1], None, ALU.is_lt))
                        link(dve.scalar_tensor_tensor(place[:, 1], place[:, 0], 0.0, place[:, 1], ALU.is_ge, ALU.mult))
                        link(dve.tensor_tensor(place[:, 2], place[:, 0], place[:, 1], ALU.mult))
                        table_steps.append(steps[0])
                        dve.wait_ge(pe_step, 4)
                        put(dve.tensor_copy(pickT[:], pv[:, P:2 * P]))
                        link(dve.tensor_copy(mineT[:], pv[:, 2 * P:3 * P]))
                        for q in range(4):
                            dve.wait_ge(pe_step, 5 + q)
                            link(dve.tensor_scalar(hot[:, 4 * q:4 * q + 4].rearrange("p e s -> p (e s)"), pr[:, q], rank[:, 0:1],
                                                   None, ALU.is_equal))
                        table_steps.append(steps[0])
                        dve.wait_ge(pe_step, 9)
                        put(dve.memset(idx[:], 0))
                        link(dve.tensor_tensor(mineT[:], mineT[:], pv[:, 0:P], ALU.mult))
                        link(dve.tensor_reduce(top[:, 0], mineT[:].rearrange("p (e c) -> p e c", c=CPE), AX, ALU.add))
                        link(dve.tensor_copy(idx[:, 0:E0], top[:, 0]))

                    @block.scalar
                    def _(act):
                        act.wait_ge(soft, 2)
                        act.activation(lg[:], lg[:], ACT.Exp).then_inc(soft_exp, 1)

                    @block.tensor
                    def _(pe):
                        least_set, counted_at, pickf_set, taken_at, placed, hot_set = table_steps
                        pe.wait_ge(c_step, 7)
                        pe.matmul(pn[:, 1:2], earlier[:], ones[:, 0:1], start=True, stop=True)
                        pe.wait_ge(step, least_set)
                        pe.matmul(pn[:, 0:1], spread[:], least[:], start=True, stop=True).then_inc(pe_step, 1)
                        pe.wait_ge(step, counted_at)
                        pe.matmul(pn[:, 2:3], same[:], num[:, GREATER:GREATER + 1], start=True, stop=True)
                        pe.matmul(pn[:, 3:4], earlier[:], num[:, EQUAL:EQUAL + 1], start=True, stop=True).then_inc(pe_step, 1)
                        pe.wait_ge(step, taken_at)
                        pe.matmul(pn[:, 4:5], earlier[:], num[:, TAKEN:TAKEN + 1], start=True, stop=True).then_inc(pe_step, 1)
                        pe.transpose(pv[:, P:2 * P], pickf[:], ident[:])
                        pe.wait_ge(step, placed)
                        pe.transpose(pv[:, 2 * P:3 * P], place[:, 1], ident[:]).then_inc(pe_step, 1)
                        for e in range(E0):
                            ins = pe.matmul(pr[:, e // 4, (e % 4) * P:(e % 4 + 1) * P], same[:, CPE * e:CPE * e + 1].to_broadcast([P, P]),
                                            place[:, 2], start=True, stop=True)
                            if e % 4 == 3:
                                ins.then_inc(pe_step, 1)
                        pe.wait_ge(step, hot_set)
                        for e in range(E0):
                            ins = pe.matmul(pv[:, CPE * e:CPE * e + CPE], hot[:, e], pickT[:, CPE * e:CPE * e + CPE],
                                            start=True, stop=True)
                        ins.then_inc(pe_step, 1)
            if upto == "route0":
                return

            def expert_phase(tag, src, width, dst, out_width, gidx, sidx, gates, from_row, b1t, b2t, w1t, w2t,
                             experts, act_fn, counts, preload):
                with ExitStack() as ph:
                    G = sb(tag + "G", [P, width + 1], into=ph)
                    XT = sb(tag + "XT", [P, KD, P], into=ph)
                    hT = sb(tag + "hT", [P, FC, P], into=ph)
                    yt = sb(tag + "yt", [P, D], into=ph)
                    yg = sb(tag + "yg", [P, out_width], into=ph)
                    pX = ps(tag + "pX", [P, 512], ph)
                    pH = ps(tag + "pH", [P, 2, 512], ph)
                    pY = ps(tag + "pY", [P, 512], ph)
                    names = ("gathered", "turned", "xt_ready", "fc1_done", "gelu_done", "fc2_done", "y_read", "yg_ready",
                             "scattered", "gi_set", "si_set", "spare_set")
                    (gathered, turned, xt_ready, fc1_done, gelu_done, fc2_done, y_read, yg_ready, scattered, gi_set,
                     si_set, spare_set) = [sem(f"{tag}_{n}") for n in names]

                    def per_block(eng, name, body, begin=None):
                        if counts is None:
                            with eng.Fori(0, experts // RING) as r:
                                for u in range(RING):
                                    if begin:
                                        begin(r, RING * r + u, u)
                                    body(RING * r + u, RING * r + u, u)
                            return
                        nblk, _ = counts
                        reg = eng.alloc_register(f"{tag}_{name}")
                        eng.reg_mov(reg, 0)
                        with eng.Fori(0, experts // RING) as r:
                            for u in range(RING):
                                e = RING * r + u
                                if begin:
                                    begin(r, e, u)
                                n = eng.value_load(nblk[0:1, ds(e, 1)], min_val=0, max_val=B * N // P)
                                with eng.If(n > 0):
                                    with eng.Fori(0, n):
                                        body(eng.snap(reg), e, u)
                                        eng.reg_add(reg, reg, 1)

                    with nc.Block() as block:
                        @block.sync
                        def _(sp):
                            if preload:
                                for u in range(RING):
                                    load_expert(sp, w1t, w2t, u, u)
                            with sp.Fori(0, experts // RING - 1) as r:
                                for u in range(RING):
                                    if counts is None:
                                        sp.wait_ge(fc2_done, RING * r + u + 1)
                                    else:
                                        end = sp.value_load(counts[1][0:1, ds(RING * r + u, 1)], min_val=0, max_val=BLK)
                                        sp.wait_ge(fc2_done, end)
                                    load_expert_at(sp, w1t, w2t, RING * r + u + RING, u)

                        @block.gpsimd
                        def _(pool):
                            def gather(j, done):
                                pool.tensor_copy(gi[:], gidx[:, ds(j, 1)] if not isinstance(j, int) else gidx[:, j:j + 1]).then_inc(gi_set, 1)
                                pool.wait_ge(gi_set, j + 1)
                                held_here(pool, 0)
                                pool.indirect_dma_start(G[:, 0:width], None, src, bass.IndirectOffsetOnAxis(ap=gi[:], axis=0)).then_inc(gathered, 16)

                            gather(0, 0)
                            pool.wait_ge(turned, 1)
                            pool.wait_ge(xt_ready, 1)
                            pool.wait_ge(gathered, 16)
                            gather(1, 1)

                            def body(j, e, u):
                                pool.wait_ge(turned, j + 2)
                                pool.wait_ge(xt_ready, j + 2)
                                pool.wait_ge(gathered, j * 16 + 32)
                                held_here(pool, 1)
                                gather(j + 2, 2)
                                pool.wait_ge(scattered, j * 16)
                                held_here(pool, 2)
                                pool.tensor_copy(si[:], sidx[:, ds(j, 1)]).then_inc(si_set, 1)
                                pool.wait_ge(yg_ready, j + 1)
                                pool.wait_ge(si_set, j + 1)
                                held_here(pool, 3)
                                pool.indirect_dma_start(dst, bass.IndirectOffsetOnAxis(ap=si[:], axis=0), yg[:], None,
                                                        compute_op=ALU.add).then_inc(scattered, 16)
                            per_block(pool, "pool", body)

                        @block.tensor
                        def _(pe):
                            def turn(j):
                                pe.wait_ge(gathered, j * 16 + 16)
                                for k in range(KD):
                                    ins = pe.transpose(pX[:, k * P:(k + 1) * P], G[:, k * P:(k + 1) * P], ident[:])
                                ins.then_inc(turned, 1)

                            turn(0)

                            def begin(r, e, u):
                                pe.wait_ge(w_in[u], r * 32 + (w_round[0] + 1) * 32)

                            def body(j, e, u):
                                pe.wait_ge(xt_ready, j + 1)
                                for c in range(FC):
                                    for k in range(KD):
                                        ins = pe.matmul(pH[:, c // 4, (c % 4) * P:(c % 4 + 1) * P], w1_sb[:, u, k, c * P:(c + 1) * P],
                                                        XT[:, k], start=(k == 0), stop=(k == KD - 1))
                                    if c % 4 == 3:
                                        ins.then_inc(fc1_done, 1)
                                turn(j + 1)
                                pe.wait_ge(y_read, j)
                                for c in range(FC):
                                    pe.wait_ge(gelu_done, j * FC + c + 1)
                                    ins = pe.matmul(pY[:, 0:D], hT[:, c], w2_sb[:, u, c], start=(c == 0), stop=(c == FC - 1))
                                ins.then_inc(fc2_done, 1)
                            per_block(pe, "pe", body, begin)

                        @block.scalar
                        def _(act):
                            def body(j, e, u):
                                act.wait_ge(fc2_done, j)
                                for c in range(FC):
                                    if c % 4 == 0:
                                        act.wait_ge(fc1_done, j * 2 + c // 4 + 1)
                                    act.activation(hT[:, c], pH[:, c // 4, (c % 4) * P:(c % 4 + 1) * P], act_fn,
                                                   bias=b1t[:, ds(e, 1), c]).then_inc(gelu_done, 1)
                            per_block(act, "act", body)

                        @block.vector
                        def _(dve):
                            def column(j):
                                dve.wait_ge(turned, j + 1)
                                if from_row:
                                    dve.tensor_scalar(gates[:, ds(j, 1)] if not isinstance(j, int) else gates[:, 0:1],
                                                      G[:, ds(D + j, 1)] if not isinstance(j, int) else G[:, D:D + 1],
                                                      1.0, None, ALU.mult)
                                dve.tensor_copy(XT[:].rearrange("p k t -> p (k t)"), pX[:, 0:D]).then_inc(xt_ready, 1)

                            dve.memset(G[:, width:width + 1], 0.0).then_inc(spare_set, 1)
                            dve.wait_ge(spare_set, 1)
                            column(0)

                            def body(j, e, u):
                                dve.wait_ge(fc1_done, j * 2 + 2)
                                column(j + 1)
                                dve.wait_ge(fc2_done, j + 1)
                                dve.wait_ge(yg_ready, j)
                                dve.tensor_tensor(yt[:], pY[:, 0:D], b2t[:, ds(e, 1)].rearrange("p a d -> p (a d)"), ALU.add).then_inc(y_read, 1)
                                dve.wait_ge(y_read, j + 1)
                                dve.wait_ge(scattered, j * 16)
                                gate = gates[:, ds(j, 1)]
                                if out_width > D:
                                    dve.tensor_scalar(yg[:, D:D + 1], gate, 1.0, None, ALU.mult)
                                dve.tensor_scalar(yg[:, 0:D], yt[:], gate, None, ALU.mult).then_inc(yg_ready, 1)
                            per_block(dve, "dve", body)

                    return gathered, scattered

            w_round = [0]
            expert_phase("m", table, ROW, acc0, D + 1, idx, idx, gtab, True, b1_sb, b2_sb, w1, w2,
                         E0, ACT.Gelu, None, False)
        if upto == "moe0":
            return

        mid.close()

        late = ctx.enter_context(ExitStack())
        xc = sb("xc", [P, T, D], into=late)
        W = sb("W", [P, T, EG], into=late)
        lg = sb("lg2", [P, T, E1], into=late)
        oh = sb("oh", [P, 2, T, E1], into=late)
        best2 = sb("best2", [P, 2, T], into=late)
        red = sb("red", [P, 2, T], into=late)
        scr = sb("scr", [P, T, E1], into=late)
        rev = sb("rev", [P, E1], into=late)
        lgc = sb("lgc", [P, B, E1], into=late)
        c1_sb = sb("c1_sb", [P, E1, FC], into=late)
        c2_sb = sb("c2_sb", [P, E1, D], into=late)
        zpad = sb("zpad", [P, D], into=late)
        late_const = sem("late_const")
        c_late = sem("c_late")
        acc1_set = sem("acc1_set")

        def softmax(dve, link, link_exp):
            link(dve.tensor_reduce(red[:, 0], lg[:], AX, ALU.max))
            link(dve.tensor_tensor(lg[:], lg[:], bcast(red[:, 0], E1), ALU.subtract))
            link_exp()
            link(dve.tensor_reduce(red[:, 0], lg[:], AX, ALU.add))
            link(dve.reciprocal(red[:, 1], red[:, 0]))
            link(dve.tensor_tensor(lg[:], lg[:], bcast(red[:, 1], E1), ALU.mult))

        def top_two(dve, link):
            for n in range(2):
                link(dve.tensor_reduce(best2[:, n], lg[:], AX, ALU.max))
                link(dve.tensor_tensor(scr[:], lg[:], bcast(best2[:, n], E1), ALU.is_equal))
                link(dve.tensor_tensor(scr[:], scr[:], repeat(rev[:], T), ALU.mult))
                link(dve.tensor_reduce(red[:, 0], scr[:], AX, ALU.max))
                link(dve.tensor_tensor(oh[:, n], scr[:], bcast(red[:, 0], E1), ALU.is_equal))
                if n == 0:
                    link(dve.scalar_tensor_tensor(lg[:], oh[:, 0], -4.0, lg[:], ALU.mult, ALU.add))

        x1T = sb("x1T", [P, KD, B * N], into=late)
        NCH, CH = 4, 512
        TC = CH // P

        class Logits:

            def __init__(self, tag, ph, rows, router, cond_bias=None):
                self.rows, self.router, self.cond_bias = rows, router, cond_bias
                self.lT = sb(tag + "lT", [E1, 2, CH], into=ph)
                self.pt = ps(tag + "pt", [P, 2, KD, 512], ph)
                self.pl = ps(tag + "pl", [P, 2, 512], ph)
                self.pb = ps(tag + "pb", [P, 512], ph)
                self.row_ready, self.turned, self.low_ready, self.high_ready, self.lg_done, self.lt_ready, self.back = [
                    sem(tag + n) for n in ("row_ready", "turned", "low_ready", "high_ready", "lg_done", "lt_ready", "back")]

            def pe_logits(self, pe, c):
                pe.wait_ge(self.low_ready, c + 1)
                pe.wait_ge(self.high_ready, c + 1)
                for k in range(KD):
                    ins = pe.matmul(self.pl[0:E1, c % 2], self.router[:, k], x1T[:, k, c * CH:(c + 1) * CH],
                                    start=(k == 0), stop=(k == KD - 1))
                ins.then_inc(self.lg_done, 1)

            def pe_back(self, pe, c):
                pe.wait_ge(self.lt_ready, c + 1)
                for i in range(TC):
                    t = TC * c + i
                    ins = pe.transpose(self.pb[:, t * E1:(t + 1) * E1], self.lT[:, c % 2, i * P:(i + 1) * P],
                                       ident[0:E1, 0:E1])
                ins.then_inc(self.back, 1)

            def tensor(self, pe):
                for c in range(NCH):
                    pe.wait_ge(self.row_ready, TC * c + TC)
                    if c >= 2:
                        pe.wait_ge(self.low_ready, c - 1)
                        pe.wait_ge(self.high_ready, c - 1)
                    for k in range(KD):
                        for i in range(TC):
                            ins = pe.transpose(self.pt[:, c % 2, k, i * P:(i + 1) * P],
                                               self.rows[:, TC * c + i, k * P:(k + 1) * P], ident[:])
                        ins.then_inc(self.turned, 1)
                    if c >= 1:
                        self.pe_logits(pe, c - 1)
                    if c >= 2:
                        self.pe_back(pe, c - 2)
                self.pe_logits(pe, NCH - 1)
                self.pe_back(pe, NCH - 2)
                self.pe_back(pe, NCH - 1)

            def scalar(self, act):
                def keep(c):
                    act.wait_ge(self.lg_done, c + 1)
                    if c >= 2:
                        act.wait_ge(self.back, c - 1)
                    bias = 0.0 if self.cond_bias is None else self.cond_bias[:, c * CH // N:c * CH // N + 1]
                    act.activation(self.lT[:, c % 2], self.pl[0:E1, c % 2], ACT.Identity, bias=bias).then_inc(self.lt_ready, 1)

                for c in range(NCH):
                    act.wait_ge(self.turned, 2 * c + 1)
                    act.activation(x1T[:, 0, c * CH:(c + 1) * CH], self.pt[:, c % 2, 0], ACT.Copy).then_inc(self.low_ready, 1)
                    if c >= 1:
                        keep(c - 1)
                keep(NCH - 1)

            def vector_half(self, dve, c):
                dve.wait_ge(self.turned, 2 * c + 2)
                dve.tensor_copy(x1T[:, 1, c * CH:(c + 1) * CH], self.pt[:, c % 2, 1]).then_inc(self.high_ready, 1)

        if True:
            with ExitStack() as ph:
                sums = sb("sums", [P, T, D + 1], into=ph)
                den = sb("den", [P, 2, T], into=ph)
                wt_sb = sb("wt_sb", [P, KD, E1], into=ph)
                wg_sb = sb("wg_sb", [DH, E1], into=ph)
                cT = sb("cT", [DH, B], into=ph)
                cond_bias = sb("cond_bias", [E1, B], into=ph)
                route = Logits("f_", ph, x_sb, wt_sb, cond_bias)
                pc = ps("f_pc", [P, 512], ph)
                sums_in, f_in, f_step, cond_done, cond_kept, f_exp = [
                    sem(f"f_{n}") for n in ("sums_in", "in", "step", "cond_done", "cond_kept", "exp")]
                with nc.Block() as block:
                    @block.sync
                    def _(sp):
                        sp.dma_start(sums[:], acc0.rearrange("(t p) d -> p t d", p=P)).then_inc(sums_in, 16)
                        sp.dma_start(wt_sb[:], wt).then_inc(f_in, 16)
                        sp.dma_start(wg_sb[:], wg).then_inc(f_in, 16)
                        sp.dma_start(cT[:], condT).then_inc(f_in, 16)
                        sp.dma_start(c1_sb[:], c1).then_inc(c_late, 16)
                        sp.dma_start(c2_sb[:].rearrange("p e d -> p (e d)"), c2.partition_broadcast(P)).then_inc(c_late, 16)
                        for u in range(RING):
                            load_expert(sp, v1, v2, u, u)
                        sp.wait_ge(route.row_ready, T)
                        sp.dma_start(acc1[0:B * N, :].rearrange("(t p) d -> p t d", p=P), x_sb[:]).then_inc(acc1_set, 16)
                        sp.wait_ge(late_const, 2)
                        sp.dma_start(acc1[B * N:B * N + P, :], zpad[:]).then_inc(acc1_set, 16)
                        sp.wait_ge(f_in, 48)
                        sp.wait_ge(c_late, 32)

                    @block.gpsimd
                    def _(pool):
                        pool.iota(rev[:], pattern=[[-1, E1]], base=E1, channel_multiplier=0,
                                  allow_small_or_imprecise_dtypes=True).then_inc(late_const, 1)
                        pool.memset(zpad[:], 0.0).then_inc(late_const, 1)
                        pool.memset(W[:, :, E1:EG], 1.0).then_inc(late_const, 1)
                    @block.vector
                    def _(dve):
                        steps = [0]

                        def link(ins):
                            steps[0] += 1
                            ins.then_inc(f_step, 1)
                            dve.wait_ge(f_step, steps[0])

                        dve.wait_ge(sums_in, 16)
                        link(dve.tensor_scalar(den[:, 0], sums[:, :, D], 0.0, None, ALU.is_le))
                        link(dve.tensor_tensor(den[:, 0], den[:, 0], sums[:, :, D], ALU.add))
                        link(dve.reciprocal(den[:, 1], den[:, 0]))
                        for c in range(NCH):
                            for t in range(TC * c, TC * c + TC):
                                dve.scalar_tensor_tensor(x_sb[:, t], sums[:, t, 0:D], den[:, 1, t:t + 1], x_sb[:, t],
                                                         ALU.mult, ALU.add).then_inc(route.row_ready, 1)
                            if c >= 1:
                                route.vector_half(dve, c - 1)
                        route.vector_half(dve, NCH - 1)
                        dve.wait_ge(route.back, NCH)
                        link(dve.tensor_copy(lg[:].rearrange("p t e -> p (t e)"), route.pb[:, 0:T * E1]))
                        softmax(dve, link, lambda: dve.wait_ge(f_exp, 1))
                        dve.wait_ge(late_const, 3)
                        top_two(dve, link)
                        link(dve.tensor_tensor(red[:, 0], best2[:, 0], best2[:, 1], ALU.add))
                        link(dve.tensor_scalar(red[:, 0], red[:, 0], 1e-20, None, ALU.add))
                        link(dve.reciprocal(red[:, 1], red[:, 0]))
                        for n in range(2):
                            link(dve.tensor_tensor(best2[:, n], best2[:, n], red[:, 1], ALU.mult))
                        link(dve.tensor_tensor(scr[:], oh[:, 0], bcast(best2[:, 0], E1), ALU.mult))
                        link(dve.tensor_tensor(lg[:], oh[:, 1], bcast(best2[:, 1], E1), ALU.mult))
                        link(dve.tensor_tensor(W[:, :, 0:E1], scr[:], lg[:], ALU.add))

                    @block.scalar
                    def _(act):
                        act.wait_ge(cond_done, 1)
                        act.activation(cond_bias[:], pc[0:E1, 0:B], ACT.Copy).then_inc(cond_kept, 1)
                        act.wait_ge(cond_kept, 1)
                        route.scalar(act)
                        act.wait_ge(f_step, 6)
                        act.activation(lg[:], lg[:], ACT.Exp, scale=0.5).then_inc(f_exp, 1)

                    @block.tensor
                    def _(pe):
                        pe.wait_ge(f_in, 48)
                        pe.matmul(pc[0:E1, 0:B], wg_sb[:], cT[:], start=True, stop=True).then_inc(cond_done, 1)
                        route.tensor(pe)
            if upto == "x1":
                return

            with ExitStack() as ph:
                STEPS = EG * NCH
                gw = sb("gw", [P, 2, KD, M1], into=ph)
                uw = sb("uw", [P, 2, KD, M1], into=ph)
                dw = sb("dw", [P, 2, D], into=ph)
                ga = sb("ga", [P, CH], into=ph)
                lk = sb("lk", [P, CH], into=ph)
                hid = sb("hid", [P, 2, CH], into=ph)
                pG = ps("pG", [P, 2, 512], ph)
                pU = ps("pU", [P, 2, 512], ph)
                pY = ps("pYc", [P, 2, 2, 512], ph)
                cw_in = [sem(f"cw_in{u}") for u in range(2)]
                up_done, ga_ready, lk_ready, hid_ready, down_done, acc_done = [
                    sem(f"d_{n}") for n in ("up_done", "ga_ready", "lk_ready", "hid_ready", "down_done", "acc_done")]

                def all_steps(eng, body):
                    def pair(r, peeled):
                        for u in range(2):
                            for c in range(NCH):
                                body(2 * r + u, (2 * r + u) * NCH + c, u, c, peeled and u == 1 and c == NCH - 1)
                    with eng.Fori(0, EG // 2 - 1) as r:
                        pair(r, False)
                    pair(EG // 2 - 1, True)

                with nc.Block() as block:
                    @block.sync
                    def _(sp):
                        def load(e, u):
                            one = ds(e, 1)
                            sp.dma_start(gw[:, u], wgate[one].rearrange("a (k p) m -> p (a k) m", p=P)).then_inc(cw_in[u], 16)
                            sp.dma_start(uw[:, u], wup[one].rearrange("a (k p) m -> p (a k) m", p=P)).then_inc(cw_in[u], 16)
                            sp.dma_start(dw[:, u], wdown[one].rearrange("a p d -> p (a d)")).then_inc(cw_in[u], 16)
                        for u in range(2):
                            load(u, u)
                        with sp.Fori(0, EG // 2 - 1) as r:
                            for u in range(2):
                                sp.wait_ge(down_done, (2 * r + u + 1) * NCH)
                                load(2 * r + u + 2, u)
                        sp.wait_ge(acc1_set, 32)

                    @block.tensor
                    def _(pe):
                        def up(s, u, c, at):
                            for ww, pp in ((gw, pG), (uw, pU)):
                                for k in range(KD):
                                    ins = pe.matmul(pp[:, at], ww[:, u, k], x1T[:, k, c * CH:(c + 1) * CH],
                                                    start=(k == 0), stop=(k == KD - 1))
                            ins.then_inc(up_done, 1)

                        pe.wait_ge(cw_in[0], 48)
                        up(0, 0, 0, 0)

                        def body(e, s, u, c, last):
                            if not last:
                                if c == NCH - 1:
                                    r = (e - u) // 2 if isinstance(e, int) else None
                                    nxt = 1 - u
                                    rounds = (s - (u * NCH + c)) * 6
                                    pe.wait_ge(cw_in[nxt], rounds + (48 if u == 0 else 96))
                                pe.wait_ge(hid_ready, s)
                                up(s + 1, u if c < NCH - 1 else 1 - u, (c + 1) % NCH, (c + 1) % 2)
                            pe.wait_ge(hid_ready, s + 1)
                            pe.wait_ge(acc_done, s)
                            for j in range(4):
                                ins = pe.matmul(pY[:, c % 2, j // 2, (j % 2) * D:(j % 2 + 1) * D], hid[:, c % 2, j * P:(j + 1) * P],
                                                dw[:, u], start=True, stop=True)
                            ins.then_inc(down_done, 1)
                        all_steps(pe, body)

                    @block.scalar
                    def _(act):
                        def body(e, s, u, c, last):
                            act.wait_ge(up_done, s + 1)
                            act.wait_ge(hid_ready, s)
                            act.activation(ga[:], pG[:, c % 2], ACT.Copy).then_inc(ga_ready, 1)
                        all_steps(act, body)

                    @block.vector
                    def _(dve):
                        dve.memset(xc[:], 0.0).then_inc(acc_done, 1)

                        def hidden(s, at):
                            dve.wait_ge(ga_ready, s + 1)
                            dve.scalar_tensor_tensor(lk[:], ga[:], 0.01, ga[:], ALU.mult, ALU.max).then_inc(lk_ready, 1)
                            dve.wait_ge(lk_ready, s + 1)
                            dve.tensor_tensor(hid[:, at], lk[:], pU[:, at], ALU.mult).then_inc(hid_ready, 1)

                        hidden(0, 0)

                        def body(e, s, u, c, last):
                            if not last:
                                dve.wait_ge(hid_ready, s + 1)
                                hidden(s + 1, (c + 1) % 2)
                            dve.wait_ge(down_done, s + 1)
                            dve.wait_ge(acc_done, s + 1)
                            for j in range(4):
                                t = 4 * c + j
                                ins = dve.scalar_tensor_tensor(xc[:, t], pY[:, c % 2, j // 2, (j % 2) * D:(j % 2 + 1) * D],
                                                               W[:, t, ds(e, 1)], xc[:, t], ALU.mult, ALU.add)
                            ins.then_inc(acc_done, 1)
                        all_steps(dve, body)
        if upto == "y":
            return

        COLS = BLK + 2
        gtab = sb("gates2", [P, COLS], into=late)
        gidx = sb("gidx", [P, COLS], U32, into=late)
        sidx = sb("sidx", [P, COLS], U32, into=late)
        nblk = sb("nblk", [1, E1], I32, into=late)
        ends = sb("ends", [1, E1], I32, into=late)
        with ExitStack() as ph:
            wr_sb = sb("wr_sb", [P, KD, E1], into=ph)
            before = sb("before", [P, P], into=ph)
            zeros = sb("zeros", [P, P], into=ph)
            lane = sb("lane", [P, P], into=ph)
            route = Logits("h_", ph, xc, wr_sb)
            token = sb("token", [P, T], into=ph)
            spare = sb("spare", [P, 1], into=ph)
            M = sb("M", [P, T, E1], into=ph)
            tot = sb("tot", [P, 2, T, E1], into=ph)
            slot = sb("slot", [P, T, E1], into=ph)
            blocks = sb("blocks", [P, 4, E1], into=ph)
            blocksi = sb("blocksi", [P, 2, E1], I32, into=ph)
            at = sb("at", [P, 2, T], into=ph)
            ati = sb("ati", [P, 2, 2, T], I32, into=ph)
            lanes = sb("lanes", [P, 2, T], into=ph)
            block_of = sb("block_of", [P, 2, T], into=ph)
            A = sb("A", [P, T, 2, P], into=ph)
            Bv = sb("Bv", [P, T, 2, 3, COLS], into=ph)
            empty = sb("empty", [P, COLS], into=ph)
            pPQ = route.pl
            pP, pQ = pPQ[:, 0], pPQ[:, 1]
            pM = ps("h_pM", [P, 512], ph)
            (h_in, h_const, h_step, y_out, h_exp, counted, a_ready, a_used) = [sem(f"h_{n}") for n in (
                "in", "const", "step", "y_out", "exp", "counted", "a_ready", "a_used")]
            m_ready = sem("h_m_ready")
            b_ready = sem("h_b_ready")
            with nc.Block() as block:
                @block.sync
                def _(sp):
                    sp.sem_inc(route.row_ready, T)
                    sp.dma_start(wr_sb[:], wr).then_inc(h_in, 16)
                    sp.dma_start(ytab.rearrange("(t p) d -> p t d", p=P), xc[:]).then_inc(y_out, 16)
                    sp.wait_ge(y_out, 16)
                    sp.wait_ge(h_in, 16)

                @block.gpsimd
                def _(pool):
                    pool.iota(lane[:], pattern=[[1, P]], base=0, channel_multiplier=0,
                              allow_small_or_imprecise_dtypes=True).then_inc(h_const, 1)
                    pool.iota(token[:], pattern=[[P, T]], base=0, channel_multiplier=1,
                              allow_small_or_imprecise_dtypes=True).then_inc(h_const, 1)
                    pool.iota(spare[:], pattern=[[0, 1]], base=B * N, channel_multiplier=1,
                              allow_small_or_imprecise_dtypes=True).then_inc(h_const, 1)
                    pool.memset(zeros[:], 0.0).then_inc(h_const, 1)
                    pool.affine_select(out=before[:], in_=ones[:], compare_op=ALU.is_ge, fill=0.0, base=-1,
                                       pattern=[[1, P]], channel_multiplier=-1).then_inc(h_const, 1)

                @block.vector
                def _(dve):
                    steps = [0]

                    def link(ins):
                        steps[0] += 1
                        ins.then_inc(h_step, 1)
                        dve.wait_ge(h_step, steps[0])

                    for c in range(NCH):
                        route.vector_half(dve, c)
                    dve.wait_ge(route.back, NCH)
                    link(dve.tensor_copy(lg[:].rearrange("p t e -> p (t e)"), route.pb[:, 0:T * E1]))
                    softmax(dve, link, lambda: dve.wait_ge(h_exp, 1))
                    top_two(dve, link)
                    dve.wait_ge(h_const, 5)
                    dve.tensor_tensor(M[:], oh[:, 0], oh[:, 1], ALU.add).then_inc(m_ready, 1)
                    dve.wait_ge(counted, 1)
                    link(dve.tensor_copy(tot[:, 0].rearrange("p t e -> p (t e)"), pQ[:, 0:T * E1]))
                    for n in range(4):
                        a, b, w = n % 2, (n + 1) % 2, 1 << n
                        link(dve.tensor_copy(tot[:, b, 0:w], tot[:, a, 0:w]))
                        link(dve.tensor_tensor(tot[:, b, w:T], tot[:, a, w:T], tot[:, a, 0:T - w], ALU.add))
                    link(dve.tensor_scalar(blocksi[:, 0], tot[:, 0, T - 1], float(P - 1), None, ALU.add))
                    link(dve.tensor_scalar(blocksi[:, 1], blocksi[:, 0], 7, None, ALU.arith_shift_right))
                    link(dve.tensor_copy(blocks[:, 0], blocksi[:, 1]))
                    link(dve.tensor_copy(blocks[:, 3], blocks[:, 0]))
                    for n in range(3):
                        a, b, w = (0, 1, 2)[n], (1, 2, 0)[n], 1 << n
                        link(dve.tensor_copy(blocks[:, b, 0:w], blocks[:, a, 0:w]))
                        link(dve.tensor_tensor(blocks[:, b, w:E1], blocks[:, a, w:E1], blocks[:, a, 0:E1 - w], ALU.add))
                    link(dve.tensor_copy(nblk[:], blocks[0:1, 3]))
                    link(dve.tensor_copy(ends[:], blocks[0:1, 0]))
                    link(dve.tensor_tensor(blocks[:, 3], blocks[:, 0], blocks[:, 3], ALU.subtract))
                    link(dve.tensor_scalar(blocks[:, 3], blocks[:, 3], float(P), None, ALU.mult))
                    link(dve.tensor_copy(slot[:, 0], blocks[:, 3]))
                    link(dve.tensor_tensor(slot[:, 1:T], tot[:, 0, 0:T - 1], repeat(blocks[:, 3], T - 1), ALU.add))
                    link(dve.tensor_tensor(slot[:].rearrange("p t e -> p (t e)"), slot[:].rearrange("p t e -> p (t e)"),
                                           pP[:, 0:T * E1], ALU.add))
                    for n in range(2):
                        link(dve.tensor_tensor(scr[:], slot[:], oh[:, n], ALU.mult))
                        link(dve.tensor_reduce(at[:, n], scr[:], AX, ALU.add))
                    link(dve.tensor_copy(ati[:, 0], at[:]))
                    link(dve.tensor_scalar(ati[:, 1], ati[:, 0], P - 1, None, ALU.bitwise_and))
                    link(dve.tensor_copy(lanes[:], ati[:, 1]))
                    link(dve.tensor_scalar(ati[:, 1], ati[:, 0], 7, None, ALU.arith_shift_right))
                    link(dve.tensor_copy(block_of[:], ati[:, 1]))
                    cols = lane[:, 0:COLS]
                    for c in range(NCH):
                        ts = slice(TC * c, TC * c + TC)
                        for n in range(2):
                            dve.tensor_tensor(A[:, ts, n], repeat(lane[:], TC), bcast(lanes[:, n, ts], P), ALU.is_equal)
                            dve.tensor_tensor(Bv[:, ts, n, 2], repeat(cols, TC), bcast(block_of[:, n, ts], COLS),
                                              ALU.is_equal).then_inc(b_ready, 1)
                        dve.wait_ge(b_ready, 2 * c + 2)
                        for n in range(2):
                            dve.tensor_tensor(Bv[:, ts, n, 0], Bv[:, ts, n, 2], bcast(token[:, ts], COLS), ALU.mult)
                            dve.tensor_tensor(Bv[:, ts, n, 1], Bv[:, ts, n, 2], bcast(best2[:, n, ts], COLS),
                                              ALU.mult).then_inc(a_ready, 1)
                    dve.wait_ge(a_used, 1)
                    link(dve.tensor_copy(gidx[:], pM[:, 0:COLS]))
                    link(dve.tensor_copy(gtab[:], pM[:, COLS:2 * COLS]))
                    link(dve.tensor_scalar(empty[:], pM[:, 2 * COLS:3 * COLS], -1.0, 1.0, ALU.mult, ALU.add))
                    link(dve.tensor_scalar(empty[:], empty[:], spare[:, 0:1], None, ALU.mult))
                    link(dve.tensor_tensor(sidx[:], empty[:], pM[:, 0:COLS], ALU.add))

                @block.scalar
                def _(act):
                    route.scalar(act)
                    act.wait_ge(h_step, 3)
                    act.activation(lg[:], lg[:], ACT.Exp).then_inc(h_exp, 1)

                @block.tensor
                def _(pe):
                    pe.wait_ge(h_in, 16)
                    route.tensor(pe)
                    pe.wait_ge(h_const, 5)
                    pe.wait_ge(m_ready, 1)
                    pe.matmul(pP[:, 0:T * E1], before[:], M[:].rearrange("p t e -> p (t e)"), start=True, stop=True)
                    pe.matmul(pQ[:, 0:T * E1], ones[:], M[:].rearrange("p t e -> p (t e)"), start=True, stop=True).then_inc(counted, 1)
                    pe.matmul(pM[:, 0:P], zeros[:], zeros[:], start=True, stop=False)
                    for t in range(T):
                        if t % TC == 0:
                            pe.wait_ge(a_ready, 2 * (t // TC) + 2)
                        for n in range(2):
                            pe.matmul(pM[:, 0:3 * COLS], A[:, t, n], Bv[:, t, n].rearrange("p v c -> p (v c)"),
                                      start=False, stop=False)
                    pe.matmul(pM[:, 0:P], zeros[:], zeros[:], start=False, stop=True).then_inc(a_used, 1)
        if upto == "route1":
            return

        w_round[0] = E0 // RING
        expert_phase("n", ytab, D, acc1, D, gidx, sidx, gtab, False, c1_sb, c2_sb, v1, v2,
                     E1, ACT.Gelu_apprx_tanh, (nblk, ends), False)
        late.close()
        result_out = sem("result_out")
        with nc.Block() as block:
            @block.sync
            def _(sp):
                sp.dma_start(out.rearrange("b n d -> (b n) d"), acc1[0:B * N, :]).then_inc(result_out, 16)
                sp.wait_ge(result_out, 16)


_OUTS = [((B, N, D), "float32")]


def kernel(**i):
    import numpy as np
    import concourse.bacc as bacc
    from concourse.bass_utils import run_bass_kernel_spmd as run

    halves = lambda w: w.reshape(D, 2, M1).transpose(1, 0, 2)
    cols = lambda w: w.reshape(KD, P, -1).transpose(1, 0, 2)
    laid = {
        "x": i["x"], "bias": i["fside_16xSxS_0"], "cond": i["cond_64"], "condT": i["cond_64"].T,
        "mask": i["mask_BxS_bk0"].reshape(1, B * N),
        "g_in": i["L0_cond_g_in"].reshape(KD, P).T, "null_bias": i["L0_cond_null_attn_bias"].reshape(1, H),
        "wq": i["L0_cond_Wq"], "wkv": i["L0_cond_Wkv"], "wo": i["L0_cond_Wo"],
        "g_out": i["L0_cond_g_out"].reshape(1, D), "norm_w": i["L0_ffn_norm_weight"].reshape(1, D),
        "rw": cols(np.asarray(i["L0_ffn_router_weight"]).T), "rb": i["L0_ffn_router_bias"].reshape(1, E0),
        "w1": i["L0_ffn_fc1_weight"].transpose(0, 2, 1), "b1": i["L0_ffn_fc1_bias"].reshape(E0, FC, P).transpose(2, 0, 1),
        "w2": i["L0_ffn_fc2_weight"].transpose(0, 2, 1), "b2": i["L0_ffn_fc2_bias"].reshape(1, E0 * D),
        "wt": cols(np.asarray(i["L1_cond_wt"]).T), "wg": i["L1_cond_wg"].T,
        "wgate": np.concatenate([i["L1_cond_w_gate"], halves(i["L1_cond_sw_gate"])]),
        "wup": np.concatenate([i["L1_cond_w_up"], halves(i["L1_cond_sw_up"])]),
        "wdown": np.concatenate([i["L1_cond_w_down"], i["L1_cond_sw_down"].reshape(2, M1, D)]),
        "wr": cols(i["L1_ffn_w_router"]), "v1": i["L1_ffn_w1"],
        "c1": i["L1_ffn_b1"].reshape(E1, FC, P).transpose(2, 0, 1),
        "v2": i["L1_ffn_w2"], "c2": i["L1_ffn_b2"].reshape(1, E1 * D),
    }
    nc = bacc.Bacc("TRN2", target_bir_lowering=False, num_devices=1)
    arrays, args = {}, []
    for name, a in laid.items():
        a = np.ascontiguousarray(a)
        arrays[f"in_{name}"] = a
        args.append(nc.dram_tensor(f"in_{name}", a.shape, mybir.dt.from_np(a.dtype), kind="ExternalInput").ap())
    shape, dtype = _OUTS[0]
    result = nc.dram_tensor("out_0", shape, mybir.dt.from_np(np.dtype(dtype)), kind="ExternalOutput").ap()
    moe_kernel(nc, *args, result)
    r = run(nc, [arrays], core_ids=[0])
    return r.results[0]["out_0"]
```

```python
from contextlib import ExitStack

import concourse.bass as bass
from concourse import mybir

P = 128
F32 = mybir.dt.float32
I32 = mybir.dt.int32
U32 = mybir.dt.uint32
U8 = mybir.dt.uint8
F32R = mybir.dt.float32r
HIGH = -4096
ALU = mybir.AluOpType
ACT = mybir.ActivationFunctionType
AX = mybir.AxisListType.X
ds = bass.ds

B, N, D = 2, 1024, 256
KD = D // P
T = B * N // P
QT = N // P
H, DH = 16, 64
E0, F0 = 16, 1024
FC = F0 // P
CAP = B * N // E0
E1, M1 = 8, 128
EG = E1 + 2
BLK = 2 * B * N // P + E1
ROW = D + E0
RING = 4
EPS = 1e-5
HIDE = -1e38
CPE = P // E0
CW = B * N // CPE
assert CAP == P and F0 == 1024


def bcast(ap, n):
    return ap.unsqueeze(2).to_broadcast([ap.shape[0], ap.shape[1], n])


def repeat(ap, n):
    return ap.unsqueeze(1).to_broadcast([ap.shape[0], n, ap.shape[1]])


def done(n):
    return n + 1


def moe_kernel(nc, x, bias, cond, condT, mask, g_in, null_bias, wq, wkv, wo, g_out, norm_w, rw, rb,
               w1, b1, w2, b2, wt, wg, wgate, wup, wdown, wr, v1, c1, v2, c2, out, upto="end"):
    with ExitStack() as ctx:
        def sem(name):
            return ctx.enter_context(nc.semaphore(name))

        def sb(name, shape, dt=F32, into=ctx):
            return into.enter_context(nc.sbuf_tensor(name, shape, dt))

        def ps(name, shape, into):
            return into.enter_context(nc.psum_tensor(name, shape, F32))

        def dram(name, shape):
            return nc.dram_tensor(name, shape, F32, kind="Internal").ap()

        table = dram("table", (B * N + P, ROW))
        acc0 = dram("acc0", (B * N, D + 1))
        ytab = dram("ytab", (B * N, D))
        acc1 = dram("acc1", (B * N + P, D))

        x_sb = sb("x_sb", [P, T, D])
        ident = sb("ident", [P, P])
        ones = sb("ones", [P, P])
        w1_sb = sb("w1_sb", [P, RING, KD, F0])
        w2_sb = sb("w2_sb", [P, RING, FC, D])
        stats = sb("stats", [P, T, 6])
        mom = sb("mom", [P, 5, T])
        MEAN, VAR, RSTD, TMP, TMQ = range(5)
        gi = sb("gi", [P, 1], U32)
        si = sb("si", [P, 1], U32)
        held = sb("held", [P, 4])

        w_in = [sem(f"w_in{u}") for u in range(RING)]
        consts_done = sem("consts_done")
        x_in = sem("x_in")

        def load_expert(eng, w1t, w2t, e, u):
            eng.dma_start(w1_sb[:, u], w1t[e].rearrange("(k p) f -> p k f", p=P)).then_inc(w_in[u], 16)
            eng.dma_start(w2_sb[:, u], w2t[e].rearrange("(c p) d -> p c d", p=P)).then_inc(w_in[u], 16)

        def load_expert_at(eng, w1t, w2t, e, u):
            eng.dma_start(w1_sb[:, u], w1t[ds(e, 1)].rearrange("a (k p) f -> p (a k) f", p=P)).then_inc(w_in[u], 16)
            eng.dma_start(w2_sb[:, u], w2t[ds(e, 1)].rearrange("a (c p) d -> p (a c) d", p=P)).then_inc(w_in[u], 16)

        def held_here(pool, n):
            pool.tensor_tensor(held[:, n:n + 1], ones[:, 0:1], ones[:, 0:1], ALU.mult)

        def finish_moments(dve, link):
            ev, od = stats[:, :, 1], stats[:, :, 4]
            link(dve.tensor_tensor(mom[:, MEAN], ev, od, ALU.add))
            link(dve.tensor_tensor(mom[:, TMP], ev, od, ALU.subtract))
            link(dve.tensor_scalar(mom[:, MEAN], mom[:, MEAN], 0.5, None, ALU.mult))
            link(dve.tensor_scalar(mom[:, TMP], mom[:, TMP], 0.5, None, ALU.mult))
            link(dve.tensor_tensor(mom[:, TMP], mom[:, TMP], mom[:, TMP], ALU.mult))
            link(dve.tensor_tensor(mom[:, TMQ], stats[:, :, 2], stats[:, :, 5], ALU.add))
            link(dve.scalar_tensor_tensor(mom[:, VAR], mom[:, TMQ], 1.0 / D, mom[:, TMP], ALU.mult, ALU.add))

        mid = ctx.enter_context(ExitStack())
        idx = sb("idx", [P, E0 + 2], U32, into=mid)
        gtab = sb("gtab", [P, E0 + 1], into=mid)
        lg_all = sb("lg", [P, T + 1, E0], into=mid)
        LT_all = sb("LT", [E0, B * N + P], into=mid)
        lg, LT = lg_all[:, 0:T], LT_all[:, 0:B * N]
        wq_in, wo_in = sem("wq_in"), sem("wo_in")

        att = ctx.enter_context(ExitStack())
        xnT = sb("xnT", [P, KD, B * N], into=att)
        kT = sb("kT", [P, B * N], into=att)
        v_sb = sb("v_sb", [P, T, DH], into=att)
        hide = sb("hide", [P, B * N], into=att)
        window = sb("window", [P, 2 * N - P], into=att)
        wq_sb = sb("wq_sb", [P, KD, H * DH], into=att)
        wo_sb = sb("wo_sb", [P, FC, D], into=att)
        wk2 = sb("wk2", [P, KD, 2, DH], into=att)
        wv = sb("wv", [P, KD, DH], into=att)
        gcol = sb("gcol", [P, KD], into=att)
        mask8 = sb("mask8", [P, B * N], U8, into=att)
        nkT = sb("nkT", [P, B], into=att)
        nk2 = sb("nk2", [P, 2], into=att)
        nv = sb("nv", [P, DH], into=att)
        unseen = sb("unseen", [P, D], into=att)
        nullb = sb("nullb", [P, H], into=att)
        blockseq = sb("blockseq", [1, B, QT], into=att)
        anylive = sb("anylive", [1, B, QT], into=att)
        startf = sb("startf", [1, B], into=att)
        start = sb("start", [1, B], I32, into=att)
        zrow = sb("zrow", [P, D + 1], into=att)
        go_b = sb("go_b", [P, D], into=att)
        nw_b = sb("nw_b", [P, D], into=att)
        rw_sb = sb("rw_sb", [P, KD, E0], into=att)
        rb_b = sb("rb_b", [P, E0], into=att)

        att_in, mask_in, moments, rooted, zeroed, acc0_zero, mask_step, pool_step = [
            sem(n) for n in ("att_in", "mask_in", "moments", "rooted", "zeroed", "acc0_zero", "mask_step", "pool_step")]
        ATT_LOADS = 12

        with nc.Block() as block:
            @block.sync
            def _(sp):
                sp.dma_start(mask8[:], mask.partition_broadcast(P)).then_inc(mask_in, 16)
                sp.dma_start(x_sb[:], x.rearrange("b (t p) d -> p (b t) d", p=P)).then_inc(x_in, 16)
                sp.dma_start(gcol[:], g_in).then_inc(att_in, 16)
                for half in range(2):
                    sp.dma_start(wk2[:, :, half], wkv[:, 0:DH].rearrange("(k p) n -> p k n", p=P)).then_inc(att_in, 16)
                    sp.dma_start(nkT[half * DH:(half + 1) * DH, :], condT).then_inc(att_in, 16)
                sp.dma_start(wv[:], wkv[:, DH:2 * DH].rearrange("(k p) n -> p k n", p=P)).then_inc(att_in, 16)
                sp.dma_start(nv[:], cond[1:2, :].partition_broadcast(P)).then_inc(att_in, 16)
                sp.dma_start(nullb[:], null_bias.partition_broadcast(P)).then_inc(att_in, 16)
                sp.dma_start(rw_sb[:], rw).then_inc(att_in, 16)
                sp.dma_start(rb_b[:], rb.partition_broadcast(P)).then_inc(att_in, 16)
                sp.dma_start(go_b[:], g_out.partition_broadcast(P)).then_inc(att_in, 16)
                sp.dma_start(nw_b[:], norm_w.partition_broadcast(P)).then_inc(att_in, 16)
                sp.dma_start(wo_sb[:], wo.rearrange("(c p) d -> p c d", p=P)).then_inc(wo_in, 16)
                sp.dma_start(wq_sb[:], wq.rearrange("(k p) n -> p k n", p=P)).then_inc(wq_in, 16)
                sp.wait_ge(zeroed, 1)
                sp.dma_start(acc0.rearrange("(t p) d -> p t d", p=P), repeat(zrow[:], T)).then_inc(acc0_zero, 16)

            @block.gpsimd
            def _(pool):
                pool.iota(blockseq[:], pattern=[[0, B], [1, QT]], base=-QT, channel_multiplier=0,
                          allow_small_or_imprecise_dtypes=True).then_inc(consts_done, 1)
                pool.memset(nk2[:], 0.0)
                pool.memset(stats[:], 0.0)
                pool.memset(zrow[:], 0.0).then_inc(zeroed, 1)
                pool.memset(ident[:], 0.0).then_inc(pool_step, 1)
                pool.wait_ge(pool_step, 1)
                pool.affine_select(out=ident[:], in_=ident[:], compare_op=ALU.not_equal, fill=1.0, base=0,
                                   pattern=[[-1, P]], channel_multiplier=1).then_inc(consts_done, 1)
                pool.memset(ones[:], 1.0).then_inc(consts_done, 1)
                pool.memset(window[:], 0.0).then_inc(pool_step, 1)
                pool.wait_ge(pool_step, 2)
                pool.affine_select(out=window[:], in_=window[:], compare_op=ALU.is_ge, fill=HIDE, base=N - P,
                                   pattern=[[-1, 2 * N - P]], channel_multiplier=1).then_inc(pool_step, 1)

            @block.vector
            def _(dve):
                dve.wait_ge(mask_in, 16)
                dve.tensor_reduce(anylive[:], mask8[0:1, :].rearrange("p (b t k) -> p b t k", b=B, k=P),
                                  AX, ALU.max).then_inc(mask_step, 1)
                dve.wait_ge(mask_step, 1)
                dve.wait_ge(consts_done, 1)
                dve.tensor_tensor(anylive[:], anylive[:], blockseq[:], ALU.mult).then_inc(mask_step, 1)
                dve.wait_ge(mask_step, 2)
                dve.tensor_reduce(startf[:], anylive[:], AX, ALU.min).then_inc(mask_step, 1)
                dve.wait_ge(mask_step, 3)
                dve.tensor_scalar(start[:], startf[:], float(QT), None, ALU.add).then_inc(mask_step, 1)
                dve.tensor_scalar(hide[:], mask8[:], 1.0, -HIDE, ALU.subtract, ALU.mult).then_inc(mask_step, 1)
                dve.wait_ge(mask_step, 5)

        def live_tiles(eng, name, on_tile, on_keys=None, after=None):
            nq, nk = eng.alloc_register(name + "_nq"), eng.alloc_register(name + "_nk")
            eng.reg_mov(nq, 0)
            eng.reg_mov(nk, 0)
            with eng.Fori(0, B) as b:
                first = eng.value_load(start[0:1, ds(b, 1)], min_val=0, max_val=QT)
                with eng.If(first < QT):
                    with eng.Fori(first, QT) as qt:
                        if on_tile:
                            on_tile(b, qt, eng.snap(nq))
                        if on_keys:
                            with eng.Fori(first, qt + 1) as kt:
                                on_keys(b, qt, kt, eng.snap(nq), eng.snap(nk))
                                eng.reg_add(nk, nk, 1)
                        if after:
                            after(b, qt, eng.snap(nq), eng.snap(nk))
                        eng.reg_add(nq, nq, 1)
            return nq

        with ExitStack() as ph:
            xrow = sb("xrow", [P, D], into=ph)
            xcol = sb("xcol", [P, KD, P], into=ph)
            pt = ps("a_pt", [P, 512], ph)
            pk = ps("a_pk", [P, 512], ph)
            pv = ps("a_pv", [P, 512], ph)
            nv2 = sb("nv2", [P, 2, DH], into=ph)
            nv2T = sb("nv2T", [P, P], into=ph)
            pn = ps("a_pn", [P, 512], ph)
            nv2_ready, nv2_turned, nv2_kept, unseen_done = [sem(n) for n in ("nv2_ready", "nv2_turned", "nv2_kept", "unseen_done")]
            stats_done, xn_row, xn_t, xn_col, xn_kept, kv_done, kv_kept = [
                sem(n) for n in ("stats_done", "xn_row", "xn_t", "xn_col", "xn_kept", "kv_done", "kv_kept")]
            with nc.Block() as block:
                @block.sync
                def _(sp):
                    for s in (stats_done, xn_t, xn_kept, kv_kept):
                        sp.sem_inc(s, 1)
                    sp.wait_ge(acc0_zero, 16)

                @block.gpsimd
                def _(pool):
                    def tile(b, qt, n):
                        pool.wait_ge(xn_col, 2 * n + 2)
                        held_here(pool, 0)
                        pool.tensor_copy(xnT[:, :, ds(b * N + qt * P, P)], xcol[:]).then_inc(xn_kept, 1)
                    live_tiles(pool, "pool_kv", tile)

                @block.vector
                def _(dve):
                    steps = [0]

                    def link(ins):
                        steps[0] += 1
                        ins.then_inc(moments, 1)
                        dve.wait_ge(moments, steps[0])

                    dve.wait_ge(x_in, 16)

                    def tile_stats(b, qt, n):
                        t = b * QT + qt
                        dve.bn_stats(stats[:, ds(t, 1)].rearrange("p a s -> p (a s)"),
                                     x_sb[:, ds(t, 1)].rearrange("p a d -> p (a d)")).then_inc(stats_done, 1)

                    tiles = live_tiles(dve, "dve_stats", tile_stats)
                    dve.wait_ge(stats_done, done(dve.snap(tiles)))
                    finish_moments(dve, link)
                    link(dve.tensor_scalar(mom[:, TMP], mom[:, VAR], EPS, None, ALU.add))
                    dve.wait_ge(rooted, 1)
                    link(dve.reciprocal(mom[:, RSTD], mom[:, TMQ]))

                    def tile(b, qt, n):
                        t = b * QT + qt
                        dve.wait_ge(xn_t, done(n))
                        dve.tensor_scalar(xrow[:], x_sb[:, ds(t, 1)].rearrange("p a d -> p (a d)"),
                                          mom[:, MEAN, ds(t, 1)], mom[:, RSTD, ds(t, 1)],
                                          ALU.subtract, ALU.mult).then_inc(xn_row, 1)
                    live_tiles(dve, "dve_kv", tile)
                    dve.wait_ge(unseen_done, 1)
                    dve.tensor_copy(unseen[:], pn[:, 0:D])

                @block.scalar
                def _(act):
                    act.wait_ge(att_in, 16 * ATT_LOADS)
                    act.activation(nv2[:], repeat(nv[:], 2), ACT.Copy).then_inc(nv2_ready, 1)
                    act.wait_ge(nv2_turned, 1)
                    act.activation(nv2T[:], pn[:, 0:P], ACT.Copy).then_inc(nv2_kept, 1)
                    act.wait_ge(moments, 8)
                    act.activation(mom[:, TMQ], mom[:, TMP], ACT.Sqrt).then_inc(rooted, 1)
                    for half in range(2):
                        rows = slice(half * DH, (half + 1) * DH)
                        act.activation(nk2[rows, half:half + 1], nkT[rows, 0:1], ACT.Copy)

                    def tile(b, qt, n):
                        act.wait_ge(xn_t, done(n + 1))
                        act.wait_ge(xn_kept, done(n))
                        for k in range(KD):
                            act.activation(xcol[:, k], pt[:, k * P:(k + 1) * P], ACT.Copy, scale=gcol[:, k:k + 1]).then_inc(xn_col, 1)
                        act.wait_ge(kv_done, n + 1)
                        act.activation(kT[:, ds(b * N + qt * P, P)], pk[:, 0:P], ACT.Copy).then_inc(kv_kept, 1)
                        act.activation(v_sb[:, ds(b * QT + qt, 1)].rearrange("p a d -> p (a d)"), pv[:, 0:DH],
                                       ACT.Copy).then_inc(kv_kept, 1)
                    live_tiles(act, "act_kv", tile)

                @block.tensor
                def _(pe):
                    pe.wait_ge(consts_done, 3)
                    pe.wait_ge(att_in, 16 * ATT_LOADS)
                    pe.wait_ge(nv2_ready, 1)
                    pe.transpose(pn[:, 0:P], nv2[:].rearrange("p a d -> p (a d)"), ident[:]).then_inc(nv2_turned, 1)
                    pe.wait_ge(nv2_kept, 1)
                    pe.wait_ge(wo_in, 16)
                    for c in range(FC):
                        ins = pe.matmul(pn[:, 0:D], nv2T[:], wo_sb[:, c], start=(c == 0), stop=(c == FC - 1))
                    ins.then_inc(unseen_done, 1)

                    def tile(b, qt, n):
                        pe.wait_ge(xn_row, n + 1)
                        for k in range(KD):
                            ins = pe.transpose(pt[:, k * P:(k + 1) * P], xrow[:, k * P:(k + 1) * P], ident[:])
                        ins.then_inc(xn_t, 1)
                        pe.wait_ge(xn_col, 2 * n + 2)
                        pe.wait_ge(kv_kept, done(2 * n))
                        for k in range(KD):
                            pe.matmul(pk[:, 0:P], wk2[:, k].rearrange("p a d -> p (a d)"), xcol[:, k],
                                      start=(k == 0), stop=(k == KD - 1))
                        for k in range(KD):
                            ins = pe.matmul(pv[:, 0:DH], xcol[:, k], wv[:, k], start=(k == 0), stop=(k == KD - 1))
                        ins.then_inc(kv_done, 1)
                    live_tiles(pe, "pe_kv", tile)

        with ExitStack() as ph:
            bias_sb = sb("bias_sb", [P, 2, H, P], into=ph)
            sc = sb("sc", [P, H, P], into=ph)
            PT = sb("PT", [P, 2, 4, P], into=ph)
            O = sb("O", [P, H, DH], into=ph)
            OT = sb("OT", [P, FC, P], into=ph)
            qT = sb("qT", [P, FC, P], into=ph)
            kblk = sb("kblk", [P, P], into=ph)
            vblk = sb("vblk", [P, DH], into=ph)
            comb = sb("comb", [P, P], into=ph)
            st = sb("st", [P, 8, H], into=ph)
            MAX, LEN, TMAX, NEG, DIF, ALPHA, RS, RL = range(8)
            yr = sb("yr", [P, D], into=ph)
            row = sb("row", [P, D], into=ph)
            col = sb("col", [P, KD, P], into=ph)
            st6 = sb("st6", [P, 6], into=ph)
            mv = sb("mv", [P, 8], into=ph)
            lgr = sb("lgr", [P, E0], into=ph)
            pS = ps("pS", [P, 4, 512], ph)
            pT = ps("pT", [P, 2, 512], ph)
            pO = ps("pO", [P, 2, 512], ph)
            (q_proj, q_ready, null_done, q_step, bias_in, staged, comb_ready, bias_ready, s_done, sc_ready, k_step, p_ready,
             alpha_ready, t_done, pt_ready, pv_done, k_done, o_ready, ot_done, ot_ready, o_proj, q_done, f_step, f_root,
             row_turned, col_ready, lg_done, lg_row, lt_done, lt_kept, row_out, ot_high) = [sem("t_" + n) for n in (
                 "q_proj", "q_ready", "null_done", "q_step", "bias_in", "staged", "comb_ready", "bias_ready", "s_done",
                 "sc_ready", "k_step", "p_ready", "alpha_ready", "t_done", "pt_ready", "pv_done", "k_done", "o_ready",
                 "ot_done", "ot_ready", "o_proj", "q_done", "f_step", "f_root", "row_turned", "col_ready", "lg_done",
                 "lg_row", "lt_done", "lt_kept", "row_out", "ot_high")]
            QSTEP = 4
            KSTEP = 20
            NEGATED = (5, 9, 13, 16)
            FSTEP = 24

            def by_bank(tile, g):
                if len(tile.shape) == 2:
                    return tile.rearrange("p (a i r) -> p a r i", a=2, r=2)[:, g // 2, g % 2]
                return tile.rearrange("p (a i r) k -> p a r i k", a=2, r=2)[:, g // 2, g % 2]

            def heads(g):
                return [8 * (g // 2) + g % 2 + 2 * i for i in range(4)]

            with nc.Block() as block:
                @block.sync
                def _(sp):
                    for s in (bias_in, pv_done, bias_ready, row_out, k_step, k_done):
                        sp.sem_inc(s, 1)
                    sp.sem_inc(ot_done, 2)
                    for s in (o_ready, ot_ready, ot_high):
                        sp.sem_inc(s, 1)
                    sp.sem_inc(sc_ready, 5)

                    def keys(b, qt, kt, nq, nk):
                        sp.wait_ge(bias_in, done(nk * 16))
                        sp.wait_ge(sc_ready, done(nk * 4))
                        sp.dma_start(bias_sb[:, ds(nk % 2, 1)].rearrange("p a h k -> p (a h) k"),
                                     bias[:, ds(qt * P, P), ds(kt * P, P)].rearrange("h q k -> q h k")).then_inc(bias_in, 16)
                    live_tiles(sp, "sp_att", None, keys)
                    for u in range(RING):
                        load_expert(sp, w1, w2, u, u)

                @block.gpsimd
                def _(pool):
                    def keys(b, qt, kt, nq, nk):
                        pool.wait_ge(pv_done, done(nk * 4))
                        pool.wait_ge(bias_ready, done(nk * 4))
                        pool.tensor_tensor(comb[:], window[:, ds((kt - qt + QT - 1) * P, P)],
                                           hide[:, ds(b * N + kt * P, P)], ALU.add).then_inc(comb_ready, 1)
                        pool.tensor_copy(kblk[:], kT[:, ds(b * N + kt * P, P)]).then_inc(staged, 1)
                        pool.tensor_copy(vblk[:], v_sb[:, ds(b * QT + kt, 1)].rearrange("p a d -> p (a d)")).then_inc(staged, 1)
                        pool.wait_ge(comb_ready, nk + 1)
                        pool.wait_ge(bias_in, done(nk * 16 + 16))
                        for g in range(4):
                            part = by_bank(bias_sb[:, ds(nk % 2, 1)].rearrange("p a h k -> p (a h) k"), g)
                            pool.tensor_tensor(part, part, repeat(comb[:], 4), ALU.add).then_inc(bias_ready, 1)
                    live_tiles(pool, "pool_att", None, keys)

                @block.tensor
                def _(pe):
                    def project(n):
                        pe.wait_ge(o_ready, n + 1)
                        for c in range(FC):
                            ins = pe.transpose(pT[:, c // 4, (c % 4) * P:(c % 4 + 1) * P],
                                               O[:, 2 * c:2 * c + 2].rearrange("p h d -> p (h d)"), ident[:])
                            if c % 4 == 3:
                                ins.then_inc(ot_done, 1)
                        pe.wait_ge(ot_ready, n + 1)
                        pe.wait_ge(ot_high, n + 1)
                        for c in range(FC):
                            ins = pe.matmul(pO[:, 0, 0:D], OT[:, c], wo_sb[:, c], start=(c == 0), stop=(c == FC - 1))
                        ins.then_inc(o_proj, 1)

                    def logits(n):
                        pe.wait_ge(f_step, n * FSTEP + FSTEP)
                        for k in range(KD):
                            ins = pe.transpose(pT[:, 0, k * P:(k + 1) * P], row[:, k * P:(k + 1) * P], ident[:])
                        ins.then_inc(row_turned, 1)
                        pe.wait_ge(col_ready, n + 1)
                        for k in range(KD):
                            ins = pe.matmul(pT[:, 1, 0:E0], col[:, k], rw_sb[:, k], start=(k == 0), stop=(k == KD - 1))
                        ins.then_inc(lg_done, 1)
                        pe.wait_ge(lg_row, n + 1)
                        pe.transpose(pT[0:E0, 0, 0:P], lgr[:], ident[:]).then_inc(lt_done, 1)

                    logits(0)
                    pe.wait_ge(wq_in, 16)

                    def queries(b, qt, nq):
                        pe.wait_ge(q_done, nq + 1)
                        for c in range(FC):
                            for k in range(KD):
                                ins = pe.matmul(pT[:, c // 4, (c % 4) * P:(c % 4 + 1) * P], wq_sb[:, k, c * P:(c + 1) * P],
                                                xnT[:, k, ds(b * N + qt * P, P)], start=(k == 0), stop=(k == KD - 1))
                        ins.then_inc(q_proj, 1)
                        pe.wait_ge(q_ready, nq * 2 + 2)
                        pe.wait_ge(f_step, nq * FSTEP + FSTEP + 1)
                        for c in range(FC):
                            ins = pe.matmul(pO[:, 0, 2 * c:2 * c + 2], qT[:, c], nk2[:], start=True, stop=True)
                        ins.then_inc(null_done, 1)
                        logits(nq + 1)

                    def keys(b, qt, kt, nq, nk):
                        pe.wait_ge(staged, nk * 2 + 2)
                        for h in range(H):
                            at = (h % 2) * DH
                            ins = pe.matmul(pS[:, 2 * (h // 8) + h % 2, (h % 8 // 2) * P:(h % 8 // 2 + 1) * P],
                                            qT[at:at + DH, h // 2], kblk[at:at + DH, :], start=True, stop=True)
                            if h % 8 >= 6:
                                ins.then_inc(s_done, 1)

                        def turn(g):
                            pe.wait_ge(p_ready, nk * 16 + 4 * g + 4)
                            if g == 0:
                                pe.wait_ge(q_done, nq + 2)
                            if g >= 2:
                                pe.wait_ge(pt_ready, nk * 4 + g - 1)
                            for i, h in enumerate(heads(g)):
                                ins = pe.transpose(pT[:, g % 2, i * P:(i + 1) * P], sc[:, h], ident[:])
                            ins.then_inc(t_done, 1)

                        def weigh(g):
                            pe.wait_ge(pt_ready, nk * 4 + g + 1)
                            for i, h in enumerate(heads(g)):
                                ins = pe.matmul(pO[:, h // 8, (h % 8) * DH:(h % 8 + 1) * DH], PT[:, g % 2, i], vblk[:],
                                                start=True, stop=True)
                            ins.then_inc(pv_done, 1)

                        turn(0)
                        for g in range(1, 4):
                            turn(g)
                            weigh(g - 1)
                        weigh(3)

                    tiles = live_tiles(pe, "pe_att", queries, keys, lambda b, qt, nq, nk: project(nq + 1))
                    logits(pe.snap(tiles) + 1)

                @block.scalar
                def _(act):
                    last = act.alloc_register("act_last")
                    act.reg_mov(last, T)

                    def roots(n):
                        for m, at in enumerate((9, 22)):
                            act.wait_ge(f_step, n * FSTEP + at)
                            act.activation(mv[:, 6:7], mv[:, 5:6], ACT.Sqrt).then_inc(f_root, 1)

                    def columns(n):
                        act.wait_ge(row_turned, n + 1)
                        act.activation(col[:].rearrange("p k t -> p (k t)"), pT[:, 0, 0:D], ACT.Copy).then_inc(col_ready, 1)

                    def rows_out(n, to, rows):
                        act.wait_ge(f_step, n * FSTEP + FSTEP)
                        act.dma_start(to, rows).then_inc(row_out, 16)

                    roots(0)
                    columns(0)
                    rows_out(0, table[0:B * N, 0:D].rearrange("(t p) d -> p t d", p=P), repeat(row[:], T))

                    def queries(b, qt, nq):
                        roots(nq + 1)
                        act.wait_ge(q_proj, nq + 1)
                        for g in range(2):
                            act.activation(qT[:, 4 * g:4 * g + 4].rearrange("p c q -> p (c q)"), pT[:, g], ACT.Copy,
                                           scale=DH ** -0.5).then_inc(q_ready, 1)
                        columns(nq + 1)
                        rows_out(nq + 1, table[ds(act.snap(last) * P, P), 0:D], row[:])

                    def keys(b, qt, kt, nq, nk):
                        def exps(g):
                            act.wait_ge(k_step, done(nk * KSTEP + NEGATED[g]))
                            for h in heads(g):
                                act.activation(sc[:, h], sc[:, h], ACT.Exp, bias=st[:, NEG, h:h + 1],
                                               accum_out=st[:, RS, h:h + 1]).then_inc(p_ready, 1)

                        def keep(g):
                            act.wait_ge(t_done, nk * 4 + g + 1)
                            if g >= 2:
                                act.wait_ge(pv_done, done(nk * 4 + g - 1))
                            act.activation(PT[:, g % 2].rearrange("p h q -> p (h q)"), pT[:, g % 2], ACT.Copy).then_inc(pt_ready, 1)

                        exps(0)
                        for g in range(1, 4):
                            exps(g)
                            keep(g - 1)
                        act.activation(st[:, ALPHA], st[:, DIF], ACT.Exp).then_inc(alpha_ready, 1)
                        keep(3)

                    def after(b, qt, nq, nk):
                        act.wait_ge(ot_done, nq * 2 + 4)
                        act.activation(OT[:, FC // 2:FC].rearrange("p c q -> p (c q)"), pT[:, 1], ACT.Copy).then_inc(ot_high, 1)
                        act.reg_mov(last, b * QT + qt)

                    tiles = act.snap(live_tiles(act, "act_att", queries, keys, after))
                    roots(tiles + 1)
                    columns(tiles + 1)
                    rows_out(tiles + 1, table[ds(act.snap(last) * P, P), 0:D], row[:])
                    act.wait_ge(row_out, done(16 * (tiles + 2)))
                    act.activation(held[:, 0:1], ones[:, 0:1], ACT.Copy)

                @block.vector
                def _(dve):
                    def moments_of(at, rows):
                        dve.bn_stats(st6[:], rows).then_inc(f_step, 1)
                        dve.wait_ge(f_step, at + 1)
                        dve.tensor_tensor(mv[:, 1:2], st6[:, 1:2], st6[:, 4:5], ALU.add).then_inc(f_step, 1)
                        dve.tensor_tensor(mv[:, 2:3], st6[:, 1:2], st6[:, 4:5], ALU.subtract).then_inc(f_step, 1)
                        dve.tensor_tensor(mv[:, 4:5], st6[:, 2:3], st6[:, 5:6], ALU.add).then_inc(f_step, 1)
                        dve.wait_ge(f_step, at + 4)
                        dve.tensor_scalar(mv[:, 0:1], mv[:, 1:2], 0.5, None, ALU.mult).then_inc(f_step, 1)
                        dve.tensor_tensor(mv[:, 3:4], mv[:, 2:3], mv[:, 2:3], ALU.mult).then_inc(f_step, 1)
                        dve.tensor_scalar(mv[:, 5:6], mv[:, 4:5], 1.0 / D, EPS, ALU.mult, ALU.add).then_inc(f_step, 1)
                        dve.wait_ge(f_step, at + 7)

                    last = dve.alloc_register("dve_last")
                    dve.reg_mov(last, T)

                    def turned(n):
                        dve.wait_ge(ot_done, 2 * n + 1)
                        dve.tensor_copy(OT[:, 0:FC // 2].rearrange("p c q -> p (c q)"), pT[:, 0]).then_inc(ot_ready, 1)

                    def norms(n, heads_done, keep):
                        at = n * FSTEP
                        dve.wait_ge(o_proj, heads_done)
                        dve.tensor_copy(yr[:], pO[:, 0, 0:D]).then_inc(f_step, 1)
                        dve.wait_ge(f_step, at + 1)
                        moments_of(at + 1, yr[:])
                        dve.scalar_tensor_tensor(mv[:, 5:6], mv[:, 3:4], 0.25, mv[:, 5:6], ALU.mult, ALU.add).then_inc(f_step, 1)
                        dve.wait_ge(f_root, n * 2 + 1)
                        dve.reciprocal(mv[:, 7:8], mv[:, 6:7]).then_inc(f_step, 1)
                        dve.wait_ge(f_step, at + 10)
                        dve.tensor_scalar(yr[:], yr[:], mv[:, 0:1], mv[:, 7:8], ALU.subtract, ALU.mult).then_inc(f_step, 1)
                        dve.wait_ge(f_step, at + 11)
                        dve.tensor_tensor(yr[:], yr[:], go_b[:], ALU.mult).then_inc(f_step, 1)
                        dve.wait_ge(f_step, at + 12)
                        moments_of(at + 12, yr[:])
                        dve.tensor_tensor(mv[:, 4:5], mv[:, 0:1], mv[:, 0:1], ALU.mult).then_inc(f_step, 1)
                        dve.scalar_tensor_tensor(mv[:, 5:6], mv[:, 3:4], 0.25, mv[:, 5:6], ALU.mult, ALU.add).then_inc(f_step, 1)
                        dve.wait_ge(f_step, at + 21)
                        dve.tensor_tensor(mv[:, 5:6], mv[:, 5:6], mv[:, 4:5], ALU.add).then_inc(f_step, 1)
                        dve.wait_ge(f_root, n * 2 + 2)
                        dve.reciprocal(mv[:, 7:8], mv[:, 6:7]).then_inc(f_step, 1)
                        dve.wait_ge(f_step, at + 23)
                        dve.wait_ge(row_out, done(n * 16))
                        dve.scalar_tensor_tensor(row[:], yr[:], mv[:, 7:8], nw_b[:], ALU.mult, ALU.mult).then_inc(f_step, 1)
                        dve.wait_ge(lg_done, n + 1)
                        dve.tensor_tensor(lgr[:], pT[:, 1, 0:E0], rb_b[:], ALU.add).then_inc(lg_row, 1)
                        dve.wait_ge(lg_row, n + 1)
                        dve.wait_ge(lt_done, n + 1)
                        keep()

                    dve.tensor_copy(pO[:, 0, 0:D], unseen[:]).then_inc(o_proj, 1)

                    def keep_dead():
                        dve.tensor_copy(lg[:], repeat(lgr[:], T)).then_inc(lt_kept, 1)
                        dve.tensor_copy(LT[:].rearrange("e (t p) -> e t p", p=P), repeat(pT[0:E0, 0, 0:P], T)).then_inc(q_done, 1)
                        dve.wait_ge(lt_kept, 1)
                        dve.wait_ge(q_done, 1)
                    norms(0, 1, keep_dead)

                    def keep():
                        tile = dve.snap(last)
                        dve.tensor_scalar(lg_all[:, ds(tile, 1)].rearrange("p a e -> p (a e)"), lgr[:], 1.0, None,
                                          ALU.mult).then_inc(lt_kept, 1)
                        dve.tensor_scalar(LT_all[:, ds(tile * P, P)], pT[0:E0, 0, 0:P], 1.0, None,
                                          ALU.mult).then_inc(q_done, 1)

                    def queries(b, qt, nq):
                        norms(nq + 1, nq + 1, keep)
                        dve.wait_ge(null_done, nq + 1)
                        dve.tensor_tensor(st[:, MAX], pO[:, 0, 0:H], nullb[:], ALU.add).then_inc(q_step, 1)
                        dve.memset(st[:, LEN], 1.0).then_inc(q_step, 1)
                        dve.tensor_copy(O[:], repeat(nv[:], H)).then_inc(q_step, 1)

                    def keys(b, qt, kt, nq, nk):
                        at = nk * KSTEP
                        dve.wait_ge(q_step, nq * QSTEP + 3)
                        dve.wait_ge(k_done, done(nk * 2))
                        dve.wait_ge(k_step, done(at))
                        mine = [[by_bank(st[:, n], g) for n in range(8)] for g in range(4)]

                        def put(step, ins):
                            ins.then_inc(k_step, 1)

                        def add(g):
                            dve.wait_ge(bias_ready, done(nk * 4 + g + 1))
                            dve.wait_ge(s_done, nk * 4 + g + 1)
                            dve.tensor_tensor(by_bank(sc[:], g), pS[:, g].rearrange("p (i k) -> p i k", k=P),
                                              by_bank(bias_sb[:, ds(nk % 2, 1)].rearrange("p a h k -> p (a h) k"), g),
                                              ALU.add).then_inc(sc_ready, 1)

                        def largest(g, step):
                            dve.wait_ge(sc_ready, done(nk * 4 + g + 5))
                            put(step, dve.tensor_reduce(mine[g][TMAX], by_bank(sc[:], g), AX, ALU.max))

                        def joined(g, step, wait):
                            dve.wait_ge(k_step, done(at + wait))
                            put(step, dve.tensor_tensor(mine[g][TMAX], mine[g][TMAX], mine[g][MAX], ALU.max))

                        def shifts(g, step, wait):
                            dve.wait_ge(k_step, done(at + wait))
                            put(step, dve.tensor_tensor(mine[g][DIF], mine[g][MAX], mine[g][TMAX], ALU.subtract))
                            put(step + 1, dve.tensor_scalar(mine[g][NEG], mine[g][TMAX], -1.0, None, ALU.mult))

                        add(0)
                        largest(0, 1)
                        add(1)
                        joined(0, 2, 1)
                        largest(1, 3)
                        shifts(0, 4, 2)
                        add(2)
                        joined(1, 6, 3)
                        largest(2, 7)
                        shifts(1, 8, 6)
                        add(3)
                        joined(2, 10, 7)
                        largest(3, 11)
                        shifts(2, 12, 10)
                        joined(3, 14, 11)
                        shifts(3, 15, 14)
                        dve.wait_ge(k_step, done(at + 16))
                        put(17, dve.tensor_copy(st[:, MAX], st[:, TMAX]))
                        dve.wait_ge(alpha_ready, nk + 1)
                        put(18, dve.tensor_tensor(O[:], O[:], bcast(st[:, ALPHA], DH), ALU.mult))
                        put(19, dve.tensor_tensor(st[:, LEN], st[:, LEN], st[:, ALPHA], ALU.mult))
                        dve.wait_ge(k_step, done(at + 19))
                        put(20, dve.tensor_tensor(st[:, LEN], st[:, LEN], st[:, RS], ALU.add))
                        for half in range(2):
                            dve.wait_ge(pv_done, done(nk * 4 + 2 * half + 2))
                            mine = O[:, 8 * half:8 * half + 8].rearrange("p h d -> p (h d)")
                            dve.tensor_tensor(mine, mine, pO[:, half], ALU.add).then_inc(k_done, 1)

                    def after(b, qt, nq, nk):
                        dve.wait_ge(k_done, done(nk * 2))
                        dve.wait_ge(k_step, done(nk * KSTEP))
                        dve.reciprocal(st[:, RL], st[:, LEN]).then_inc(q_step, 1)
                        dve.wait_ge(q_step, nq * QSTEP + 4)
                        dve.tensor_tensor(O[:], O[:], bcast(st[:, RL], DH), ALU.mult).then_inc(o_ready, 1)
                        turned(nq + 1)
                        dve.reg_mov(last, b * QT + qt)

                    tiles = dve.snap(live_tiles(dve, "dve_att", queries, keys, after))
                    norms(tiles + 1, tiles + 1, keep)
        if upto == "att":
            return

        att.close()

        with ExitStack() as picked:
            b1_sb = sb("b1_sb", [P, E0, FC], into=picked)
            b2_sb = sb("b2_sb", [P, E0, D], into=picked)
            with ExitStack() as ph:
                top = sb("top", [P, 2, T], into=ph)
                chunk = sb("chunk", [P, 2, CW], into=ph)
                best = sb("best", [P, CAP], into=ph)
                pick = sb("pick", [P, CAP], U32, into=ph)
                pickf = sb("pickf", [P, CAP], into=ph)
                lists = sb("lists", [E0, CPE, CAP], into=ph)
                merge = sb("merge", [E0, 2, CPE // 2, CAP], into=ph)
                least = sb("least", [E0, 1], into=ph)
                lowest = sb("lowest", [P, 1], into=ph)
                test = sb("test", [P, 2, CAP], into=ph)
                num = sb("num", [P, 8], into=ph)
                GREATER, EQUAL, LEFT, TAKEN, FIRST, BASE = range(6)
                place = sb("place", [P, 3, CAP], into=ph)
                hot = sb("hot", [P, E0, CAP], into=ph)
                pickT = sb("pickT", [P, P], into=ph)
                mineT = sb("mineT", [P, P], into=ph)
                same = sb("same", [P, P], into=ph)
                earlier = sb("earlier", [P, P], into=ph)
                spread = sb("spread", [E0, P], into=ph)
                slots = sb("slots", [P, CAP], into=ph)
                rank = sb("rank", [P, 1], into=ph)
                pr = ps("c_pr", [P, 4, 512], ph)
                pv = ps("c_pv", [P, 512], ph)
                pn = ps("c_pn", [P, 512], ph)
                soft, soft_exp, gates_out, step, e_in, chunk_in, lists_in, pe_step, c_step = [
                    sem(n) for n in ("soft", "soft_exp", "gates_out", "pick_step", "e_in", "chunk_in", "lists_in",
                                     "pe_step", "c_step")]
                SORTED = 3 * CAP // 8
                table_steps = []
                with nc.Block() as block:
                    @block.sync
                    def _(sp):
                        sp.dma_start(chunk[:, 0], LT[:].rearrange("e (c k) -> e c k", c=CPE)).then_inc(chunk_in, 16)
                        sp.dma_start(b1_sb[:], b1).then_inc(e_in, 16)
                        sp.dma_start(b2_sb[:].rearrange("p e d -> p (e d)"), b2.partition_broadcast(P)).then_inc(e_in, 16)
                        sp.wait_ge(soft, 5)
                        sp.dma_start(table[0:B * N, D:ROW].rearrange("(t p) e -> p t e", p=P), lg[:]).then_inc(gates_out, 16)
                        sp.wait_ge(step, SORTED)
                        sp.dma_start(lists[:], best[:]).then_inc(lists_in, 16)
                        sp.wait_ge(lists_in, 16)
                        sp.wait_ge(gates_out, 16)
                        sp.wait_ge(e_in, 32)

                    @block.gpsimd
                    def _(pool):
                        pool.memset(spread[:], 0.0).then_inc(c_step, 1)
                        pool.affine_select(out=same[:].rearrange("p (e c) -> p e c", c=CPE), in_=ones[:].rearrange("p (e c) -> p e c", c=CPE),
                                           compare_op=ALU.is_ge, fill=0.0, base=0, pattern=[[-CPE, E0], [0, CPE]],
                                           channel_multiplier=1).then_inc(c_step, 1)
                        pool.wait_ge(c_step, 2)
                        pool.affine_select(out=same[:].rearrange("p (e c) -> p e c", c=CPE), in_=same[:].rearrange("p (e c) -> p e c", c=CPE),
                                           compare_op=ALU.is_ge, fill=0.0, base=CPE - 1, pattern=[[CPE, E0], [0, CPE]],
                                           channel_multiplier=-1).then_inc(c_step, 1)
                        pool.affine_select(out=spread[:].rearrange("p (e c) -> p e c", c=CPE), in_=spread[:].rearrange("p (e c) -> p e c", c=CPE),
                                           compare_op=ALU.not_equal, fill=1.0, base=0, pattern=[[-1, E0], [0, CPE]],
                                           channel_multiplier=1).then_inc(c_step, 1)
                        pool.wait_ge(c_step, 3)
                        pool.affine_select(out=earlier[:], in_=same[:], compare_op=ALU.is_ge, fill=0.0, base=-1,
                                           pattern=[[1, P]], channel_multiplier=-1).then_inc(c_step, 1)
                        pool.iota(slots[:], pattern=[[1, CAP]], base=0, channel_multiplier=0,
                                  allow_small_or_imprecise_dtypes=True).then_inc(c_step, 1)
                        pool.iota(rank[:], pattern=[[0, 1]], base=0, channel_multiplier=1,
                                  allow_small_or_imprecise_dtypes=True).then_inc(c_step, 1)

                    @block.vector
                    def _(dve):
                        dve.tensor_reduce(top[:, 0], lg[:], AX, ALU.max).then_inc(soft, 1)
                        dve.wait_ge(soft, 1)
                        dve.tensor_tensor(lg[:], lg[:], bcast(top[:, 0], E0), ALU.subtract).then_inc(soft, 1)
                        dve.wait_ge(soft_exp, 1)
                        dve.tensor_reduce(top[:, 0], lg[:], AX, ALU.add).then_inc(soft, 1)
                        dve.wait_ge(soft, 3)
                        dve.reciprocal(top[:, 1], top[:, 0]).then_inc(soft, 1)
                        dve.wait_ge(soft, 4)
                        dve.tensor_tensor(lg[:], lg[:], bcast(top[:, 1], E0), ALU.mult).then_inc(soft, 1)
                        steps = [0]

                        def put(ins):
                            steps[0] += 1
                            ins.then_inc(step, 1)

                        def link(ins):
                            put(ins)
                            dve.wait_ge(step, steps[0])

                        dve.wait_ge(chunk_in, 16)
                        for r in range(CAP // 8):
                            now = slice(8 * r, 8 * r + 8)
                            at, other = chunk[:, r % 2], chunk[:, 1 - r % 2]
                            link(dve.max(best[:, now], at))
                            put(dve.max_index(pick[:, now], best[:, now], at))
                            link(dve.match_replace(other, best[:, now], at, -3e38))
                        dve.wait_ge(lists_in, 16)
                        left, many = lists[:], CPE
                        while many > 1:
                            many //= 2
                            pairs = left.rearrange("e (j r) k -> e j r k", r=2)
                            out_at = merge[:, 0, 0:many]
                            link(dve.tensor_tensor(out_at, pairs[:, :, 0], pairs[:, :, 1, ::-1], ALU.max))
                            side, w = 0, CAP // 2
                            while w and many > 1:
                                view = [merge[:, n, 0:many].rearrange("e j (b r w) -> e (j b) r w", r=2, w=w) for n in (side, 1 - side)]
                                put(dve.tensor_tensor(view[1][:, :, 0], view[0][:, :, 0], view[0][:, :, 1], ALU.max))
                                link(dve.tensor_tensor(view[1][:, :, 1], view[0][:, :, 0], view[0][:, :, 1], ALU.min))
                                side, w = 1 - side, w // 2
                            left = merge[:, side, 0:many]
                        link(dve.tensor_reduce(least[:], merge[:, 0, 0], AX, ALU.min))
                        table_steps.append(steps[0])
                        put(dve.tensor_copy(pickf[:], pick[:]))
                        dve.wait_ge(pe_step, 1)
                        link(dve.tensor_copy(lowest[:], pn[:, 0:1]))
                        link(dve.tensor_scalar(num[:, BASE:BASE + 1], pn[:, 1:2], float(CW), None, ALU.mult))
                        put(dve.tensor_scalar(test[:, 0], best[:], lowest[:, 0:1], None, ALU.is_gt))
                        link(dve.tensor_scalar(test[:, 1], best[:], lowest[:, 0:1], None, ALU.is_equal))
                        link(dve.tensor_reduce(num[:, GREATER:EQUAL + 1], test[:], AX, ALU.add))
                        table_steps.append(steps[0])
                        link(dve.tensor_scalar(pickf[:], pickf[:], num[:, BASE:BASE + 1], None, ALU.add))
                        table_steps.append(steps[0])
                        dve.wait_ge(pe_step, 2)
                        link(dve.tensor_scalar(num[:, LEFT:LEFT + 1], pn[:, 2:3], -1.0, float(CAP), ALU.mult, ALU.add))
                        link(dve.tensor_tensor(num[:, LEFT:LEFT + 1], num[:, LEFT:LEFT + 1], pn[:, 3:4], ALU.subtract))
                        link(dve.tensor_scalar(num[:, LEFT:LEFT + 1], num[:, LEFT:LEFT + 1], 0.0, None, ALU.max))
                        link(dve.tensor_tensor(num[:, LEFT:LEFT + 1], num[:, LEFT:LEFT + 1], num[:, EQUAL:EQUAL + 1], ALU.min))
                        link(dve.tensor_tensor(num[:, TAKEN:TAKEN + 1], num[:, LEFT:LEFT + 1], num[:, GREATER:GREATER + 1], ALU.add))
                        table_steps.append(steps[0])
                        dve.wait_ge(c_step, 7)
                        dve.wait_ge(pe_step, 3)
                        link(dve.tensor_copy(num[:, FIRST:FIRST + 1], pn[:, 4:5]))
                        link(dve.tensor_scalar(place[:, 0], slots[:], num[:, FIRST:FIRST + 1], None, ALU.subtract))
                        link(dve.tensor_scalar(place[:, 1], place[:, 0], num[:, TAKEN:TAKEN + 1], None, ALU.is_lt))
                        link(dve.scalar_tensor_tensor(place[:, 1], place[:, 0], 0.0, place[:, 1], ALU.is_ge, ALU.mult))
                        link(dve.tensor_tensor(place[:, 2], place[:, 0], place[:, 1], ALU.mult))
                        table_steps.append(steps[0])
                        dve.wait_ge(pe_step, 4)
                        put(dve.tensor_copy(pickT[:], pv[:, P:2 * P]))
                        link(dve.tensor_copy(mineT[:], pv[:, 2 * P:3 * P]))
                        for q in range(4):
                            dve.wait_ge(pe_step, 5 + q)
                            link(dve.tensor_scalar(hot[:, 4 * q:4 * q + 4].rearrange("p e s -> p (e s)"), pr[:, q], rank[:, 0:1],
                                                   None, ALU.is_equal))
                        table_steps.append(steps[0])
                        put(dve.memset(idx[:], 0))
                        dve.wait_ge(pe_step, 9)
                        link(dve.tensor_tensor(mineT[:], mineT[:], pv[:, 0:P], ALU.mult))
                        link(dve.tensor_reduce(top[:, 0], mineT[:].rearrange("p (e c) -> p e c", c=CPE), AX, ALU.add))
                        link(dve.tensor_copy(idx[:, 0:E0], top[:, 0]))

                    @block.scalar
                    def _(act):
                        act.wait_ge(soft, 2)
                        act.activation(lg[:], lg[:], ACT.Exp).then_inc(soft_exp, 1)

                    @block.tensor
                    def _(pe):
                        least_set, counted_at, pickf_set, taken_at, placed, hot_set = table_steps
                        pe.wait_ge(c_step, 7)
                        pe.matmul(pn[:, 1:2], earlier[:], ones[:, 0:1], start=True, stop=True)
                        pe.wait_ge(step, least_set)
                        pe.matmul(pn[:, 0:1], spread[:], least[:], start=True, stop=True).then_inc(pe_step, 1)
                        pe.wait_ge(step, counted_at)
                        pe.matmul(pn[:, 2:3], same[:], num[:, GREATER:GREATER + 1], start=True, stop=True)
                        pe.matmul(pn[:, 3:4], earlier[:], num[:, EQUAL:EQUAL + 1], start=True, stop=True).then_inc(pe_step, 1)
                        pe.wait_ge(step, taken_at)
                        pe.matmul(pn[:, 4:5], earlier[:], num[:, TAKEN:TAKEN + 1], start=True, stop=True).then_inc(pe_step, 1)
                        pe.transpose(pv[:, P:2 * P], pickf[:], ident[:])
                        pe.wait_ge(step, placed)
                        pe.transpose(pv[:, 2 * P:3 * P], place[:, 1], ident[:]).then_inc(pe_step, 1)
                        for e in range(E0):
                            ins = pe.matmul(pr[:, e // 4, (e % 4) * P:(e % 4 + 1) * P], same[:, CPE * e:CPE * e + 1].to_broadcast([P, P]),
                                            place[:, 2], start=True, stop=True)
                            if e % 4 == 3:
                                ins.then_inc(pe_step, 1)
                        for e in range(E0):
                            if e % 4 == 0:
                                pe.wait_ge(step, hot_set - 3 + e // 4)
                            ins = pe.matmul(pv[:, CPE * e:CPE * e + CPE], hot[:, e], pickT[:, CPE * e:CPE * e + CPE],
                                            start=True, stop=True)
                        ins.then_inc(pe_step, 1)
            if upto == "route0":
                return

            def expert_phase(tag, src, width, dst, out_width, gidx, sidx, gates, from_row, b1t, b2t, w1t, w2t,
                             experts, act_fn, counts):
                with ExitStack() as ph:
                    G = sb(tag + "G", [P, width + 1], into=ph)
                    XT = sb(tag + "XT", [P, KD, P], into=ph)
                    hT = sb(tag + "hT", [P, FC, P], into=ph)
                    yt = sb(tag + "yt", [P, D], into=ph)
                    yg = sb(tag + "yg", [P, out_width], into=ph)
                    pX = ps(tag + "pX", [P, 512], ph)
                    pH = ps(tag + "pH", [P, 2, 512], ph)
                    pY = ps(tag + "pY", [P, 512], ph)
                    names = ("gathered", "turned", "xt_ready", "fc1_done", "gelu_done", "fc2_done", "y_read", "yg_ready",
                             "scattered", "gi_set", "si_set", "spare_set")
                    (gathered, turned, xt_ready, fc1_done, gelu_done, fc2_done, y_read, yg_ready, scattered, gi_set,
                     si_set, spare_set) = [sem(f"{tag}_{n}") for n in names]

                    def per_block(eng, name, body, begin=None):
                        if counts is None:
                            with eng.Fori(0, experts // RING) as r:
                                for u in range(RING):
                                    if begin:
                                        begin(r, RING * r + u, u)
                                    body(RING * r + u, RING * r + u, u)
                            return
                        nblk, _ = counts
                        reg = eng.alloc_register(f"{tag}_{name}")
                        eng.reg_mov(reg, 0)
                        with eng.Fori(0, experts // RING) as r:
                            for u in range(RING):
                                e = RING * r + u
                                if begin:
                                    begin(r, e, u)
                                n = eng.value_load(nblk[0:1, ds(e, 1)], min_val=0, max_val=B * N // P)
                                with eng.If(n > 0):
                                    with eng.Fori(0, n):
                                        body(eng.snap(reg), e, u)
                                        eng.reg_add(reg, reg, 1)

                    with nc.Block() as block:
                        @block.sync
                        def _(sp):
                            for s in (fc2_done, y_read, yg_ready):
                                sp.sem_inc(s, 1)
                            with sp.Fori(0, experts // RING - 1) as r:
                                for u in range(RING):
                                    if counts is None:
                                        sp.wait_ge(fc2_done, done(RING * r + u + 1))
                                    else:
                                        end = sp.value_load(counts[1][0:1, ds(RING * r + u, 1)], min_val=0, max_val=BLK)
                                        sp.wait_ge(fc2_done, done(end))
                                    load_expert_at(sp, w1t, w2t, RING * r + u + RING, u)

                        @block.gpsimd
                        def _(pool):
                            def gather(j, n):
                                pool.tensor_copy(gi[:], gidx[:, ds(j, 1)] if not isinstance(j, int) else gidx[:, j:j + 1]).then_inc(gi_set, 1)
                                pool.wait_ge(gi_set, j + 1)
                                held_here(pool, 0)
                                pool.indirect_dma_start(G[:, 0:width], None, src, bass.IndirectOffsetOnAxis(ap=gi[:], axis=0)).then_inc(gathered, 16)

                            gather(0, 0)
                            pool.dma_start(held[:, 1:2], ones[:, 0:1]).then_inc(scattered, 16)
                            pool.wait_ge(scattered, 16)
                            pool.wait_ge(turned, 1)
                            pool.wait_ge(xt_ready, 1)
                            pool.wait_ge(gathered, 16)
                            gather(1, 1)

                            def body(j, e, u):
                                pool.wait_ge(turned, j + 2)
                                pool.wait_ge(xt_ready, j + 2)
                                pool.wait_ge(gathered, j * 16 + 32)
                                held_here(pool, 1)
                                gather(j + 2, 2)
                                pool.wait_ge(scattered, j * 16 + 16)
                                held_here(pool, 2)
                                pool.tensor_copy(si[:], sidx[:, ds(j, 1)]).then_inc(si_set, 1)
                                pool.wait_ge(yg_ready, done(j + 1))
                                pool.wait_ge(si_set, j + 1)
                                held_here(pool, 3)
                                pool.indirect_dma_start(dst, bass.IndirectOffsetOnAxis(ap=si[:], axis=0), yg[:], None,
                                                        compute_op=ALU.add).then_inc(scattered, 16)
                            per_block(pool, "pool", body)

                        @block.tensor
                        def _(pe):
                            def turn(j):
                                pe.wait_ge(gathered, j * 16 + 16)
                                for k in range(KD):
                                    ins = pe.transpose(pX[:, k * P:(k + 1) * P], G[:, k * P:(k + 1) * P], ident[:])
                                ins.then_inc(turned, 1)

                            turn(0)

                            def begin(r, e, u):
                                pe.wait_ge(w_in[u], r * 32 + (w_round[0] + 1) * 32)

                            def body(j, e, u):
                                pe.wait_ge(xt_ready, j + 1)
                                for c in range(FC):
                                    for k in range(KD):
                                        ins = pe.matmul(pH[:, c // 4, (c % 4) * P:(c % 4 + 1) * P], w1_sb[:, u, k, c * P:(c + 1) * P],
                                                        XT[:, k], start=(k == 0), stop=(k == KD - 1))
                                    if c % 4 == 3:
                                        ins.then_inc(fc1_done, 1)
                                turn(j + 1)
                                pe.wait_ge(y_read, done(j))
                                for c in range(FC):
                                    pe.wait_ge(gelu_done, j * FC + c + 1)
                                    ins = pe.matmul(pY[:, 0:D], hT[:, c], w2_sb[:, u, c], start=(c == 0), stop=(c == FC - 1))
                                ins.then_inc(fc2_done, 1)
                            per_block(pe, "pe", body, begin)

                        @block.scalar
                        def _(act):
                            def body(j, e, u):
                                act.wait_ge(fc2_done, done(j))
                                for c in range(FC):
                                    if c % 4 == 0:
                                        act.wait_ge(fc1_done, j * 2 + c // 4 + 1)
                                    act.activation(hT[:, c], pH[:, c // 4, (c % 4) * P:(c % 4 + 1) * P], act_fn,
                                                   bias=b1t[:, ds(e, 1), c]).then_inc(gelu_done, 1)
                            per_block(act, "act", body)

                        @block.vector
                        def _(dve):
                            def column(j):
                                dve.wait_ge(turned, j + 1)
                                if from_row:
                                    dve.tensor_scalar(gates[:, ds(j, 1)] if not isinstance(j, int) else gates[:, 0:1],
                                                      G[:, ds(D + j, 1)] if not isinstance(j, int) else G[:, D:D + 1],
                                                      1.0, None, ALU.mult)
                                dve.tensor_copy(XT[:].rearrange("p k t -> p (k t)"), pX[:, 0:D]).then_inc(xt_ready, 1)

                            dve.memset(G[:, width:width + 1], 0.0).then_inc(spare_set, 1)
                            dve.wait_ge(spare_set, 1)
                            column(0)

                            def body(j, e, u):
                                dve.wait_ge(fc1_done, j * 2 + 2)
                                column(j + 1)
                                dve.wait_ge(fc2_done, done(j + 1))
                                dve.wait_ge(yg_ready, done(j))
                                dve.tensor_tensor(yt[:], pY[:, 0:D], b2t[:, ds(e, 1)].rearrange("p a d -> p (a d)"), ALU.add).then_inc(y_read, 1)
                                dve.wait_ge(y_read, done(j + 1))
                                dve.wait_ge(scattered, j * 16 + 16)
                                gate = gates[:, ds(j, 1)]
                                if out_width > D:
                                    dve.tensor_scalar(yg[:, D:D + 1], gate, 1.0, None, ALU.mult)
                                dve.tensor_scalar(yg[:, 0:D], yt[:], gate, None, ALU.mult).then_inc(yg_ready, 1)
                            per_block(dve, "dve", body)

                    return gathered, scattered

            w_round = [0]
            expert_phase("m", table[0:B * N, :], ROW, acc0, D + 1, idx, idx, gtab, True, b1_sb, b2_sb, w1, w2,
                         E0, ACT.Gelu, None)
        if upto == "moe0":
            return

        mid.close()

        late = ctx.enter_context(ExitStack())
        xc = sb("xc", [P, T, D], into=late)
        W = sb("W", [P, T, EG], into=late)
        lg = sb("lg2", [P, T, E1], into=late)
        oh = sb("oh", [P, 2, T, E1], into=late)
        best2 = sb("best2", [P, 2, T], into=late)
        red = sb("red", [P, 2, T], into=late)
        scr = sb("scr", [P, T, E1], into=late)
        rev = sb("rev", [P, E1], into=late)
        c1_sb = sb("c1_sb", [P, E1, FC], into=late)
        c2_sb = sb("c2_sb", [P, E1, D], into=late)
        zpad = sb("zpad", [P, D], into=late)
        late_const = sem("late_const")
        c_late = sem("c_late")
        acc1_set = sem("acc1_set")
        x_high, x_split, x_kept = sem("x_high"), sem("x_split"), sem("x_kept")

        def softmax(dve, link, link_exp):
            link(dve.tensor_reduce(red[:, 0], lg[:], AX, ALU.max))
            link(dve.tensor_tensor(lg[:], lg[:], bcast(red[:, 0], E1), ALU.subtract))
            link_exp()
            link(dve.tensor_reduce(red[:, 0], lg[:], AX, ALU.add))
            link(dve.reciprocal(red[:, 1], red[:, 0]))
            link(dve.tensor_tensor(lg[:], lg[:], bcast(red[:, 1], E1), ALU.mult))

        def top_two(dve, link):
            for n in range(2):
                link(dve.tensor_reduce(best2[:, n], lg[:], AX, ALU.max))
                link(dve.tensor_tensor(scr[:], lg[:], bcast(best2[:, n], E1), ALU.is_equal))
                link(dve.tensor_tensor(scr[:], scr[:], repeat(rev[:], T), ALU.mult))
                link(dve.tensor_reduce(red[:, 0], scr[:], AX, ALU.max))
                link(dve.tensor_tensor(oh[:, n], scr[:], bcast(red[:, 0], E1), ALU.is_equal))
                if n == 0:
                    link(dve.scalar_tensor_tensor(lg[:], oh[:, 0], -4.0, lg[:], ALU.mult, ALU.add))

        x1T = sb("x1T", [P, KD, B * N], into=late)
        xparts = sb("xparts", [P, 2, KD, B * N], F32R, into=late)
        NCH, CH = 4, 512
        STEPS = EG * NCH
        TC = CH // P

        def upper_bits(eng, part, whole):
            return eng.tensor_scalar(part.bitcast(I32), whole.bitcast(I32), HIGH, None, ALU.bitwise_and)

        gw = sb("gw", [P, 2, KD, M1], into=late)
        uw = sb("uw", [P, 2, KD, M1], into=late)
        dw = sb("dw", [P, 2, D], into=late)
        cw_in = [sem(f"cw_in{u}") for u in range(2)]

        def load_gated(eng, e, u):
            one = ds(e, 1)
            eng.dma_start(gw[:, u], wgate[one].rearrange("a (k p) m -> p (a k) m", p=P)).then_inc(cw_in[u], 16)
            eng.dma_start(uw[:, u], wup[one].rearrange("a (k p) m -> p (a k) m", p=P)).then_inc(cw_in[u], 16)
            eng.dma_start(dw[:, u], wdown[one].rearrange("a p d -> p (a d)")).then_inc(cw_in[u], 16)

        class Logits:

            def __init__(self, tag, ph, rows, router, banks, cond_bias=None, shared=None):
                self.rows, self.router, self.cond_bias = rows, router, cond_bias
                self.lT = shared.lT if shared else sb(tag + "lT", [E1, 2, CH], into=ph)
                self.pt = shared.pt if shared else ps(tag + "pt", [P, 2, KD, 512], ph)
                self.pl, self.pb = banks[:, 0:2], banks[:, 2]
                self.row_ready, self.turned, self.low_ready, self.high_ready, self.lg_done, self.lt_ready, self.back = [
                    sem(tag + n) for n in ("row_ready", "turned", "low_ready", "high_ready", "lg_done", "lt_ready", "back")]

            def pe_logits(self, pe, c):
                pe.wait_ge(self.low_ready, c + 1)
                pe.wait_ge(self.high_ready, c + 1)
                for k in range(KD):
                    ins = pe.matmul(self.pl[0:E1, c % 2], self.router[:, k], x1T[:, k, c * CH:(c + 1) * CH],
                                    start=(k == 0), stop=(k == KD - 1))
                ins.then_inc(self.lg_done, 1)

            def pe_back(self, pe, c):
                pe.wait_ge(self.lt_ready, c + 1)
                for i in range(TC):
                    t = TC * c + i
                    ins = pe.transpose(self.pb[:, t * E1:(t + 1) * E1], self.lT[:, c % 2, i * P:(i + 1) * P],
                                       ident[0:E1, 0:E1])
                ins.then_inc(self.back, 1)

            def tensor(self, pe, rows_are, logits_may, back_may):
                for c in range(NCH):
                    rows_are(c)
                    if c >= 2:
                        pe.wait_ge(self.low_ready, c - 1)
                        pe.wait_ge(self.high_ready, c - 1)
                    for k in range(KD):
                        for i in range(TC):
                            ins = pe.transpose(self.pt[:, c % 2, k, i * P:(i + 1) * P],
                                               self.rows[:, TC * c + i, k * P:(k + 1) * P], ident[:])
                        ins.then_inc(self.turned, 1)
                    if c == 1:
                        logits_may()
                    if c >= 1:
                        self.pe_logits(pe, c - 1)
                    if c == 2:
                        back_may()
                    if c >= 2:
                        self.pe_back(pe, c - 2)
                self.pe_logits(pe, NCH - 1)
                self.pe_back(pe, NCH - 2)
                self.pe_back(pe, NCH - 1)

            def scalar(self, act, between=None):
                def keep(c):
                    act.wait_ge(self.lg_done, c + 1)
                    if c >= 2:
                        act.wait_ge(self.back, c - 1)
                    bias = 0.0 if self.cond_bias is None else self.cond_bias[:, c * CH // N:c * CH // N + 1]
                    act.activation(self.lT[:, c % 2], self.pl[0:E1, c % 2], ACT.Identity, bias=bias).then_inc(self.lt_ready, 1)

                for c in range(NCH):
                    act.wait_ge(self.turned, 2 * c + 1)
                    act.activation(x1T[:, 0, c * CH:(c + 1) * CH], self.pt[:, c % 2, 0], ACT.Copy).then_inc(self.low_ready, 1)
                    if c >= 1:
                        keep(c - 1)
                    if between:
                        between(c)
                keep(NCH - 1)

            def vector_half(self, dve, c):
                dve.wait_ge(self.turned, 2 * c + 2)
                dve.tensor_copy(x1T[:, 1, c * CH:(c + 1) * CH], self.pt[:, c % 2, 1]).then_inc(self.high_ready, 1)

        with ExitStack() as ph:
            sums = sb("sums", [P, T, D + 1], into=ph)
            den = sb("den", [P, 2, T], into=ph)
            wt_sb = sb("wt_sb", [P, KD, E1], into=ph)
            wg_sb = sb("wg_sb", [DH, E1], into=ph)
            cT = sb("cT", [DH, B], into=ph)
            cond_bias = sb("cond_bias", [E1, B], into=ph)
            xhigh = xc[:].rearrange("p t d -> p (t d)").rearrange("p (k n) -> p k n", k=KD)
            low_banks = ps("low_banks", [P, 4, 512], ph)
            route = Logits("f_", ph, x_sb, wt_sb, low_banks, cond_bias)
            wr_sb = sb("wr_sb", [P, KD, E1], into=ph)
            second = Logits("h_", ph, xc, wr_sb, low_banks, None, route)
            y_out = sem("y_out")
            pc = low_banks[:, 3]
            sums_in = [sem(f"f_sums_in{c}") for c in range(NCH)]
            f_in, f_step, cond_done, cond_kept, f_exp = [
                sem(f"f_{n}") for n in ("in", "step", "cond_done", "cond_kept", "exp")]

            high = sb("high", [P, 2, 2, KD, M1], into=ph)
            gparts = sb("gparts", [P, 2, 2, KD, M1], F32R, into=ph)
            uparts = sb("uparts", [P, 2, 2, KD, M1], F32R, into=ph)
            ga = sb("ga", [P, CH], into=ph)
            lk = sb("lk", [P, CH], into=ph)
            hid = sb("hid", [P, 2, CH], into=ph)
            pG, pU = route.pt[:, :, 0], route.pt[:, :, 1]
            pY = low_banks[:].rearrange("p (a b) n -> p a b n", a=2)
            w_high, w_split, w_kept, up_done, ga_ready, lk_ready, hid_ready, down_done, acc_done = [
                sem(f"d_{n}") for n in ("w_high", "w_split", "w_kept", "up_done", "ga_ready", "lk_ready",
                                        "hid_ready", "down_done", "acc_done")]

            def all_steps(eng, body):
                def pair(r, peeled):
                    for u in range(2):
                        for c in range(NCH):
                            body(2 * r + u, (2 * r + u) * NCH + c, u, c, peeled and u == 1 and c == NCH - 1)
                with eng.Fori(0, EG // 2 - 1) as r:
                    pair(r, False)
                pair(EG // 2 - 1, True)

            def gated_sync(sp):
                for u in range(RING):
                    load_expert(sp, v1, v2, u, u)
                with sp.Fori(0, EG // 2 - 1) as r:
                    for u in range(2):
                        sp.wait_ge(down_done, (2 * r + u + 1) * NCH)
                        load_gated(sp, 2 * r + u + 2, u)
                sp.wait_ge(acc1_set, 32)

            def gated_pool(pool):
                with pool.Fori(0, EG // 2) as r:
                    for u in range(2):
                        pool.wait_ge(w_high, 2 * (2 * r + u) + 2)
                        for n, (part, whole) in enumerate(((gparts, gw), (uparts, uw))):
                            pool.tensor_tensor(part[:, u, 1], whole[:, u], high[:, u, n], ALU.subtract).then_inc(w_split, 1)

            def gated_tensor(pe):
                def up(s, u, c, at):
                    chunk = slice(c * CH, (c + 1) * CH)
                    for parts, pp in ((gparts, pG), (uparts, pU)):
                        for k in range(KD):
                            for wn, xn in ((0, 1), (1, 0), (0, 0)):
                                ins = pe.matmul(pp[:, at], parts[:, u, wn, k], xparts[:, xn, k, chunk],
                                                start=(k == 0 and (wn, xn) == (0, 1)), stop=(k == KD - 1 and (wn, xn) == (0, 0)))
                    ins.then_inc(up_done, 1)

                pe.wait_ge(x_split, 1)
                pe.wait_ge(x_kept, 1)
                pe.wait_ge(w_split, 2)
                pe.wait_ge(w_kept, 2)
                pe.wait_ge(cw_in[0], 48)
                up(0, 0, 0, 0)

                def body(e, s, u, c, last):
                    if not last:
                        if c == NCH - 1:
                            nxt = 1 - u
                            rounds = (s - (u * NCH + c)) * 6
                            pe.wait_ge(cw_in[nxt], rounds + (48 if u == 0 else 96))
                            pe.wait_ge(w_split, 2 * e + 4)
                            pe.wait_ge(w_kept, 2 * e + 4)
                        pe.wait_ge(x_split, NCH)
                        pe.wait_ge(x_kept, NCH)
                        pe.wait_ge(hid_ready, done(s))
                        up(s + 1, u if c < NCH - 1 else 1 - u, (c + 1) % NCH, (c + 1) % 2)
                    pe.wait_ge(hid_ready, done(s + 1))
                    pe.wait_ge(acc_done, done(s))
                    for j in range(4):
                        ins = pe.matmul(pY[:, c % 2, j // 2, (j % 2) * D:(j % 2 + 1) * D], hid[:, c % 2, j * P:(j + 1) * P],
                                        dw[:, u], start=True, stop=True)
                    ins.then_inc(down_done, 1)
                all_steps(pe, body)

            def gated_keep(act, u):
                for n, part in enumerate((gparts, uparts)):
                    act.activation(part[:, u, 0], high[:, u, n], ACT.Copy).then_inc(w_kept, 1)

            def gated_scalar(act):
                def body(e, s, u, c, last):
                    if c == 2 and not (isinstance(e, int) and e == EG - 1):
                        act.wait_ge(w_high, 2 * e + 4)
                        gated_keep(act, 1 - u)
                    act.wait_ge(up_done, s + 1)
                    act.wait_ge(hid_ready, done(s))
                    act.activation(ga[:], pG[:, c % 2], ACT.Copy).then_inc(ga_ready, 1)
                all_steps(act, body)

            def split_weights(dve, u):
                for n, whole in enumerate((gw, uw)):
                    upper_bits(dve, high[:, u, n], whole[:, u]).then_inc(w_high, 1)

            def gated_vector(dve):
                dve.wait_ge(x_kept, NCH)
                dve.wait_ge(x_split, NCH)
                dve.memset(xc[:], 0.0).then_inc(acc_done, 1)

                def hidden(s, at):
                    dve.wait_ge(ga_ready, s + 1)
                    dve.scalar_tensor_tensor(lk[:], ga[:], 0.01, ga[:], ALU.mult, ALU.max).then_inc(lk_ready, 1)
                    dve.wait_ge(lk_ready, s + 1)
                    dve.tensor_tensor(hid[:, at], lk[:], pU[:, at], ALU.mult).then_inc(hid_ready, 1)

                hidden(0, 0)

                def body(e, s, u, c, last):
                    if c == 1 and not (isinstance(e, int) and e == EG - 1):
                        dve.wait_ge(cw_in[1 - u], (s - (u * NCH + c)) * 6 + (48 if u == 0 else 96))
                        split_weights(dve, 1 - u)
                    if not last:
                        dve.wait_ge(hid_ready, done(s + 1))
                        hidden(s + 1, (c + 1) % 2)
                    dve.wait_ge(down_done, s + 1)
                    dve.wait_ge(acc_done, done(s + 1))
                    for j in range(4):
                        t = 4 * c + j
                        ins = dve.scalar_tensor_tensor(xc[:, t], pY[:, c % 2, j // 2, (j % 2) * D:(j % 2 + 1) * D],
                                                       W[:, t, ds(e, 1)], xc[:, t], ALU.mult, ALU.add)
                    ins.then_inc(acc_done, 1)
                all_steps(dve, body)

            with nc.Block() as block:
                @block.sync
                def _(sp):
                    for s in (hid_ready, acc_done):
                        sp.sem_inc(s, 1)
                    sp.dma_start(wt_sb[:], wt).then_inc(f_in, 16)
                    sp.dma_start(wg_sb[:], wg).then_inc(f_in, 16)
                    sp.dma_start(cT[:], condT).then_inc(f_in, 16)
                    sp.dma_start(wr_sb[:], wr).then_inc(f_in, 16)
                    for c in range(NCH):
                        sp.dma_start(sums[:, TC * c:TC * c + TC],
                                     acc0[CH * c:CH * (c + 1), :].rearrange("(t p) d -> p t d", p=P)).then_inc(sums_in[c], 16)
                    sp.dma_start(c1_sb[:], c1).then_inc(c_late, 16)
                    sp.dma_start(c2_sb[:].rearrange("p e d -> p (e d)"), c2.partition_broadcast(P)).then_inc(c_late, 16)
                    for u in range(2):
                        load_gated(sp, u, u)
                    sp.wait_ge(route.row_ready, T)
                    sp.dma_start(acc1[0:B * N, :].rearrange("(t p) d -> p t d", p=P), x_sb[:]).then_inc(acc1_set, 16)
                    sp.wait_ge(late_const, 2)
                    sp.dma_start(acc1[B * N:B * N + P, :], zpad[:]).then_inc(acc1_set, 16)
                    sp.wait_ge(f_in, 64)
                    sp.wait_ge(c_late, 32)
                    gated_sync(sp)
                    sp.wait_ge(acc_done, done(STEPS + 1))
                    sp.dma_start(ytab.rearrange("(t p) d -> p t d", p=P), xc[:]).then_inc(y_out, 16)
                    sp.wait_ge(y_out, 16)

                @block.gpsimd
                def _(pool):
                    pool.iota(rev[:], pattern=[[-1, E1]], base=E1, channel_multiplier=0,
                              allow_small_or_imprecise_dtypes=True).then_inc(late_const, 1)
                    pool.memset(zpad[:], 0.0).then_inc(late_const, 1)
                    pool.memset(W[:, :, E1:EG], 1.0).then_inc(late_const, 1)
                    for c in range(NCH):
                        at = slice(CH * c, CH * c + CH)
                        pool.wait_ge(x_high, c + 1)
                        pool.tensor_tensor(xparts[:, 1, :, at], x1T[:, :, at], xhigh[:, :, at], ALU.subtract).then_inc(x_split, 1)
                    gated_pool(pool)

                @block.vector
                def _(dve):
                    steps = [0]

                    def link(ins):
                        steps[0] += 1
                        ins.then_inc(f_step, 1)
                        dve.wait_ge(f_step, steps[0])

                    def columns(c):
                        route.vector_half(dve, c)
                        dve.wait_ge(route.low_ready, c + 1)
                        dve.wait_ge(route.high_ready, c + 1)
                        at = slice(CH * c, CH * c + CH)
                        upper_bits(dve, xhigh[:, :, at], x1T[:, :, at]).then_inc(x_high, 1)

                    for c in range(NCH):
                        ts = slice(TC * c, TC * c + TC)
                        dve.wait_ge(sums_in[c], 16)
                        link(dve.tensor_scalar(den[:, 0, ts], sums[:, ts, D], 0.0, None, ALU.is_le))
                        link(dve.tensor_tensor(den[:, 0, ts], den[:, 0, ts], sums[:, ts, D], ALU.add))
                        link(dve.reciprocal(den[:, 1, ts], den[:, 0, ts]))
                        for t in range(TC * c, TC * c + TC):
                            dve.scalar_tensor_tensor(x_sb[:, t], sums[:, t, 0:D], den[:, 1, t:t + 1], x_sb[:, t],
                                                     ALU.mult, ALU.add).then_inc(route.row_ready, 1)
                        if c >= 1:
                            columns(c - 1)
                    columns(NCH - 1)
                    dve.wait_ge(cw_in[0], 48)
                    split_weights(dve, 0)
                    dve.wait_ge(route.back, NCH)
                    link(dve.tensor_copy(lg[:].rearrange("p t e -> p (t e)"), route.pb[:, 0:T * E1]))
                    softmax(dve, link, lambda: dve.wait_ge(f_exp, 1))
                    dve.wait_ge(late_const, 3)
                    top_two(dve, link)
                    link(dve.tensor_tensor(red[:, 0], best2[:, 0], best2[:, 1], ALU.add))
                    link(dve.tensor_scalar(red[:, 0], red[:, 0], 1e-20, None, ALU.add))
                    link(dve.reciprocal(red[:, 1], red[:, 0]))
                    for n in range(2):
                        link(dve.tensor_tensor(best2[:, n], best2[:, n], red[:, 1], ALU.mult))
                    link(dve.tensor_tensor(scr[:], oh[:, 0], bcast(best2[:, 0], E1), ALU.mult))
                    link(dve.tensor_tensor(lg[:], oh[:, 1], bcast(best2[:, 1], E1), ALU.mult))
                    link(dve.tensor_tensor(W[:, :, 0:E1], scr[:], lg[:], ALU.add))
                    gated_vector(dve)
                    for c in range(NCH):
                        second.vector_half(dve, c)
                    dve.wait_ge(second.back, NCH)
                    link(dve.tensor_copy(lg[:].rearrange("p t e -> p (t e)"), second.pb[:, 0:T * E1]))

                @block.scalar
                def _(act):
                    act.wait_ge(cond_done, 1)
                    act.activation(cond_bias[:], pc[0:E1, 0:B], ACT.Copy).then_inc(cond_kept, 1)
                    act.wait_ge(cond_kept, 1)

                    def keep_high(c):
                        at = slice(CH * c, CH * c + CH)
                        act.wait_ge(x_high, c + 1)
                        act.activation(xparts[:, 0, :, at], xhigh[:, :, at], ACT.Copy).then_inc(x_kept, 1)

                    route.scalar(act, lambda c: keep_high(c - 2) if c >= 2 else None)
                    act.wait_ge(f_step, 3 * NCH + 3)
                    act.activation(lg[:], lg[:], ACT.Exp, scale=0.5).then_inc(f_exp, 1)
                    act.wait_ge(w_high, 2)
                    gated_keep(act, 0)
                    keep_high(2)
                    keep_high(3)
                    gated_scalar(act)
                    second.scalar(act)

                @block.tensor
                def _(pe):
                    pe.wait_ge(f_in, 64)
                    pe.matmul(pc[0:E1, 0:B], wg_sb[:], cT[:], start=True, stop=True).then_inc(cond_done, 1)
                    route.tensor(pe, lambda c: pe.wait_ge(route.row_ready, TC * c + TC), lambda: None, lambda: None)
                    gated_tensor(pe)

                    def sums_are(s):
                        pe.wait_ge(acc_done, done(s + 2))

                    second.tensor(pe, lambda c: sums_are(STEPS - NCH + c), lambda: sums_are(STEPS - 2),
                                  lambda: sums_are(STEPS - 1))
        if upto == "y":
            return

        COLS = BLK + 2
        gtab = sb("gates2", [P, COLS], into=late)
        gidx = sb("gidx", [P, COLS], U32, into=late)
        sidx = sb("sidx", [P, COLS], U32, into=late)
        nblk = sb("nblk", [1, E1], I32, into=late)
        ends = sb("ends", [1, E1], I32, into=late)
        with ExitStack() as ph:
            before = sb("before", [P, P], into=ph)
            zeros = sb("zeros", [P, P], into=ph)
            lane = sb("lane", [P, P], into=ph)
            token = sb("token", [P, T], into=ph)
            spare = sb("spare", [P, 1], into=ph)
            M = sb("M", [P, T, E1], into=ph)
            tot = sb("tot", [P, 2, T, E1], into=ph)
            slot = sb("slot", [P, T, E1], into=ph)
            blocks = sb("blocks", [P, 4, E1], into=ph)
            blocksi = sb("blocksi", [P, 2, E1], I32, into=ph)
            at = sb("at", [P, 2, T], into=ph)
            ati = sb("ati", [P, 2, 2, T], I32, into=ph)
            lanes = sb("lanes", [P, 2, T], into=ph)
            block_of = sb("block_of", [P, 2, T], into=ph)
            A = sb("A", [P, T, 2, P], into=ph)
            Bv = sb("Bv", [P, T, 2, 3, COLS], into=ph)
            empty = sb("empty", [P, COLS], into=ph)
            pP = ps("h_pP", [P, 512], ph)
            pQ = ps("h_pQ", [P, 512], ph)
            pM = ps("h_pM", [P, 512], ph)
            (h_const, h_step, h_exp, counted, a_ready, a_used) = [sem(f"h_{n}") for n in (
                "const", "step", "exp", "counted", "a_ready", "a_used")]
            m_ready = sem("h_m_ready")
            b_ready = sem("h_b_ready")
            with nc.Block() as block:
                @block.gpsimd
                def _(pool):
                    pool.iota(lane[:], pattern=[[1, P]], base=0, channel_multiplier=0,
                              allow_small_or_imprecise_dtypes=True).then_inc(h_const, 1)
                    pool.iota(token[:], pattern=[[P, T]], base=0, channel_multiplier=1,
                              allow_small_or_imprecise_dtypes=True).then_inc(h_const, 1)
                    pool.iota(spare[:], pattern=[[0, 1]], base=B * N, channel_multiplier=1,
                              allow_small_or_imprecise_dtypes=True).then_inc(h_const, 1)
                    pool.memset(zeros[:], 0.0).then_inc(h_const, 1)
                    pool.affine_select(out=before[:], in_=ones[:], compare_op=ALU.is_ge, fill=0.0, base=-1,
                                       pattern=[[1, P]], channel_multiplier=-1).then_inc(h_const, 1)
                    pool.wait_ge(h_const, 5)
                    for c in range(NCH):
                        ts = slice(TC * c, TC * c + TC)
                        for n in range(2):
                            pool.wait_ge(b_ready, 2 * c + n + 1)
                            pool.tensor_tensor(Bv[:, ts, n, 0], Bv[:, ts, n, 2], bcast(token[:, ts], COLS), ALU.mult)
                            pool.tensor_tensor(Bv[:, ts, n, 1], Bv[:, ts, n, 2], bcast(best2[:, n, ts], COLS),
                                               ALU.mult).then_inc(a_ready, 1)

                @block.vector
                def _(dve):
                    steps = [0]

                    def link(ins):
                        steps[0] += 1
                        ins.then_inc(h_step, 1)
                        dve.wait_ge(h_step, steps[0])

                    softmax(dve, link, lambda: dve.wait_ge(h_exp, 1))
                    top_two(dve, link)
                    dve.wait_ge(h_const, 5)
                    dve.tensor_tensor(M[:], oh[:, 0], oh[:, 1], ALU.add).then_inc(m_ready, 1)
                    dve.wait_ge(counted, 1)
                    link(dve.tensor_copy(tot[:, 0].rearrange("p t e -> p (t e)"), pQ[:, 0:T * E1]))
                    for n in range(4):
                        a, b, w = n % 2, (n + 1) % 2, 1 << n
                        link(dve.tensor_copy(tot[:, b, 0:w], tot[:, a, 0:w]))
                        link(dve.tensor_tensor(tot[:, b, w:T], tot[:, a, w:T], tot[:, a, 0:T - w], ALU.add))
                    link(dve.tensor_scalar(blocksi[:, 0], tot[:, 0, T - 1], float(P - 1), None, ALU.add))
                    link(dve.tensor_scalar(blocksi[:, 1], blocksi[:, 0], 7, None, ALU.arith_shift_right))
                    link(dve.tensor_copy(blocks[:, 0], blocksi[:, 1]))
                    link(dve.tensor_copy(blocks[:, 3], blocks[:, 0]))
                    for n in range(3):
                        a, b, w = (0, 1, 2)[n], (1, 2, 0)[n], 1 << n
                        link(dve.tensor_copy(blocks[:, b, 0:w], blocks[:, a, 0:w]))
                        link(dve.tensor_tensor(blocks[:, b, w:E1], blocks[:, a, w:E1], blocks[:, a, 0:E1 - w], ALU.add))
                    link(dve.tensor_copy(nblk[:], blocks[0:1, 3]))
                    link(dve.tensor_copy(ends[:], blocks[0:1, 0]))
                    link(dve.tensor_tensor(blocks[:, 3], blocks[:, 0], blocks[:, 3], ALU.subtract))
                    link(dve.tensor_scalar(blocks[:, 3], blocks[:, 3], float(P), None, ALU.mult))
                    link(dve.tensor_copy(slot[:, 0], blocks[:, 3]))
                    link(dve.tensor_tensor(slot[:, 1:T], tot[:, 0, 0:T - 1], repeat(blocks[:, 3], T - 1), ALU.add))
                    link(dve.tensor_tensor(slot[:].rearrange("p t e -> p (t e)"), slot[:].rearrange("p t e -> p (t e)"),
                                           pP[:, 0:T * E1], ALU.add))
                    for n in range(2):
                        ins = dve.tensor_tensor(oh[:, n], slot[:], oh[:, n], ALU.mult)
                    link(ins)
                    link(dve.tensor_reduce(at[:], oh[:], AX, ALU.add))
                    link(dve.tensor_copy(ati[:, 0], at[:]))
                    link(dve.tensor_scalar(ati[:, 1], ati[:, 0], P - 1, None, ALU.bitwise_and))
                    link(dve.tensor_copy(lanes[:], ati[:, 1]))
                    link(dve.tensor_scalar(ati[:, 1], ati[:, 0], 7, None, ALU.arith_shift_right))
                    link(dve.tensor_copy(block_of[:], ati[:, 1]))
                    cols = lane[:, 0:COLS]
                    for c in range(NCH):
                        ts = slice(TC * c, TC * c + TC)
                        for n in range(2):
                            dve.tensor_tensor(A[:, ts, n], repeat(lane[:], TC), bcast(lanes[:, n, ts], P), ALU.is_equal)
                            dve.tensor_tensor(Bv[:, ts, n, 2], repeat(cols, TC), bcast(block_of[:, n, ts], COLS),
                                              ALU.is_equal).then_inc(b_ready, 1)
                    dve.wait_ge(a_used, 1)
                    link(dve.tensor_copy(gidx[:], pM[:, 0:COLS]))
                    link(dve.tensor_copy(gtab[:], pM[:, COLS:2 * COLS]))
                    link(dve.tensor_scalar(empty[:], pM[:, 2 * COLS:3 * COLS], -1.0, 1.0, ALU.mult, ALU.add))
                    link(dve.tensor_scalar(empty[:], empty[:], spare[:, 0:1], None, ALU.mult))
                    link(dve.tensor_tensor(sidx[:], empty[:], pM[:, 0:COLS], ALU.add))

                @block.scalar
                def _(act):
                    act.wait_ge(h_step, 2)
                    act.activation(lg[:], lg[:], ACT.Exp).then_inc(h_exp, 1)

                @block.tensor
                def _(pe):
                    pe.wait_ge(h_const, 5)
                    pe.wait_ge(m_ready, 1)
                    pe.matmul(pP[:, 0:T * E1], before[:], M[:].rearrange("p t e -> p (t e)"), start=True, stop=True)
                    pe.matmul(pQ[:, 0:T * E1], ones[:], M[:].rearrange("p t e -> p (t e)"), start=True, stop=True).then_inc(counted, 1)
                    pe.matmul(pM[:, 0:P], zeros[:], zeros[:], start=True, stop=False)
                    for t in range(T):
                        if t % TC == 0:
                            pe.wait_ge(a_ready, 2 * (t // TC) + 2)
                        for n in range(2):
                            pe.matmul(pM[:, 0:3 * COLS], A[:, t, n], Bv[:, t, n].rearrange("p v c -> p (v c)"),
                                      start=False, stop=False)
                    pe.matmul(pM[:, 0:P], zeros[:], zeros[:], start=False, stop=True).then_inc(a_used, 1)
        if upto == "route1":
            return

        w_round[0] = E0 // RING
        expert_phase("n", ytab, D, acc1, D, gidx, sidx, gtab, False, c1_sb, c2_sb, v1, v2,
                     E1, ACT.Gelu_apprx_tanh, (nblk, ends))
        late.close()
        result_out = sem("result_out")
        with nc.Block() as block:
            @block.sync
            def _(sp):
                sp.dma_start(out.rearrange("b n d -> (b n) d"), acc1[0:B * N, :]).then_inc(result_out, 16)
                sp.wait_ge(result_out, 16)


_OUTS = [((B, N, D), "float32")]


def kernel(**i):
    import numpy as np
    import concourse.bacc as bacc
    from concourse.bass_utils import run_bass_kernel_spmd as run

    halves = lambda w: w.reshape(D, 2, M1).transpose(1, 0, 2)
    cols = lambda w: w.reshape(KD, P, -1).transpose(1, 0, 2)
    laid = {
        "x": i["x"], "bias": i["fside_16xSxS_0"], "cond": i["cond_64"], "condT": i["cond_64"].T,
        "mask": i["mask_BxS_bk0"].reshape(1, B * N),
        "g_in": i["L0_cond_g_in"].reshape(KD, P).T, "null_bias": i["L0_cond_null_attn_bias"].reshape(1, H),
        "wq": i["L0_cond_Wq"], "wkv": i["L0_cond_Wkv"], "wo": i["L0_cond_Wo"],
        "g_out": i["L0_cond_g_out"].reshape(1, D), "norm_w": i["L0_ffn_norm_weight"].reshape(1, D),
        "rw": cols(np.asarray(i["L0_ffn_router_weight"]).T), "rb": i["L0_ffn_router_bias"].reshape(1, E0),
        "w1": i["L0_ffn_fc1_weight"].transpose(0, 2, 1), "b1": i["L0_ffn_fc1_bias"].reshape(E0, FC, P).transpose(2, 0, 1),
        "w2": i["L0_ffn_fc2_weight"].transpose(0, 2, 1), "b2": i["L0_ffn_fc2_bias"].reshape(1, E0 * D),
        "wt": cols(np.asarray(i["L1_cond_wt"]).T), "wg": i["L1_cond_wg"].T,
        "wgate": np.concatenate([i["L1_cond_w_gate"], halves(i["L1_cond_sw_gate"])]),
        "wup": np.concatenate([i["L1_cond_w_up"], halves(i["L1_cond_sw_up"])]),
        "wdown": np.concatenate([i["L1_cond_w_down"], i["L1_cond_sw_down"].reshape(2, M1, D)]),
        "wr": cols(i["L1_ffn_w_router"]), "v1": i["L1_ffn_w1"],
        "c1": i["L1_ffn_b1"].reshape(E1, FC, P).transpose(2, 0, 1),
        "v2": i["L1_ffn_w2"], "c2": i["L1_ffn_b2"].reshape(1, E1 * D),
    }
    nc = bacc.Bacc("TRN2", target_bir_lowering=False, num_devices=1)
    arrays, args = {}, []
    for name, a in laid.items():
        a = np.ascontiguousarray(a)
        arrays[f"in_{name}"] = a
        args.append(nc.dram_tensor(f"in_{name}", a.shape, mybir.dt.from_np(a.dtype), kind="ExternalInput").ap())
    shape, dtype = _OUTS[0]
    result = nc.dram_tensor("out_0", shape, mybir.dt.from_np(np.dtype(dtype)), kind="ExternalOutput").ap()
    moe_kernel(nc, *args, result)
    r = run(nc, [arrays], core_ids=[0])
    return r.results[0]["out_0"]
```
